# Optimizing a Trainium2 kernel written in Bass

```python
import numpy as np
import jax
import jax.numpy as jnp

def _softmax(x, axis=-1):
    return jax.nn.softmax(x, axis=axis)

def _gelu(x):
    return jax.nn.gelu(x, approximate=True)

def _silu(x):
    return jax.nn.silu(x)

def _sigmoid(x):
    return jax.nn.sigmoid(x)

def _layernorm(x, axis=-1, eps=1e-05):
    m = jnp.mean(x, axis=axis, keepdims=True)
    v = jnp.var(x, axis=axis, keepdims=True)
    return (x - m) / jnp.sqrt(v + eps)

def _scatter_add(tgt, idx, src, axis=0):
    return tgt.at[idx].add(src)

def _segment_sum(src, seg, n):
    return jax.ops.segment_sum(src, seg, n)
kernel_name = 'mk_adj_preln_d4_adj_r2_ec1466'

def setup_inputs(seed: int=0):
    np.random.seed(seed)
    _w = jnp.asarray

    def _rec_inputs():
        import jax
        import jax.numpy as jnp
        _gk = jax.random.key(seed)
        x = -0.0002928 + 1 * jax.random.normal(jax.random.fold_in(_gk, 1), (2048, 512), jnp.float32)
        _a = jax.random.bernoulli(jax.random.fold_in(_gk, 2), 0.000976562, (2048, 2048))
        _a = jnp.logical_or(_a, jnp.swapaxes(_a, -1, -2))
        _a = jnp.logical_or(_a, jnp.eye(2048, dtype=bool))
        _af = _a.astype(jnp.float32)
        _af = _af * jax.random.uniform(jax.random.fold_in(_gk, 3), (2048, 2048), jnp.float32, 0.05, 1)
        adj = _af
        return (x, adj)
    x, adj = _rec_inputs()

    def _L0_gnn_setup():
        import jax, jax.numpy as jnp
        import numpy as np
        D_IN, D_ATTN, STEPS = (512, 64, 2)
        P_TOP, TAU, LN_EPS = (0.9, 1.0, 1e-05)
        N = 2048

        def _xavier(key, shape):
            fan_in, fan_out = (shape[0], shape[1])
            lim = jnp.sqrt(6.0 / (fan_in + fan_out))
            return jax.random.uniform(key, shape, jnp.float32, -lim, lim)

        def _adj_from_feats(Xa, W1, W2, W3):
            Q = Xa @ W1
            K = Xa @ W3
            logits = Q @ W2 @ K.T / TAU
            n = logits.shape[1]
            order = jnp.argsort(-logits, axis=1)
            vals = jnp.take_along_axis(logits, order, axis=1)
            probs = jax.nn.softmax(vals, axis=1)
            csum = jnp.cumsum(probs, axis=1)
            k_i = jnp.sum(csum < P_TOP, axis=1) + 1
            keep = jnp.arange(n)[None, :] < k_i[:, None]
            masked_sorted = jnp.where(keep, vals, -jnp.inf)
            rows = jnp.arange(n)[:, None]
            masked = jnp.full_like(logits, -jnp.inf).at[rows, order].set(masked_sorted)
            return jax.nn.softmax(masked, axis=1)
        key = jax.random.key(seed)
        ks = jax.random.split(key, 12)
        X = jax.random.normal(ks[0], (N, D_IN), jnp.float32)
        S = jax.random.uniform(ks[1], (N, N), jnp.float32)
        W1 = _xavier(ks[2], (D_IN, D_ATTN))
        W3 = _xavier(ks[3], (D_IN, D_ATTN))
        W2 = _xavier(ks[4], (D_ATTN, D_ATTN))
        U1_0 = _xavier(ks[5], (D_IN, D_IN))
        U1_1 = _xavier(ks[6], (D_IN, D_IN))
        U2_0 = _xavier(ks[7], (D_IN, D_IN))
        U2_1 = _xavier(ks[8], (D_IN, D_IN))
        gamma = jnp.ones((D_IN,), jnp.float32)
        beta = jnp.zeros((D_IN,), jnp.float32)
        return {'X': X, 'S': S, 'W1': W1, 'W2': W2, 'W3': W3, 'U1_0': U1_0, 'U1_1': U1_1, 'U2_0': U2_0, 'U2_1': U2_1, 'gamma': gamma, 'beta': beta}
    _L0_gnn_all = _L0_gnn_setup()
    _L0_gnn_in = {k: v for k, v in _L0_gnn_all.items() if k in ('W1', 'W2', 'W3', 'U1_0', 'U1_1', 'U2_0', 'U2_1', 'gamma', 'beta')}
    del _L0_gnn_all

    def _L1_gnn_setup():
        import jax, jax.numpy as jnp
        import numpy as np
        N = 4096
        IN_FEATURES = 512
        OUT_FEATURES = 512
        key = jax.random.key(seed)
        k_x, k_adj, k_w, k_b = jax.random.split(key, 4)
        x = jax.random.normal(k_x, (N, IN_FEATURES), dtype=jnp.float32)
        adj = jax.random.uniform(k_adj, (N, N), dtype=jnp.float32)
        stdv = 1.0 / np.sqrt(OUT_FEATURES)
        weight = jax.random.uniform(k_w, (IN_FEATURES, OUT_FEATURES), dtype=jnp.float32, minval=-stdv, maxval=stdv)
        bias = jax.random.uniform(k_b, (OUT_FEATURES,), dtype=jnp.float32, minval=-stdv, maxval=stdv)
        return {'x': x, 'adj': adj, 'weight': weight, 'bias': bias}
    _L1_gnn_all = _L1_gnn_setup()
    _L1_gnn_in = {k: v for k, v in _L1_gnn_all.items() if k in ('weight', 'bias')}
    del _L1_gnn_all

    def _L2_gnn_setup():
        import jax, jax.numpy as jnp
        import numpy as np
        N, H, E, HEADS = (1500, 512, 10000, 8)
        DK = H // HEADS
        key = jax.random.key(seed)
        k1, k2, k3, k4 = jax.random.split(key, 4)
        inst_feature = jax.random.normal(k1, (N, H), dtype=jnp.float32)
        rel_pair_index = jax.random.randint(k2, (E, 2), 0, N, dtype=jnp.int64)
        agg = jnp.zeros((N, N), dtype=jnp.float32)
        agg = agg.at[rel_pair_index[:, 0], rel_pair_index[:, 1]].set(1.0)
        agg = agg.at[jnp.arange(N), jnp.arange(N)].set(1.0)
        std = float(np.sqrt(2.0 / (H + DK)))
        Wq = jax.random.normal(k3, (H, H), dtype=jnp.float32) * std
        Wk = jax.random.normal(k4, (H, H), dtype=jnp.float32) * std
        bq = jnp.zeros((H,), dtype=jnp.float32)
        bk = jnp.zeros((H,), dtype=jnp.float32)
        return {'inst_feature': inst_feature, 'aggregator_matrix': agg, 'rel_pair_index': rel_pair_index, 'Wq': Wq, 'bq': bq, 'Wk': Wk, 'bk': bk}
    _L2_gnn_all = _L2_gnn_setup()
    _L2_gnn_in = {k: v for k, v in _L2_gnn_all.items() if k in ('rel_pair_index', 'Wq', 'bq', 'Wk', 'bk')}
    del _L2_gnn_all

    def _L3_gnn_setup():
        import jax, jax.numpy as jnp
        import numpy as np
        N = 2048
        D_IN = 512
        H = 16
        DH = D_IN // H
        ALPHA = 0.2
        MASK_VAL = -65500.0
        key = jax.random.key(seed)
        ks = jax.random.split(key, 7)
        x = jax.random.normal(ks[0], (N, D_IN), dtype=jnp.float32)
        adj = jax.random.randint(ks[1], (N, N), 0, 2).astype(jnp.float32)
        s = 1.0 / np.sqrt(D_IN)
        W_seq = jax.random.normal(ks[2], (D_IN, D_IN), dtype=jnp.float32) * s
        a1 = jax.random.normal(ks[3], (DH,), dtype=jnp.float32) / np.sqrt(DH)
        a2 = jax.random.normal(ks[4], (DH,), dtype=jnp.float32) / np.sqrt(DH)
        W_out = jax.random.normal(ks[5], (D_IN, D_IN), dtype=jnp.float32) * s
        b_out = jax.random.normal(ks[6], (D_IN,), dtype=jnp.float32) * 0.01
        return {'x': x, 'adj': adj, 'W_seq': W_seq, 'a1': a1, 'a2': a2, 'W_out': W_out, 'b_out': b_out}
    _L3_gnn_all = _L3_gnn_setup()
    _L3_gnn_in = {k: v for k, v in _L3_gnn_all.items() if k in ('W_seq', 'a1', 'a2', 'W_out', 'b_out')}
    del _L3_gnn_all
    return {'x': x, 'adj': adj, 'L0_gnn_W1': _L0_gnn_in['W1'], 'L0_gnn_W2': _L0_gnn_in['W2'], 'L0_gnn_W3': _L0_gnn_in['W3'], 'L0_gnn_U1_0': _L0_gnn_in['U1_0'], 'L0_gnn_U1_1': _L0_gnn_in['U1_1'], 'L0_gnn_U2_0': _L0_gnn_in['U2_0'], 'L0_gnn_U2_1': _L0_gnn_in['U2_1'], 'L0_gnn_gamma': _L0_gnn_in['gamma'], 'L0_gnn_beta': _L0_gnn_in['beta'], 'L1_gnn_weight': _L1_gnn_in['weight'], 'L1_gnn_bias': _L1_gnn_in['bias'], 'L2_gnn_rel_pair_index': _L2_gnn_in['rel_pair_index'], 'L2_gnn_Wq': _L2_gnn_in['Wq'], 'L2_gnn_bq': _L2_gnn_in['bq'], 'L2_gnn_Wk': _L2_gnn_in['Wk'], 'L2_gnn_bk': _L2_gnn_in['bk'], 'L3_gnn_W_seq': _L3_gnn_in['W_seq'], 'L3_gnn_a1': _L3_gnn_in['a1'], 'L3_gnn_a2': _L3_gnn_in['a2'], 'L3_gnn_W_out': _L3_gnn_in['W_out'], 'L3_gnn_b_out': _L3_gnn_in['b_out']}

def reference(x, adj, L0_gnn_W1, L0_gnn_W2, L0_gnn_W3, L0_gnn_U1_0, L0_gnn_U1_1, L0_gnn_U2_0, L0_gnn_U2_1, L0_gnn_gamma, L0_gnn_beta, L1_gnn_weight, L1_gnn_bias, L2_gnn_rel_pair_index, L2_gnn_Wq, L2_gnn_bq, L2_gnn_Wk, L2_gnn_bk, L3_gnn_W_seq, L3_gnn_a1, L3_gnn_a2, L3_gnn_W_out, L3_gnn_b_out):
    import jax
    import jax.numpy as jnp

    def _L0_gnn_ref(X, S, W1, W2, W3, U1_0, U1_1, U2_0, U2_1, gamma, beta):
        import jax, jax.numpy as jnp
        import numpy as np
        D_IN, D_ATTN, STEPS = (512, 64, 2)
        P_TOP, TAU, LN_EPS = (0.9, 1.0, 1e-05)
        N = 2048

        def _xavier(key, shape):
            fan_in, fan_out = (shape[0], shape[1])
            lim = jnp.sqrt(6.0 / (fan_in + fan_out))
            return jax.random.uniform(key, shape, jnp.float32, -lim, lim)

        def _adj_from_feats(Xa, W1, W2, W3):
            Q = Xa @ W1
            K = Xa @ W3
            logits = Q @ W2 @ K.T / TAU
            n = logits.shape[1]
            order = jnp.argsort(-logits, axis=1)
            vals = jnp.take_along_axis(logits, order, axis=1)
            probs = jax.nn.softmax(vals, axis=1)
            csum = jnp.cumsum(probs, axis=1)
            k_i = jnp.sum(csum < P_TOP, axis=1) + 1
            keep = jnp.arange(n)[None, :] < k_i[:, None]
            masked_sorted = jnp.where(keep, vals, -jnp.inf)
            rows = jnp.arange(n)[:, None]
            masked = jnp.full_like(logits, -jnp.inf).at[rows, order].set(masked_sorted)
            return jax.nn.softmax(masked, axis=1)
        n = X.shape[0]
        S = S + jnp.eye(n, dtype=X.dtype)
        R = S / jnp.clip(S.sum(axis=1, keepdims=True), 1e-12)
        Z = jnp.zeros_like(X)
        Xf, Xa = (X, X)
        U1s, U2s = ((U1_0, U1_1), (U2_0, U2_1))
        for s in range(STEPS):
            A = _adj_from_feats(Xa, W1, W2, W3)
            Xf = R @ Xf
            Xa = A @ Xa
            Z = Z + (Xf @ U1s[s] + Xa @ U2s[s])
        Y = X + Z
        mu = Y.mean(axis=-1, keepdims=True)
        var = Y.var(axis=-1, keepdims=True)
        return (Y - mu) * jax.lax.rsqrt(var + LN_EPS) * gamma + beta

    def _L1_gnn_ref(x, adj, weight, bias):
        import jax, jax.numpy as jnp
        import numpy as np
        N = 4096
        IN_FEATURES = 512
        OUT_FEATURES = 512
        support = jnp.matmul(x, weight)
        output = jnp.matmul(adj, support)
        return output + bias

    def _L2_gnn_ref(inst_feature, aggregator_matrix, rel_pair_index, Wq, bq, Wk, bk):
        import jax, jax.numpy as jnp
        import numpy as np
        N, H, E, HEADS = (1500, 512, 10000, 8)
        DK = H // HEADS
        n = inst_feature.shape[0]
        sub = rel_pair_index[:, 0]
        obj = rel_pair_index[:, 1]
        q = (inst_feature[sub] @ Wq.T + bq).reshape(-1, HEADS, DK)
        k = (inst_feature[obj] @ Wk.T + bk).reshape(-1, HEADS, DK)
        att = ((q * k).sum(-1) / np.sqrt(DK)).T.astype(inst_feature.dtype)
        scores = jnp.zeros((HEADS, n, n), dtype=inst_feature.dtype)
        scores = scores.at[:, sub, obj].set(att)
        mask = (1.0 - aggregator_matrix).astype(bool)
        scores = jnp.where(mask[None], -jnp.inf, scores)
        di = jnp.arange(n)
        scores = scores.at[:, di, di].set(1e-07)
        attn = jax.nn.softmax(scores, axis=2)
        aggregator_factor = attn.sum(axis=0) / HEADS
        return aggregator_factor @ inst_feature

    def _L3_gnn_ref(x, adj, W_seq, a1, a2, W_out, b_out):
        import jax, jax.numpy as jnp
        import numpy as np
        N = 2048
        D_IN = 512
        H = 16
        DH = D_IN // H
        ALPHA = 0.2
        MASK_VAL = -65500.0
        seq = (x @ W_seq).reshape(N, H, DH)
        score1 = jnp.einsum('nhd,d->hn', seq, a1)
        score2 = jnp.einsum('nhd,d->hn', seq, a2)
        scores = score1[:, :, None] + score2[:, None, :]
        scores = jax.nn.leaky_relu(scores, negative_slope=ALPHA)
        scores = scores + (1.0 - adj)[None, :, :] * MASK_VAL
        attn = jax.nn.softmax(scores, axis=-1)
        hidden = jnp.einsum('hij,jhd->ihd', attn, seq).reshape(N, D_IN)
        hidden = hidden @ W_out + b_out
        return jax.nn.elu(hidden)
    h = jnp.maximum(_layernorm(x, axis=-1), 0.0)
    x = x + _L0_gnn_ref(h, adj, L0_gnn_W1, L0_gnn_W2, L0_gnn_W3, L0_gnn_U1_0, L0_gnn_U1_1, L0_gnn_U2_0, L0_gnn_U2_1, L0_gnn_gamma, L0_gnn_beta)
    h = jnp.maximum(_layernorm(x, axis=-1), 0.0)
    x = x + _L1_gnn_ref(h, adj, L1_gnn_weight, L1_gnn_bias)
    h = jnp.maximum(_layernorm(x, axis=-1), 0.0)
    x = x + _L2_gnn_ref(h, adj, L2_gnn_rel_pair_index, L2_gnn_Wq, L2_gnn_bq, L2_gnn_Wk, L2_gnn_bk)
    h = jnp.maximum(_layernorm(x, axis=-1), 0.0)
    x = x + _L3_gnn_ref(h, adj, L3_gnn_W_seq, L3_gnn_a1, L3_gnn_a2, L3_gnn_W_out, L3_gnn_b_out)
    return x

_drawn_inputs = setup_inputs


def setup_inputs(seed=0):
    import zlib

    import numpy as np

    out = dict(_drawn_inputs(seed))
    spreads = {'L0_gnn_gamma': (1.0, 0.2),
     'L0_gnn_beta': (0.0, 0.1),
     'L2_gnn_bq': (0.0, 0.1),
     'L2_gnn_bk': (0.0, 0.1)}
    factors = {'L1_gnn_bias': 4.51, 'L3_gnn_a1': 8.0, 'L3_gnn_a2': 8.0, 'L3_gnn_b_out': 8.0}
    for name, (base, spread) in spreads.items():
        noise = np.random.default_rng([zlib.crc32(name.encode()), seed]).standard_normal(out[name].shape)
        drawn = base * np.exp(spread * noise) if base else spread * noise
        out[name] = jnp.asarray(drawn.astype(out[name].dtype))
    for name, factor in factors.items():
        out[name] = (out[name] * factor).astype(out[name].dtype)
    return out
```

```python
import math
from contextlib import ExitStack

import concourse.bass as bass
from concourse import mybir

P = 128
N = 2048
D = 512
T = N // P
G = T // 2
DC = D // P
DA = 64
HEADS3, DH3 = 16, 32
HEADS2, DH2 = 8, 64
E_PAIRS = 10000
EPS = 1e-5

F32 = mybir.dt.float32
F16 = mybir.dt.float16
I32 = mybir.dt.int32
ALU = mybir.AluOpType
ACT = mybir.ActivationFunctionType
AX = mybir.AxisListType

SX = 256.0
SW = 256.0
SE = 1024.0
SQ = 64.0
SS = 64.0

P_TOP = 0.9
SEARCH = ((6, 1), (9, 2))

H1, XF1, XA1, XF2, XA2, SUP, H3, SEQ = range(8)


def at(i, n=1):
    return bass.ds(i, n)


def wait(eng, sem, value):
    if not isinstance(value, int) or value > 0:
        eng.wait_ge(sem, value)


def groups(eng, body):
    body(0, 0)
    body(1, 1)
    with eng.Fori(1, G // 2 - 1) as k:
        body(2 * k, 0)
        body(2 * k + 1, 1)
    body(G - 2, 0)
    body(G - 1, 1)


class Memory:

    def __init__(self, nc, ctx):
        self.nc, self.ctx, self.made, self.sems = nc, ctx, 0, []

    def sb(self, name, shape, dt=F32, ctx=None):
        self.made += 1
        return (ctx or self.ctx).enter_context(self.nc.sbuf_tensor(f"{name}_{self.made}", shape, dt))

    def ps(self, name, shape, dt=F32, ctx=None):
        self.made += 1
        return (ctx or self.ctx).enter_context(self.nc.psum_tensor(f"{name}_{self.made}", shape, dt))

    def sem(self, name):
        self.sems.append(self.nc.alloc_semaphore(name=name))
        return self.sems[-1]

    def stage_done(self):
        self.nc.clear_and_free_semaphores(self.sems)
        self.nc.all_engine_barrier()
        self.sems = []

    def dram(self, name, shape, dt=F32):
        return self.nc.dram_tensor(name, shape, dt, kind="Internal").ap()


def stage_constants(nc, m):
    m.ident = m.sb("ident", [P, P], F16)
    m.ident_sw = m.sb("ident_sw", [P, P], F16)
    m.minus_half = m.sb("minus_half", [P, 1], F32)
    m.minus_one = m.sb("minus_one", [P, 1], F32)
    zeroed = m.sem("c_zeroed")
    with nc.Block() as block:
        @block.gpsimd
        def _(pool):
            pool.memset(m.ident[:, :], 0.0).then_inc(zeroed, 1)
            pool.memset(m.ident_sw[:, :], 0.0).then_inc(zeroed, 1)
            pool.memset(m.minus_half[:, :], -0.5).then_inc(zeroed, 1)
            pool.memset(m.minus_one[:, :], -1.0)
            pool.wait_ge(zeroed, 3)
            for tile, fill in ((m.ident, 1.0), (m.ident_sw, SW)):
                pool.affine_select(out=tile[:, :], in_=tile[:, :], compare_op=ALU.not_equal, fill=fill,
                                   base=0, pattern=[[-1, P]], channel_multiplier=1).then_inc(zeroed, 1)


def stage_weights(nc, m, name, sources, dests):
    with ExitStack() as ctx:
        width = max(s.shape[1] * s.shape[2] for s in sources)
        raw = m.sb(f"{name}_raw", [P, 2, width], F32, ctx)
        loaded = [m.sem(f"{name}_loaded{b}") for b in range(2)]
        scaled, high, low = m.sem(f"{name}_scaled"), m.sem(f"{name}_high"), m.sem(f"{name}_low")

        def raw_tile(i):
            p, c, n = sources[i].shape
            return raw[0:p, i % 2, 0:c * n].rearrange("p (c n) -> p c n", c=c)

        with nc.Block() as block:
            @block.sync
            def _(sp):
                for i, s in enumerate(sources):
                    wait(sp, low, i - 1)
                    sp.dma_start(raw_tile(i), s).then_inc(loaded[i % 2], 16)

            @block.scalar
            def _(act):
                for i, d in enumerate(dests):
                    p = sources[i].shape[0]
                    act.wait_ge(loaded[i % 2], 16 * (i // 2 + 1))
                    act.activation(d[0:p, 0], raw_tile(i), ACT.Copy, scale=SW).then_inc(high, 1)

            @block.vector
            def _(dve):
                for i, d in enumerate(dests):
                    p = sources[i].shape[0]
                    for c in range(sources[i].shape[1]):
                        dve.wait_ge(high, i + 1)
                        last = dve.scalar_tensor_tensor(out=d[0:p, 1, c], in0=raw_tile(i)[:, c], scalar=SW,
                                                        in1=d[0:p, 0, c], op0=ALU.mult, op1=ALU.subtract)
                    last.then_inc(low, 1)


def product(pe, out, pairs, start=True, stop=True):
    n = len(pairs)
    for i, ((ah, al), (bh, bl)) in enumerate(pairs):
        pe.matmul(out, ah, bh, start=start and i == 0, stop=False)
        pe.matmul(out, ah, bl, start=False, stop=False)
        last = pe.matmul(out, al, bh, start=False, stop=stop and i == n - 1)
    return last


def transposes(pe, m, bank, split):
    for half in range(2):
        for c in range(DC):
            k = half * DC + c
            last = pe.transpose(bank[:, k * P:(k + 1) * P], split[:, half, c * P:(c + 1) * P], m.ident[:, :])
    return last

class Norm:

    def __init__(self, m, name, ctx, factor, eps=EPS):
        self.m, self.factor, self.eps = m, factor, eps
        self.stats = m.sb(f"{name}_stats", [P, 2, 6], F32, ctx)
        self.moments = m.sb(f"{name}_moments", [P, 2, 2], F32, ctx)
        self.parts = m.sb(f"{name}_parts", [P, 2, 4], F32, ctx)
        self.var, self.pow, self.done = m.sem(f"{name}_var"), m.sem(f"{name}_pow"), m.sem(f"{name}_norm_done")

    def vector(self, dve, t, b, src):
        dve.bn_stats(self.stats[:, b], src)
        dve.drain()
        dve.bn_aggr(self.moments[:, b], self.stats[:, b])
        dve.drain()
        dve.tensor_scalar(self.parts[:, b, 0:1], self.moments[:, b, 1:2], self.eps, None, ALU.add).then_inc(self.var, 1)
        dve.wait_ge(self.pow, t + 1)
        dve.tensor_scalar(self.parts[:, b, 2:3], self.parts[:, b, 1:2], self.factor, None, ALU.mult)
        dve.drain()
        dve.scalar_tensor_tensor(out=self.parts[:, b, 3:4], in0=self.moments[:, b, 0:1], scalar=-1.0,
                                 in1=self.parts[:, b, 2:3], op0=ALU.mult, op1=ALU.mult).then_inc(self.done, 1)

    def gpsimd(self, pool, t, b):
        pool.wait_ge(self.var, t + 1)
        pool.tensor_tensor(self.parts[:, b, 1:2], self.parts[:, b, 0:1], self.m.minus_half[:, 0:1],
                           ALU.pow).then_inc(self.pow, 1)

    def relu(self, act, out, src, b):
        return act.activation(out, src, ACT.Relu, bias=self.parts[:, b, 3:4], scale=self.parts[:, b, 2:3])


class Turner:

    def __init__(self, m, name, ctx):
        self.m = m
        self.split = m.sb(f"{name}_split", [P, 2, 2, D], F16, ctx)
        self.turned = m.sb(f"{name}_turned", [P, 2, 2, DC, P], F16, ctx)
        self.bank = m.ps(f"{name}_bank", [P, 2, 8 * P], F16, ctx)
        self.high, self.low = m.sem(f"{name}_high"), m.sem(f"{name}_low")
        self.ready, self.read = m.sem(f"{name}_turn_ready"), m.sem(f"{name}_turn_read")

    def scalar_high(self, act, t, b, src):
        wait(act, self.ready, t - 1)
        act.copy(self.split[:, b, 0], src).then_inc(self.high, 1)

    def gpsimd_low(self, pool, t, b, src):
        pool.wait_ge(self.high, t + 1)
        pool.tensor_tensor(self.split[:, b, 1], src, self.split[:, b, 0], ALU.subtract).then_inc(self.low, 1)

    def tensor_turn(self, pe, t, b):
        pe.wait_ge(self.low, t + 1)
        wait(pe, self.read, t - 1)
        transposes(pe, self.m, self.bank[:, b], self.split[:, b]).then_inc(self.ready, 1)

    def scalar_copy(self, act, t, b):
        act.wait_ge(self.ready, t + 1)
        act.copy(self.turned[:, b].rearrange("p a c n -> p (a c n)").bitcast(F32),
                 self.bank[:, b].bitcast(F32)).then_inc(self.read, 1)

    def pairs(self, b, w):
        return [((self.turned[:, b, 0, c], self.turned[:, b, 1, c]), (w[:, 0, c], w[:, 1, c])) for c in range(DC)]


def stage_norm(nc, m, name, x_view, kind):
    with ExitStack() as ctx:
        x = m.sb(f"{name}_x", [P, 2, D], F32, ctx)
        h = m.sb(f"{name}_h", [P, 2, D], F32, ctx)
        norm, turner = Norm(m, name, ctx, SX), Turner(m, name, ctx)
        loaded = [m.sem(f"{name}_loaded{b}") for b in range(2)]
        stored = [m.sem(f"{name}_stored{b}") for b in range(2)]
        turned_stored = [m.sem(f"{name}_turned_stored{b}") for b in range(2)]
        made = m.sem(f"{name}_made")

        with nc.Block() as block:
            @block.sync
            def _(sp):
                def body(g, _):
                    for b in range(2):
                        t = 2 * g + b
                        wait(sp, made, t - 1)
                        sp.dma_start(x[:, b], x_view[at(t)]).then_inc(loaded[b], 16)
                groups(sp, body)

            @block.vector
            def _(dve):
                def body(g, _):
                    for b in range(2):
                        t = 2 * g + b
                        dve.wait_ge(loaded[b], 16 * (g + 1))
                        wait(dve, made, t - 1)
                        norm.vector(dve, t, b, x[:, b])
                groups(dve, body)

            @block.gpsimd
            def _(pool):
                def body(g, _):
                    for b in range(2):
                        t = 2 * g + b
                        norm.gpsimd(pool, t, b)
                        turner.gpsimd_low(pool, t, b, h[:, b])
                groups(pool, body)

            @block.scalar
            def _(act):
                def body(g, _):
                    for b in range(2):
                        t = 2 * g + b
                        act.wait_ge(norm.done, t + 1)
                        wait(act, turner.low, t - 1)
                        norm.relu(act, h[:, b], x[:, b], b).then_inc(made, 1)
                        act.wait_ge(made, t + 1)
                        wait(act, stored[b], 16 * g)
                        turner.scalar_high(act, t, b, h[:, b])
                        act.wait_ge(turner.low, t + 1)
                        act.dma_start(m.nat[kind][at(t)], turner.split[:, b]).then_inc(stored[b], 16)
                        wait(act, turned_stored[b], 16 * g)
                        turner.scalar_copy(act, t, b)
                        act.wait_ge(turner.read, t + 1)
                        act.dma_start(m.turned[kind][at(t)],
                                      turner.turned[:, b].rearrange("p a c n -> p (a c n)")).then_inc(turned_stored[b], 16)
                groups(act, body)
                for b in range(2):
                    act.wait_ge(stored[b], 16 * G)
                    act.wait_ge(turned_stored[b], 16 * G)

            @block.tensor
            def _(pe):
                def body(g, _):
                    for b in range(2):
                        turner.tensor_turn(pe, 2 * g + b, b)
                groups(pe, body)


def stage_queries_keys(nc, m, s, kind):
    with ExitStack() as ctx:
        xt = m.sb("q_xt", [P, T, 2 * DC, P], F16, ctx)
        qs = m.sb("q_qs", [P, 512], F16, ctx)
        ps_q = m.ps("q_ps_q", [P, 512], F32, ctx)
        ps_p = m.ps("q_ps_p", [P, 512], F32, ctx)
        ps_k = m.ps("q_ps_k", [P, 512], F32, ctx)
        loaded = m.sem(f"q{s}_loaded")
        q_ready, q_high, q_low = m.sem(f"q{s}_q_ready"), m.sem(f"q{s}_q_high"), m.sem(f"q{s}_q_low")
        p_ready, p_high, p_low = m.sem(f"q{s}_p_ready"), m.sem(f"q{s}_p_high"), m.sem(f"q{s}_p_low")
        k_ready, k_high, k_low = m.sem(f"q{s}_k_ready"), m.sem(f"q{s}_k_high"), m.sem(f"q{s}_k_low")
        chunks = N // 512

        with nc.Block() as block:
            @block.sync
            def _(sp):
                sp.dma_start(xt[:, :, :, :].rearrange("p t a n -> p t (a n)"),
                             m.turned[kind].rearrange("t p n -> p t n")).then_inc(loaded, 16)

            @block.tensor
            def _(pe):
                pe.wait_ge(loaded, 16)
                for c in range(chunks):
                    cols = [(xt[:, 4 * c:4 * c + 4, d], xt[:, 4 * c:4 * c + 4, DC + d]) for d in range(DC)]
                    wait(pe, q_low, c)
                    product(pe, ps_q[:, :], [((m.w1[:, 0, d], m.w1[:, 1, d]), cols[d]) for d in range(DC)]).then_inc(q_ready, 1)
                    wait(pe, k_low, c)
                    product(pe, ps_k[:, :], [((m.w3[:, 0, d], m.w3[:, 1, d]), cols[d]) for d in range(DC)]).then_inc(k_ready, 1)
                    wait(pe, p_low, c)
                    pe.wait_ge(q_low, c + 1)
                    pe.matmul(ps_p[:, :], m.w2[:, 0, 0], qs[:, :], start=True, stop=False)
                    pe.matmul(ps_p[:, :], m.w2[:, 1, 0], qs[:, :], start=False, stop=True).then_inc(p_ready, 1)

            @block.scalar
            def _(act):
                for c in range(chunks):
                    act.wait_ge(q_ready, c + 1)
                    wait(act, p_ready, c)
                    act.activation(qs[:, :], ps_q[:, :], ACT.Copy, scale=SQ / (SX * SW)).then_inc(q_high, 1)
                    act.wait_ge(k_ready, c + 1)
                    act.activation(m.k_high[:, at(512 * c, 512)], ps_k[:, :], ACT.Copy,
                                   scale=SQ / (SX * SW)).then_inc(k_high, 1)
                    act.wait_ge(p_ready, c + 1)
                    act.activation(m.qw[:, at(512 * c, 512)], ps_p[:, :], ACT.Copy, scale=1.0 / SW).then_inc(p_high, 1)

            @block.vector
            def _(dve):
                half = slice(DA, P)
                for c in range(chunks):
                    dve.wait_ge(q_high, c + 1)
                    dve.scalar_tensor_tensor(out=qs[half, :], in0=ps_q[half, :], scalar=SQ / (SX * SW),
                                             in1=qs[half, :], op0=ALU.mult, op1=ALU.subtract).then_inc(q_low, 1)
                    dve.wait_ge(k_high, c + 1)
                    dve.scalar_tensor_tensor(out=m.k_low[:, 512 * c:512 * c + 512], in0=ps_k[:, :],
                                             scalar=SQ / (SX * SW), in1=m.k_high[:, 512 * c:512 * c + 512],
                                             op0=ALU.mult, op1=ALU.subtract).then_inc(k_low, 1)
                    dve.wait_ge(p_high, c + 1)
                    q = m.qw[half, 512 * c:512 * c + 512]
                    dve.scalar_tensor_tensor(out=q, in0=ps_p[half, :], scalar=1.0 / SW, in1=q,
                                             op0=ALU.mult, op1=ALU.subtract).then_inc(p_low, 1)


def stage_propagate(nc, m, s):
    first = s == 0
    probes, rounds = SEARCH[s]
    xf_in, xa_in = (H1, H1) if first else (XF1, XA1)
    xf_out, xa_out = (XF1, XA1) if first else (XF2, XA2)
    with ExitStack() as ctx:
        sb = lambda name, shape, dt=F32: m.sb(f"a_{name}", shape, dt, ctx)
        sem = lambda name: m.sem(f"a{s}_{name}")
        xf = sb("xf", [P, T, 2, D], F16)
        xa = xf if first else sb("xa", [P, T, 2, D], F16)
        panel = sb("panel", [P, 2, 2, T, P], F16)
        if first:
            raw_panel = sb("raw_panel", [P, 2, T, P])
            adj_row = sb("adj_row", [P, N])
            row_sum = sb("row_sum", [P, 4])
        e = sb("e", [P, 4, N])
        eh = sb("eh", [P, 2, 2, N], F16)
        et = sb("et", [P, 2, 4, 8, P], F16)
        below = sb("below", [P, 2, N + 8])
        mid_bits, bits = sb("mid_bits", [P, 4], I32), sb("bits", [P, 2], I32)
        top, prefix = sb("top", [P, 8]), sb("prefix", [P, 9])
        wanted = sb("wanted", [P, 8])
        flags, flags_t = sb("flags", [P, 32]), sb("flags_t", [P, 32])
        more, more_int = sb("more", [P, 1]), sb("more_int", [P, 1], I32)
        out32 = {"r": sb("r32", [P, 2, D]), "a": sb("a32", [P, 2, D])}
        split = {"r": sb("r_split", [P, 2, 2, D], F16), "a": sb("a_split", [P, 2, 2, D], F16)}
        turned = {"r": sb("r_turned", [P, 2, 8 * P], F16), "a": sb("a_turned", [P, 2, 8 * P], F16)}
        stat = sb("stat", [P, 16, 4])
        (neg_max, total, squares, low_bits, span, f, hit, goal, kept, inv, row_max, under, picked,
         tmp) = (stat[:, i] for i in range(14))
        ps_l = m.ps("a_logits", [P, N], F32, ctx)
        ps_t = m.ps("a_turn", [P, 2, 8 * P], F16, ctx)
        ps = {"r": m.ps("a_out_r", [P, D], F32, ctx), "a": m.ps("a_out_a", [P, D], F32, ctx)}

        x_loaded = sem("x_loaded")
        raw_loaded = [sem(f"raw_loaded{b}") for b in range(2)]
        panel_loaded = [sem(f"panel_loaded{b}") for b in range(2)]
        panel_stored = [sem(f"panel_stored{b}") for b in range(2)]
        adj_loaded = sem("adj_loaded")
        panel_high, panel_low, row_summed, inv_row = sem("panel_high"), sem("panel_low"), sem("row_summed"), sem("inv_row")
        logits, max_done, e_made = sem("logits"), sem("max_done"), sem("e_made")
        exp_done, top_found, e_cut = sem("exp_done"), sem("top_found"), sem("e_cut")
        e_high, e_low = sem("e_high"), sem("e_low")
        turn_ready, turn_read = sem("turn_ready"), sem("turn_read")
        out_ready = {k: sem(f"{k}_ready") for k in "ra"}
        out_read = {k: sem(f"{k}_read") for k in "ra"}
        high = {k: sem(f"{k}_high") for k in "ra"}
        low = {k: sem(f"{k}_low") for k in "ra"}
        split_stored = {k: [sem(f"{k}_split_stored{b}") for b in range(2)] for k in "ra"}
        turned_stored = {k: [sem(f"{k}_turned_stored{b}") for b in range(2)] for k in "ra"}
        kinds = {"r": xf_out, "a": xa_out}

        def turns_before(g):
            return 0 if isinstance(g, int) and g == 0 else 12 * g - 10

        ALL = turns_before(G)

        with nc.Block() as block:
            @block.sync
            def _(sp):
                sp.dma_start(xf[:, :, :, :].rearrange("p t a n -> p t (a n)"),
                             m.nat[xf_in].rearrange("t p a n -> p t (a n)")).then_inc(x_loaded, 16)
                if not first:
                    sp.dma_start(xa[:, :, :, :].rearrange("p t a n -> p t (a n)"),
                                 m.nat[xa_in].rearrange("t p a n -> p t (a n)")).then_inc(x_loaded, 16)

                def load_raw(t, b):
                    sp.dma_start(raw_panel[:, b], m.adj_panels[at(t)]).then_inc(raw_loaded[b], 16)

                def load_row(t):
                    sp.dma_start(adj_row[:, :], m.adj_rows[at(t)]).then_inc(adj_loaded, 16)

                if first:
                    load_raw(0, 0)
                    load_raw(1, 1)
                    load_row(0)

                def body(g, _):
                    for b in range(2):
                        t = 2 * g + b
                        last_tile = isinstance(g, int) and t == T - 1
                        if first:
                            sp.wait_ge(panel_low, t + 1)
                            sp.dma_start(m.panels[at(t)], panel[:, b]).then_inc(panel_stored[b], 16)
                            if not (isinstance(g, int) and g == G - 1):
                                load_raw(t + 2, b)
                            sp.wait_ge(inv_row, t + 1)
                            if not last_tile:
                                load_row(t + 1)
                            sp.wait_ge(low["r"], t + 1)
                            sp.dma_start(m.nat[xf_out][at(t)], split["r"][:, b]).then_inc(split_stored["r"][b], 16)
                        else:
                            wait(sp, out_ready["r"], t - 1)
                            sp.dma_start(panel[:, b], m.panels[at(t)]).then_inc(panel_loaded[b], 16)
                    if first and not (isinstance(g, int) and g == 0):
                        store_a(g - 1)

                def store_a(g):
                    for b in range(2):
                        t = 2 * g + b
                        sp.wait_ge(low["a"], t + 1)
                        sp.dma_start(m.nat[xa_out][at(t)], split["a"][:, b]).then_inc(split_stored["a"][b], 16)

                groups(sp, body)
                if first:
                    store_a(G - 1)
                    for b in range(2):
                        sp.wait_ge(panel_stored[b], 16 * G)
                        for k in "ra":
                            sp.wait_ge(split_stored[k][b], 16 * G)

            @block.tensor
            def _(pe):
                pe.wait_ge(x_loaded, 16 if first else 32)

                def turn_slot(n):
                    wait(pe, turn_read, n - 1)

                def finish(k, t, b, n, bank):
                    pe.wait_ge(low[k], t + 1)
                    turn_slot(n)
                    transposes(pe, m, ps_t[:, bank], split[k][:, b]).then_inc(turn_ready, 1)

                def attend(t, b, n, bank):
                    pe.wait_ge(e_low, t + 1)
                    for c in range(5):
                        if c < 4:
                            turn_slot(n + c)
                            for half in range(2):
                                for j in range(4):
                                    k = 4 * half + j
                                    last = pe.transpose(ps_t[:, (bank + c) % 2, k * P:(k + 1) * P],
                                                        eh[:, b, half, (4 * c + j) * P:(4 * c + j + 1) * P],
                                                        m.ident[:, :])
                            last.then_inc(turn_ready, 1)
                        if c:
                            d = c - 1
                            if d == 0:
                                wait(pe, out_read["a"], t)
                            pe.wait_ge(turn_read, n + d + 1)
                            pairs = [((et[:, b, d, j], et[:, b, d, 4 + j]),
                                      (xa[:, 4 * d + j, 0], xa[:, 4 * d + j, 1])) for j in range(4)]
                            last = product(pe, ps["a"][:, :], pairs, start=d == 0, stop=d == 3)
                    last.then_inc(out_ready["a"], 1)

                def body(g, _):
                    n0 = turns_before(g)
                    with_a = not (isinstance(g, int) and g == 0)
                    for b in range(2):
                        t = 2 * g + b
                        wait(pe, e_made, t)
                        for c in range(4):
                            q, cols = m.qw[:, at(t * P, P)], slice(512 * c, 512 * c + 512)
                            pe.matmul(ps_l[:, cols], q, m.k_high[:, cols], start=True, stop=False)
                            last = pe.matmul(ps_l[:, cols], q, m.k_low[:, cols], start=False, stop=True)
                        last.then_inc(logits, 1)
                    for b in range(2):
                        t = 2 * g + b
                        if first:
                            pe.wait_ge(panel_low, t + 1)
                        else:
                            pe.wait_ge(panel_loaded[b], 16 * (g + 1))
                        wait(pe, out_read["r"], t)
                        pe.matmul(ps["r"][:, :], m.ident[:, :], xf[:, at(t), 0], start=True, stop=False)
                        pe.matmul(ps["r"][:, :], m.ident[:, :], xf[:, at(t), 1], start=False, stop=False)
                        pairs = [((panel[:, b, 0, j], panel[:, b, 1, j]), (xf[:, j, 0], xf[:, j, 1])) for j in range(T)]
                        product(pe, ps["r"][:, :], pairs, start=False).then_inc(out_ready["r"], 1)
                    finish("r", 2 * g, 0, n0, 0)
                    if with_a:
                        attend(2 * g - 2, 0, n0 + 1, 1)
                        finish("r", 2 * g + 1, 1, n0 + 5, 1)
                        attend(2 * g - 1, 1, n0 + 6, 0)
                        finish("a", 2 * g - 2, 0, n0 + 10, 0)
                        finish("a", 2 * g - 1, 1, n0 + 11, 1)
                    else:
                        finish("r", 2 * g + 1, 1, n0 + 1, 1)

                groups(pe, body)
                attend(T - 2, 0, ALL, 0)
                attend(T - 1, 1, ALL + 4, 0)
                finish("a", T - 2, 0, ALL + 8, 0)
                finish("a", T - 1, 1, ALL + 9, 1)

            @block.scalar
            def _(act):
                def turn_copy(dst, n, bank):
                    act.wait_ge(turn_ready, n + 1)
                    act.copy(dst.bitcast(F32), ps_t[:, bank].bitcast(F32)).then_inc(turn_read, 1)

                def finish(k, t, b, g, n, bank):
                    wait(act, turned_stored[k][b], 16 * g)
                    turn_copy(turned[k][:, b], n, bank)
                    act.wait_ge(turn_read, n + 1)
                    act.dma_start(m.turned[kinds[k]][at(t)], turned[k][:, b]).then_inc(turned_stored[k][b], 16)

                def take(k, t, b, g, scale):
                    act.wait_ge(out_ready[k], t + 1)
                    wait(act, low[k], t - 1)
                    act.activation(out32[k][:, b], ps[k][:, :], ACT.Copy, scale=scale).then_inc(out_read[k], 1)
                    act.wait_ge(out_read[k], t + 1)
                    if first:
                        wait(act, split_stored[k][b], 16 * g)
                    act.copy(split[k][:, b, 0], out32[k][:, b]).then_inc(high[k], 1)

                def attend(t, b, g, n, bank):
                    for c in range(4):
                        turn_copy(et[:, b, c].rearrange("p k n -> p (k n)"), n + c, (bank + c) % 2)
                    take("a", t, b, g, inv[:, 2 * (bank_par[0]) + b:2 * (bank_par[0]) + b + 1])

                bank_par = [0]

                def e_split(t, b, par):
                    act.wait_ge(e_cut, t + 1)
                    wait(act, out_ready["a"], t - 1)
                    act.copy(eh[:, b, 0], e[:, 2 * par + b]).then_inc(e_high, 1)

                def body(g, par):
                    n0 = turns_before(g)
                    with_a = not (isinstance(g, int) and g == 0)
                    bank_par[0] = 1 - par
                    for b in range(2):
                        t = 2 * g + b
                        i = 2 * par + b
                        act.wait_ge(max_done, t + 1)
                        act.activation(e[:, i], ps_l[:, :], ACT.Exp, bias=neg_max[:, i:i + 1],
                                       scale=1.0 / (SQ * SQ), accum_out=total[:, i:i + 1]).then_inc(exp_done, 1)
                        act.wait_ge(exp_done, t + 1)
                        act.activation(ps_l[:, :], e[:, i], ACT.Square,
                                       accum_out=squares[:, i:i + 1]).then_inc(e_made, 1)
                    if first:
                        for b in range(2):
                            t = 2 * g + b
                            act.wait_ge(raw_loaded[b], 16 * (g + 1))
                            wait(act, out_ready["r"], t - 1)
                            wait(act, panel_stored[b], 16 * g)
                            act.copy(panel[:, b, 0], raw_panel[:, b]).then_inc(panel_high, 1)
                            act.wait_ge(adj_loaded, 16 * (t + 1))
                            act.activation(adj_row[:, :], adj_row[:, :], ACT.Copy,
                                           accum_out=row_sum[:, 2 * par + b:2 * par + b + 1]).then_inc(row_summed, 1)
                    if with_a:
                        e_split(2 * g - 2, 0, 1 - par)
                        e_split(2 * g - 1, 1, 1 - par)
                    for b in range(2):
                        t = 2 * g + b
                        if first:
                            act.wait_ge(inv_row, t + 1)
                        take("r", t, b, g, m.inv_row[:, at(t)])
                    finish("r", 2 * g, 0, g, n0, 0)
                    if with_a:
                        attend(2 * g - 2, 0, g - 1, n0 + 1, 1)
                        finish("r", 2 * g + 1, 1, g, n0 + 5, 1)
                        attend(2 * g - 1, 1, g - 1, n0 + 6, 0)
                        finish("a", 2 * g - 2, 0, g - 1, n0 + 10, 0)
                        finish("a", 2 * g - 1, 1, g - 1, n0 + 11, 1)
                    else:
                        finish("r", 2 * g + 1, 1, g, n0 + 1, 1)

                groups(act, body)
                bank_par[0] = 1
                e_split(T - 2, 0, 1)
                e_split(T - 1, 1, 1)
                attend(T - 2, 0, G - 1, ALL, 0)
                attend(T - 1, 1, G - 1, ALL + 4, 0)
                finish("a", T - 2, 0, G - 1, ALL + 8, 0)
                finish("a", T - 1, 1, G - 1, ALL + 9, 1)
                for k in "ra":
                    for b in range(2):
                        act.wait_ge(turned_stored[k][b], 16 * G)

            @block.gpsimd
            def _(pool):
                def e_cut_down(t, b, par):
                    pool.wait_ge(top_found, t + 1)
                    pool.tensor_tensor(e[:, 2 * par + b], e[:, 2 * par + b], below[:, b, 0:N],
                                       ALU.subtract).then_inc(e_cut, 1)

                def e_split(t, b, par):
                    pool.wait_ge(e_high, t + 1)
                    pool.tensor_tensor(eh[:, b, 1], e[:, 2 * par + b], eh[:, b, 0], ALU.subtract).then_inc(e_low, 1)

                def split_low(k, t, b):
                    pool.wait_ge(high[k], t + 1)
                    pool.tensor_tensor(split[k][:, b, 1], out32[k][:, b], split[k][:, b, 0],
                                       ALU.subtract).then_inc(low[k], 1)

                def body(g, par):
                    with_a = not (isinstance(g, int) and g == 0)
                    if first:
                        for b in range(2):
                            pool.wait_ge(panel_high, 2 * g + b + 1)
                            pool.tensor_tensor(panel[:, b, 1], raw_panel[:, b], panel[:, b, 0],
                                               ALU.subtract).then_inc(panel_low, 1)
                    if with_a:
                        e_cut_down(2 * g - 2, 0, 1 - par)
                        e_cut_down(2 * g - 1, 1, 1 - par)
                        e_split(2 * g - 2, 0, 1 - par)
                        e_split(2 * g - 1, 1, 1 - par)
                    split_low("r", 2 * g, 0)
                    split_low("r", 2 * g + 1, 1)
                    if with_a:
                        split_low("a", 2 * g - 2, 0)
                        split_low("a", 2 * g - 1, 1)

                groups(pool, body)
                for b in range(2):
                    e_cut_down(T - 2 + b, b, 1)
                for b in range(2):
                    e_split(T - 2 + b, b, 1)
                for b in range(2):
                    split_low("a", T - 2 + b, b)

            @block.vector
            def _(dve):
                def body(g, par):
                    pair = slice(2 * par, 2 * par + 2)
                    for b in range(2):
                        t = 2 * g + b
                        i = 2 * par + b
                        dve.wait_ge(logits, t + 1)
                        dve.tensor_reduce(row_max[:, i:i + 1], ps_l[:, :], AX.X, ALU.max)
                        dve.drain()
                        dve.tensor_scalar(neg_max[:, i:i + 1], row_max[:, i:i + 1], -1.0 / (SQ * SQ), math.log(SE),
                                          ALU.mult, ALU.add).then_inc(max_done, 1)
                    if first:
                        for b in range(2):
                            t = 2 * g + b
                            i = 2 * par + b
                            dve.wait_ge(row_summed, t + 1)
                            dve.tensor_reduce(m.adj_max[:, at(t)], adj_row[:, :], AX.X, ALU.max)
                            dve.tensor_scalar(hit[:, 0:1], row_sum[:, i:i + 1], 1.0, 1e-12, ALU.add, ALU.max)
                            dve.drain()
                            dve.reciprocal(m.inv_row[:, at(t)], hit[:, 0:1]).then_inc(inv_row, 1)
                    dve.wait_ge(e_made, 2 * g + 2)
                    dve.tensor_scalar(goal[:, pair], total[:, pair], P_TOP, None, ALU.mult)
                    dve.tensor_scalar(tmp[:, pair], total[:, pair], 0.999 * (1 - P_TOP) / N, None, ALU.mult)
                    dve.drain()
                    dve.tensor_copy(low_bits[:, pair], tmp[:, pair].bitcast(I32))
                    dve.reciprocal(hit[:, pair], goal[:, pair])
                    dve.drain()
                    dve.scalar_tensor_tensor(out=tmp[:, pair], in0=squares[:, pair], scalar=1.001, in1=hit[:, pair],
                                             op0=ALU.mult, op1=ALU.mult)
                    dve.drain()
                    dve.tensor_scalar(tmp[:, pair], tmp[:, pair], 1.001 * SE, None, ALU.min)
                    dve.drain()
                    dve.tensor_tensor(span[:, pair], tmp[:, pair].bitcast(I32), low_bits[:, pair], ALU.subtract)
                    for k in range(probes):
                        dve.drain()
                        dve.scalar_tensor_tensor(out=mid_bits[:, pair], in0=span[:, pair], scalar=0.5 ** (k + 1),
                                                 in1=low_bits[:, pair], op0=ALU.mult, op1=ALU.add)
                        dve.drain()
                        if k == 0 and not (isinstance(g, int) and g == 0):
                            dve.wait_ge(e_cut, 2 * g)
                        for b in range(2):
                            i = 2 * par + b
                            dve.scalar_tensor_tensor(out=below[:, b, 0:N], in0=e[:, i],
                                                     scalar=mid_bits[:, i:i + 1].bitcast(F32), in1=e[:, i],
                                                     op0=ALU.is_ge, op1=ALU.mult, accum_out=f[:, i:i + 1])
                        dve.drain()
                        dve.tensor_tensor(hit[:, pair], f[:, pair], goal[:, pair], ALU.is_ge)
                        dve.drain()
                        dve.tensor_tensor(hit[:, pair], hit[:, pair], mid_bits[:, pair], ALU.mult)
                        dve.drain()
                        dve.tensor_tensor(low_bits[:, pair], low_bits[:, pair], hit[:, pair], ALU.max)
                    dve.drain()
                    dve.tensor_scalar(hit[:, pair], span[:, pair], 0.5 ** probes, 256.0, ALU.mult, ALU.add)
                    dve.drain()
                    dve.tensor_tensor(mid_bits[:, pair], hit[:, pair], low_bits[:, pair], ALU.add)
                    dve.drain()
                    for b in range(2):
                        i = 2 * par + b
                        dve.scalar_tensor_tensor(out=below[:, b, 0:N], in0=e[:, i],
                                                 scalar=mid_bits[:, i:i + 1].bitcast(F32), in1=e[:, i],
                                                 op0=ALU.is_lt, op1=ALU.mult, accum_out=under[:, i:i + 1])
                    dve.drain()
                    dve.tensor_tensor(kept[:, pair], total[:, pair], under[:, pair], ALU.subtract)
                    dve.drain()
                    for _round in range(rounds):
                        for b in range(2):
                            take_top(2 * par + b, b)
                    dve.tensor_scalar(mid_bits[:, pair], low_bits[:, pair], -256.0, None, ALU.add)
                    dve.tensor_tensor(tmp[:, pair], goal[:, pair], kept[:, pair], ALU.subtract)
                    dve.drain()
                    dve.reciprocal(hit[:, pair], mid_bits[:, pair].bitcast(F32))
                    dve.tensor_scalar(under[:, pair], tmp[:, pair], 0.0, None, ALU.is_gt)
                    dve.drain()
                    dve.tensor_tensor(hit[:, pair], hit[:, pair], tmp[:, pair], ALU.mult)
                    dve.drain()
                    dve.tensor_scalar(hit[:, pair], hit[:, pair], 0.125, 1.6, ALU.mult, ALU.add)
                    dve.drain()
                    dve.tensor_tensor(hit[:, pair], hit[:, pair], under[:, pair], ALU.mult)
                    dve.drain()
                    dve.tensor_reduce(flags[:, 0:1], hit[:, pair], AX.X, ALU.max)
                    dve.drain()
                    dve.transpose(flags_t[:, :], flags[:, :])
                    dve.drain()
                    dve.tensor_reduce(more[:, :], flags_t[:, :], AX.X, ALU.max)
                    dve.drain()
                    dve.tensor_scalar(more_int[:, :], more[:, :], float(N // 8), None, ALU.min)
                    dve.drain()
                    extra = sum(dve.value_load(more_int[q:q + 1, 0:1], min_val=0, max_val=N // 8)
                                for q in range(0, P, 32))
                    with dve.If(extra > 0):
                        with dve.Fori(0, extra):
                            for b in range(2):
                                take_top(2 * par + b, b)
                    for b in range(2):
                        i = 2 * par + b
                        dve.reciprocal(inv[:, i:i + 1], kept[:, i:i + 1]).then_inc(top_found, 1)

                def take_top(i, b):
                    one = slice(i, i + 1)
                    dve.max(top[:, :], below[:, b])
                    dve.tensor_copy(prefix[:, 0:1], kept[:, one])
                    dve.drain()
                    dve.tensor_tensor_scan(prefix[:, 1:9], top[:, :], top[:, :], kept[:, one], ALU.add, ALU.max)
                    dve.drain()
                    dve.scalar_tensor_tensor(out=wanted[:, :], in0=prefix[:, 0:8], scalar=goal[:, one], in1=top[:, :],
                                             op0=ALU.is_lt, op1=ALU.mult, accum_out=picked[:, one])
                    dve.drain()
                    dve.tensor_tensor(kept[:, one], kept[:, one], picked[:, one], ALU.add)
                    dve.match_replace(below[:, b], wanted[:, :], below[:, b], 0.0)
                    dve.drain()

                dve.memset(below[:, :, N:N + 8], 0.0)
                dve.memset(flags[:, :], 0.0)
                dve.drain()
                groups(dve, body)


def stage_w2(nc, m, w2):
    with ExitStack() as ctx:
        raw = m.sb("w2_raw", [P, 1, P], F32, ctx)
        loaded, high, low = m.sem("w2_loaded"), m.sem("w2_high"), m.sem("w2_low")
        with nc.Block() as block:
            @block.sync
            def _(sp):
                for r in range(2):
                    for c in range(2):
                        sp.dma_start(raw[r * DA:(r + 1) * DA, :, c * DA:(c + 1) * DA], w2).then_inc(loaded, 16)

            @block.scalar
            def _(act):
                act.wait_ge(loaded, 64)
                act.activation(m.w2[:, 0], raw[:, :, :], ACT.Copy, scale=SW).then_inc(high, 1)

            @block.vector
            def _(dve):
                dve.wait_ge(high, 1)
                dve.scalar_tensor_tensor(out=m.w2[:, 1], in0=raw[:, :, :], scalar=SW, in1=m.w2[:, 0],
                                         op0=ALU.mult, op1=ALU.subtract).then_inc(low, 1)



def load_row_vector(sp, tile, vector, sem):
    sp.dma_start(tile, vector.partition_broadcast(P)).then_inc(sem, 16)


def stage_l0_output(nc, m, a, x_view):
    with ExitStack() as ctx:
        sb = lambda name, shape, dt=F32: m.sb(f"o_{name}", shape, dt, ctx)
        sem = lambda name: m.sem(f"o_{name}")
        names = {XF1: "L0_gnn_U1_0", XA1: "L0_gnn_U2_0", XF2: "L0_gnn_U1_1", XA2: "L0_gnn_U2_1"}
        u = {k: sb(f"u{k}", [P, 2, DC, D], F16) for k in names}
        w = sb("w", [P, 2, DC, D], F16)
        chunked = lambda v: v.rearrange("(c p) n -> p c n", p=P)
        stage_weights(nc, m, "ow", [chunked(a[names[k]]) for k in names] + [chunked(a["L1_gnn_weight"])],
                      [u[k] for k in names] + [w])
        gamma, beta = sb("gamma", [P, D]), sb("beta", [P, D])
        parts = sb("parts", [P, 2, 4, 2, DC, P], F16)
        h = sb("h", [P, 2, 2, D], F16)
        x, x1 = sb("x", [P, 2, D]), sb("x1", [P, 2, D])
        h2, sup = sb("h2", [P, 2, D]), sb("sup", [P, 2, D])
        sup_split = sb("sup_split", [P, 2, 2, D], F16)
        ps_y = m.ps("o_y", [P, 2, D], F32, ctx)
        ps_s = m.ps("o_s", [P, 2, D], F32, ctx)
        first_norm = Norm(m, "o1", ctx, 1.0, EPS * (SX * SW) ** 2)
        second_norm = Norm(m, "o2", ctx, SX)
        turner = Turner(m, "ot", ctx)
        vectors = sem("vectors")
        loaded = [sem(f"loaded{b}") for b in range(2)]
        y_ready, x1_made, h2_made = sem("y_ready"), sem("x1_made"), sem("h2_made")
        s_ready, s_read, s_high, s_low = sem("s_ready"), sem("s_read"), sem("s_high"), sem("s_low")
        scaled = sem("scaled")
        x1_stored = [sem(f"x1_stored{b}") for b in range(2)]
        s_stored = [sem(f"s_stored{b}") for b in range(2)]

        with nc.Block() as block:
            @block.sync
            def _(sp):
                load_row_vector(sp, gamma[:, :], a["L0_gnn_gamma"], vectors)
                load_row_vector(sp, beta[:, :], a["L0_gnn_beta"], vectors)

                def body(g, _):
                    for b in range(2):
                        t = 2 * g + b
                        wait(sp, x1_made, t - 1)
                        sp.dma_start(parts[:, b].rearrange("p k a c n -> p k (a c n)"),
                                     m.turned[XF1:XA2 + 1, at(t)].rearrange("k o p n -> p (k o) n")).then_inc(loaded[b], 16)
                        sp.dma_start(h[:, b], m.nat[H1][at(t)]).then_inc(loaded[b], 16)
                        sp.dma_start(x[:, b], x_view[at(t)]).then_inc(loaded[b], 16)
                groups(sp, body)

            @block.tensor
            def _(pe):
                def y_product(g, b):
                    t = 2 * g + b
                    pe.wait_ge(loaded[b], 48 * (g + 1))
                    wait(pe, x1_made, t - 1)
                    pe.matmul(ps_y[:, b], m.ident_sw[:, :], h[:, b, 0], start=True, stop=False)
                    pe.matmul(ps_y[:, b], m.ident_sw[:, :], h[:, b, 1], start=False, stop=False)
                    pairs = [((parts[:, b, i, 0, c], parts[:, b, i, 1, c]), (u[k][:, 0, c], u[k][:, 1, c]))
                             for i, k in enumerate(names) for c in range(DC)]
                    product(pe, ps_y[:, b], pairs, start=False).then_inc(y_ready, 1)

                def s_product(t, b):
                    turner.tensor_turn(pe, t, b)
                    pe.wait_ge(turner.read, t + 1)
                    wait(pe, s_read, t - 1)
                    product(pe, ps_s[:, b], turner.pairs(b, w)).then_inc(s_ready, 1)

                def body(g, _):
                    y_product(g, 0)
                    if not (isinstance(g, int) and g == 0):
                        s_product(2 * g - 1, 1)
                    y_product(g, 1)
                    s_product(2 * g, 0)
                groups(pe, body)
                s_product(T - 1, 1)

            @block.vector
            def _(dve):
                dve.wait_ge(vectors, 32)

                def body(g, _):
                    for b in range(2):
                        t = 2 * g + b
                        dve.wait_ge(y_ready, t + 1)
                        dve.wait_ge(loaded[b], 48 * (g + 1))
                        first_norm.vector(dve, t, b, ps_y[:, b])
                        dve.drain()
                        wait(dve, h2_made, t - 1)
                        wait(dve, x1_stored[b], 16 * g)
                        dve.tensor_scalar(x1[:, b], ps_y[:, b], first_norm.moments[:, b, 0:1],
                                          first_norm.parts[:, b, 1:2], ALU.subtract, ALU.mult)
                        dve.drain()
                        dve.tensor_tensor(x1[:, b], x1[:, b], gamma[:, :], ALU.mult)
                        dve.drain()
                        dve.tensor_tensor(x1[:, b], x1[:, b], beta[:, :], ALU.add)
                        dve.drain()
                        dve.tensor_tensor(x1[:, b], x1[:, b], x[:, b], ALU.add).then_inc(x1_made, 1)
                        dve.drain()
                        second_norm.vector(dve, t, b, x1[:, b])
                groups(dve, body)

            @block.gpsimd
            def _(pool):
                def support_low(t, b):
                    pool.wait_ge(s_high, t + 1)
                    pool.tensor_tensor(sup_split[:, b, 1], sup[:, b], sup_split[:, b, 0], ALU.subtract).then_inc(s_low, 1)

                def body(g, _):
                    for b in range(2):
                        t = 2 * g + b
                        first_norm.gpsimd(pool, t, b)
                        second_norm.gpsimd(pool, t, b)
                        turner.gpsimd_low(pool, t, b, h2[:, b])
                        support_low(t, b)
                groups(pool, body)

            @block.scalar
            def _(act):
                def body(g, _):
                    for b in range(2):
                        t = 2 * g + b
                        act.wait_ge(x1_made, t + 1)
                        act.dma_start(m.x1[at(t)], x1[:, b]).then_inc(x1_stored[b], 16)
                        act.wait_ge(second_norm.done, t + 1)
                        wait(act, turner.low, t - 1)
                        second_norm.relu(act, h2[:, b], x1[:, b], b).then_inc(h2_made, 1)
                        act.wait_ge(h2_made, t + 1)
                        turner.scalar_high(act, t, b, h2[:, b])
                        turner.scalar_copy(act, t, b)
                        act.wait_ge(s_ready, t + 1)
                        wait(act, s_low, t - 1)
                        act.activation(sup[:, b], ps_s[:, b], ACT.Copy, scale=SS / (SX * SW)).then_inc(s_read, 1)
                        act.wait_ge(s_read, t + 1)
                        wait(act, s_stored[b], 16 * g)
                        act.copy(sup_split[:, b, 0], sup[:, b]).then_inc(s_high, 1)
                        act.wait_ge(s_low, t + 1)
                        act.dma_start(m.nat[SUP][at(t)], sup_split[:, b]).then_inc(s_stored[b], 16)
                groups(act, body)
                for b in range(2):
                    act.wait_ge(x1_stored[b], 16 * G)
                    act.wait_ge(s_stored[b], 16 * G)


def stage_l1(nc, m, a):
    with ExitStack() as ctx:
        sb = lambda name, shape, dt=F32: m.sb(f"l_{name}", shape, dt, ctx)
        sem = lambda name: m.sem(f"l_{name}")
        sup = sb("sup", [P, T, 2, D], F16)
        panel = sb("panel", [P, 2, 2, T, P], F16)
        bias = sb("bias", [P, D])
        x1, x2, h3 = sb("x1", [P, 2, D]), sb("x2", [P, 2, D]), sb("h3", [P, 2, D])
        ps_o = m.ps("l_o", [P, 2, D], F32, ctx)
        norm = Norm(m, "ln", ctx, 1.0)
        whole = sem("whole")
        loaded = [sem(f"loaded{b}") for b in range(2)]
        ready, x2_made, h3_made, x3_made = sem("ready"), sem("x2_made"), sem("h3_made"), sem("x3_made")
        x2_stored = [sem(f"x2_stored{b}") for b in range(2)]
        x3_stored = [sem(f"x3_stored{b}") for b in range(2)]

        with nc.Block() as block:
            @block.sync
            def _(sp):
                sp.dma_start(sup[:, :, :, :].rearrange("p t a n -> p t (a n)"),
                             m.nat[SUP].rearrange("t p a n -> p t (a n)")).then_inc(whole, 16)
                load_row_vector(sp, bias[:, :], a["L1_gnn_bias"], whole)

                def body(g, _):
                    for b in range(2):
                        t = 2 * g + b
                        wait(sp, x2_made, t - 1)
                        sp.dma_start(panel[:, b], m.panels[at(t)]).then_inc(loaded[b], 16)
                        sp.dma_start(x1[:, b], m.x1[at(t)]).then_inc(loaded[b], 16)
                groups(sp, body)

            @block.tensor
            def _(pe):
                pe.wait_ge(whole, 32)

                def body(g, _):
                    for b in range(2):
                        t = 2 * g + b
                        pe.wait_ge(loaded[b], 32 * (g + 1))
                        wait(pe, x2_made, t - 1)
                        pairs = [((panel[:, b, 0, j], panel[:, b, 1, j]), (sup[:, j, 0], sup[:, j, 1])) for j in range(T)]
                        product(pe, ps_o[:, b], pairs).then_inc(ready, 1)
                groups(pe, body)

            @block.vector
            def _(dve):
                dve.wait_ge(whole, 32)

                def body(g, _):
                    for b in range(2):
                        t = 2 * g + b
                        dve.wait_ge(ready, t + 1)
                        dve.wait_ge(loaded[b], 32 * (g + 1))
                        wait(dve, x2_stored[b], 16 * g)
                        dve.scalar_tensor_tensor(out=x2[:, b], in0=ps_o[:, b], scalar=1.0 / SS, in1=x1[:, b],
                                                 op0=ALU.mult, op1=ALU.add)
                        dve.drain()
                        dve.tensor_tensor(x2[:, b], x2[:, b], bias[:, :], ALU.add).then_inc(x2_made, 1)
                        dve.drain()
                        norm.vector(dve, t, b, x2[:, b])
                        dve.wait_ge(h3_made, t + 1)
                        dve.tensor_tensor(h3[:, b], h3[:, b], x2[:, b], ALU.add).then_inc(x3_made, 1)
                groups(dve, body)

            @block.gpsimd
            def _(pool):
                def body(g, _):
                    for b in range(2):
                        norm.gpsimd(pool, 2 * g + b, b)
                groups(pool, body)

            @block.scalar
            def _(act):
                def body(g, _):
                    for b in range(2):
                        t = 2 * g + b
                        act.wait_ge(x2_made, t + 1)
                        act.dma_start(m.x2[at(t)], x2[:, b]).then_inc(x2_stored[b], 16)
                        act.wait_ge(norm.done, t + 1)
                        wait(act, x3_stored[b], 16 * g)
                        norm.relu(act, h3[:, b], x2[:, b], b).then_inc(h3_made, 1)
                        act.wait_ge(x3_made, t + 1)
                        act.dma_start(m.x3[at(t)], h3[:, b]).then_inc(x3_stored[b], 16)
                groups(act, body)
                for b in range(2):
                    act.wait_ge(x2_stored[b], 16 * G)
                    act.wait_ge(x3_stored[b], 16 * G)


def stage_l3_sequence(nc, m, a):
    with ExitStack() as ctx:
        sb = lambda name, shape, dt=F32: m.sb(f"s_{name}", shape, dt, ctx)
        sem = lambda name: m.sem(f"s_{name}")
        w = sb("w", [P, 2, DC, D], F16)
        stage_weights(nc, m, "sw", [a["L3_gnn_W_seq"].rearrange("(c p) n -> p c n", p=P)], [w])
        ident32 = sb("ident32", [P, P])
        a_rows = sb("a_rows", [P, 2, DH3])
        x, h, seq = sb("x", [P, 2, D]), sb("h", [P, 2, D]), sb("seq", [P, 2, D])
        weighed = sb("weighed", [P, D])
        score2 = sb("score2", [P, 2, HEADS3])
        score2_t = sb("score2_t", [HEADS3, N])
        split = sb("split", [P, 2, 2, D], F16)
        ps_s = m.ps("s_s", [P, 2, D], F32, ctx)
        ps_t = m.ps("s_t", [P, 2, D], F32, ctx)
        norm = Norm(m, "sn", ctx, SX)
        turner = Turner(m, "st", ctx)
        vectors = sem("vectors")
        loaded = [sem(f"loaded{b}") for b in range(2)]
        h_made, ready, read, high, low = sem("h_made"), sem("ready"), sem("read"), sem("high"), sem("low")
        scored, t_ready, t_read = sem("scored"), sem("t_ready"), sem("t_read")
        stored = [sem(f"stored{b}") for b in range(2)]
        score_stored = sem("score_stored")

        with nc.Block() as block:
            @block.sync
            def _(sp):
                load_row_vector(sp, a_rows[:, 0], a["L3_gnn_a1"], vectors)
                load_row_vector(sp, a_rows[:, 1], a["L3_gnn_a2"], vectors)

                def body(g, _):
                    for b in range(2):
                        t = 2 * g + b
                        wait(sp, h_made, t - 1)
                        sp.dma_start(x[:, b], m.x3[at(t)]).then_inc(loaded[b], 16)
                groups(sp, body)
                sp.wait_ge(t_read, T)
                sp.dma_start(m.score2, score2_t[:, :]).then_inc(score_stored, 16)
                sp.wait_ge(score_stored, 16)

            @block.vector
            def _(dve):
                dve.tensor_copy(ident32[:, :], m.ident[:, :])
                dve.wait_ge(vectors, 32)

                def scores(t, b):
                    dve.wait_ge(read, t + 1)
                    wait(dve, t_read, t - 1)
                    seq_h = seq[:, b].rearrange("p (h d) -> p h d", d=DH3)
                    for i in range(2):
                        for k in range(HEADS3):
                            dve.tensor_tensor(weighed[:, DH3 * k:DH3 * k + DH3], seq[:, b, DH3 * k:DH3 * k + DH3],
                                              a_rows[:, i], ALU.mult)
                        dve.drain()
                        out = score2[:, b] if i else m.score1[:, at(t)]
                        last = dve.tensor_reduce(out, weighed[:, :].rearrange("p (h d) -> p h d", d=DH3), AX.X, ALU.add)
                        if i:
                            last.then_inc(scored, 1)
                        dve.drain()

                def body(g, _):
                    for b in range(2):
                        t = 2 * g + b
                        dve.wait_ge(loaded[b], 16 * (g + 1))
                        wait(dve, h_made, t - 1)
                        norm.vector(dve, t, b, x[:, b])
                        if b:
                            scores(t - 1, 0)
                        elif not (isinstance(g, int) and g == 0):
                            scores(t - 1, 1)
                groups(dve, body)
                scores(T - 1, 1)

            @block.gpsimd
            def _(pool):
                def body(g, _):
                    for b in range(2):
                        t = 2 * g + b
                        norm.gpsimd(pool, t, b)
                        turner.gpsimd_low(pool, t, b, h[:, b])
                        pool.wait_ge(high, t + 1)
                        pool.tensor_tensor(split[:, b, 1], seq[:, b], split[:, b, 0], ALU.subtract).then_inc(low, 1)
                groups(pool, body)

            @block.tensor
            def _(pe):
                def score_turn(t, b):
                    pe.wait_ge(scored, t + 1)
                    wait(pe, t_read, t - 1)
                    pe.transpose(ps_t[0:HEADS3, b, 0:P], score2[:, b], ident32[:, :]).then_inc(t_ready, 1)

                def body(g, _):
                    for b in range(2):
                        t = 2 * g + b
                        turner.tensor_turn(pe, t, b)
                        if b:
                            score_turn(t - 1, 0)
                        elif not (isinstance(g, int) and g == 0):
                            score_turn(t - 1, 1)
                        pe.wait_ge(turner.read, t + 1)
                        wait(pe, read, t - 1)
                        product(pe, ps_s[:, b], turner.pairs(b, w)).then_inc(ready, 1)
                groups(pe, body)
                score_turn(T - 1, 1)

            @block.scalar
            def _(act):
                def score_copy(t, b):
                    act.wait_ge(t_ready, t + 1)
                    act.copy(score2_t[:, at(t * P, P)], ps_t[0:HEADS3, b, 0:P]).then_inc(t_read, 1)

                def body(g, _):
                    for b in range(2):
                        t = 2 * g + b
                        act.wait_ge(norm.done, t + 1)
                        wait(act, turner.low, t - 1)
                        norm.relu(act, h[:, b], x[:, b], b).then_inc(h_made, 1)
                        act.wait_ge(h_made, t + 1)
                        turner.scalar_high(act, t, b, h[:, b])
                        if b:
                            score_copy(t - 1, 0)
                        elif not (isinstance(g, int) and g == 0):
                            score_copy(t - 1, 1)
                        turner.scalar_copy(act, t, b)
                        act.wait_ge(ready, t + 1)
                        wait(act, low, t - 1)
                        wait(act, scored, t - 1)
                        act.activation(seq[:, b], ps_s[:, b], ACT.Copy, scale=SS / (SX * SW)).then_inc(read, 1)
                        act.wait_ge(read, t + 1)
                        wait(act, stored[b], 16 * g)
                        act.copy(split[:, b, 0], seq[:, b]).then_inc(high, 1)
                        act.wait_ge(low, t + 1)
                        act.dma_start(m.nat[SEQ][at(t)], split[:, b]).then_inc(stored[b], 16)
                groups(act, body)
                score_copy(T - 1, 1)
                for b in range(2):
                    act.wait_ge(stored[b], 16 * G)


def stage_l3_attention(nc, m):
    MASK, ALPHA = -65500.0, 0.2
    HH = 8
    with ExitStack() as ctx:
        sb = lambda name, shape, dt=F32: m.sb(f"g_{name}", shape, dt, ctx)
        sem = lambda name: m.sem(f"g_{name}")
        seq = sb("seq", [P, T, 2, D], F16)
        row2 = sb("row2", [P, HH, N])
        mask = sb("mask", [P, N])
        sums = sb("sums", [P, 2, N])
        score = sb("score", [P, 1, N])
        eh = sb("eh", [P, 2, 2, N], F16)
        et = sb("et", [P, 2, 4, 8, P], F16)
        bias1 = sb("bias1", [P, HH])
        stat = sb("stat", [P, 4, 2])
        row_max, neg_max, total, inv = (stat[:, i] for i in range(4))
        hidden = sb("hidden", [P, HH * DH3])
        ps_t = m.ps("g_turn", [P, 2, 8 * P], F16, ctx)
        ps_o = m.ps("g_out", [P, 2, 512], F32, ctx)
        seq_loaded, row2_loaded, adj_loaded = sem("seq_loaded"), sem("row2_loaded"), sem("adj_loaded")
        mask_made, bias_made, sum_made, scored = sem("mask_made"), sem("bias_made"), sem("sum_made"), sem("scored")
        e_made, e_high, e_low = sem("e_made"), sem("e_high"), sem("e_low")
        turn_ready, turn_read, out_ready, out_read = sem("turn_ready"), sem("turn_read"), sem("out_ready"), sem("out_read")
        stored, half_done = sem("stored"), sem("half_done")

        def tiles(eng, half, body):
            if half == 0:
                body(0, 0)
                with eng.Fori(1, T) as t:
                    body(t, t)
            else:
                with eng.Fori(0, T) as t:
                    body(t, t + T)

        with nc.Block() as block:
            @block.sync
            def _(sp):
                sp.dma_start(seq[:, :, :, :].rearrange("p t a n -> p t (a n)"),
                             m.nat[SEQ].rearrange("t p a n -> p t (a n)")).then_inc(seq_loaded, 16)
                for half in range(2):
                    wait(sp, out_read, half * T * HH)
                    for k in range(HH):
                        sp.dma_start(row2[:, k], m.score2[half * HH + k].partition_broadcast(P)).then_inc(row2_loaded, 16)

                    def body(t, n):
                        wait(sp, scored, HH * n)
                        sp.dma_start(mask[:, :], m.adj_rows[at(t)]).then_inc(adj_loaded, 16)
                    tiles(sp, half, body)

            @block.vector
            def _(dve):
                for half in range(2):
                    def turn_copies(n, k):
                        for c in range(4):
                            dve.wait_ge(turn_ready, 4 * (HH * n + k) + c + 1)
                            dve.tensor_copy(et[:, k % 2, c].rearrange("p k n -> p (k n)").bitcast(F32),
                                            ps_t[:, c % 2].bitcast(F32)).then_inc(turn_read, 1)

                    def body(t, n):
                        dve.wait_ge(adj_loaded, 16 * (n + 1))
                        dve.tensor_scalar(mask[:, :], mask[:, :], -1.0, 1.0, ALU.mult, ALU.add)
                        dve.drain()
                        dve.tensor_scalar(mask[:, :], mask[:, :], MASK, None, ALU.mult)
                        wait(dve, sum_made, HH * n)
                        dve.tensor_scalar(bias1[:, :], m.score1[:, at(t), half * HH:(half + 1) * HH], 1.0 / SS, None,
                                          ALU.mult).then_inc(bias_made, 1)
                        dve.drain()
                        for k in range(HH + 1):
                            if k < HH:
                                u = HH * n + k
                                dve.wait_ge(sum_made, u + 1)
                                wait(dve, e_made, u)
                                one = slice(k % 2, k % 2 + 1)
                                dve.scalar_tensor_tensor(out=score[:, 0], in0=sums[:, k % 2], scalar=ALPHA,
                                                         in1=sums[:, k % 2], op0=ALU.mult, op1=ALU.max)
                                dve.drain()
                                dve.tensor_tensor(score[:, 0], score[:, 0], mask[:, :], ALU.add)
                                dve.drain()
                                dve.tensor_reduce(row_max[:, one], score[:, 0], AX.X, ALU.max)
                                dve.drain()
                                dve.tensor_scalar(neg_max[:, one], row_max[:, one], -1.0, math.log(SE),
                                                  ALU.mult, ALU.add).then_inc(scored, 1)
                            if k:
                                turn_copies(n, k - 1)
                    tiles(dve, half, body)

            @block.scalar
            def _(act):
                for half in range(2):
                    act.wait_ge(row2_loaded, 16 * HH * (half + 1))

                    def body(t, n):
                        act.wait_ge(bias_made, n + 1)
                        wait(act, stored, 16 * n)
                        for k in range(HH + 2):
                            if k < HH:
                                wait(act, e_low, HH * n + k - 1)
                                act.activation(sums[:, k % 2], row2[:, k], ACT.Identity, bias=bias1[:, k:k + 1],
                                               scale=1.0 / SS).then_inc(sum_made, 1)
                            if 1 <= k <= HH:
                                u, b = HH * n + k - 1, (k - 1) % 2
                                act.wait_ge(scored, u + 1)
                                act.activation(sums[:, b], score[:, 0], ACT.Exp, bias=neg_max[:, b:b + 1],
                                               accum_out=total[:, b:b + 1]).then_inc(e_made, 1)
                                act.wait_ge(e_made, u + 1)
                                wait(act, out_ready, u - 1)
                                act.copy(eh[:, b, 0], sums[:, b]).then_inc(e_high, 1)
                            if k >= 2:
                                u, b = HH * n + k - 2, k % 2
                                act.wait_ge(out_ready, u + 1)
                                act.activation(hidden[:, (k - 2) * DH3:(k - 1) * DH3], ps_o[:, b, 0:DH3], ACT.Copy,
                                               scale=inv[:, b:b + 1]).then_inc(out_read, 1)
                        act.wait_ge(out_read, HH * (n + 1))
                        act.dma_start(m.hidden[at(t), :, half * HH * DH3:(half + 1) * HH * DH3].rearrange("o p n -> p (o n)"),
                                      hidden[:, :]).then_inc(stored, 16)
                    tiles(act, half, body)
                act.wait_ge(stored, 16 * 2 * T)

            @block.gpsimd
            def _(pool):
                for half in range(2):
                    def body(t, n):
                        for k in range(HH):
                            b = k % 2
                            pool.wait_ge(e_high, HH * n + k + 1)
                            pool.tensor_tensor(inv[:, b:b + 1], total[:, b:b + 1], m.minus_one[:, 0:1], ALU.pow)
                            pool.tensor_tensor(eh[:, b, 1], sums[:, b], eh[:, b, 0], ALU.subtract).then_inc(e_low, 1)
                    tiles(pool, half, body)

            @block.tensor
            def _(pe):
                pe.wait_ge(seq_loaded, 16)
                for half in range(2):
                    def body(t, n):
                        for k in range(HH):
                            u, b = HH * n + k, k % 2
                            pe.wait_ge(e_low, u + 1)
                            for c in range(5):
                                if c < 4:
                                    wait(pe, turn_read, 4 * u + c - 1)
                                    for h in range(2):
                                        for j in range(4):
                                            q = 4 * h + j
                                            last = pe.transpose(ps_t[:, c % 2, q * P:(q + 1) * P],
                                                                eh[:, b, h, (4 * c + j) * P:(4 * c + j + 1) * P], m.ident[:, :])
                                    last.then_inc(turn_ready, 1)
                                if c:
                                    d = c - 1
                                    if d == 0:
                                        wait(pe, out_read, u - 1)
                                    pe.wait_ge(turn_read, 4 * u + d + 1)
                                    cols = slice((half * HH + k) * DH3, (half * HH + k + 1) * DH3)
                                    pairs = [((et[:, b, d, j], et[:, b, d, 4 + j]),
                                              (seq[:, 4 * d + j, 0, cols], seq[:, 4 * d + j, 1, cols])) for j in range(4)]
                                    last = product(pe, ps_o[:, b, 0:DH3], pairs, start=d == 0, stop=d == 3)
                            last.then_inc(out_ready, 1)
                    tiles(pe, half, body)


def stage_l3_output(nc, m, a, out_view):
    with ExitStack() as ctx:
        sb = lambda name, shape, dt=F32: m.sb(f"e_{name}", shape, dt, ctx)
        sem = lambda name: m.sem(f"e_{name}")
        w = sb("w", [P, 2, DC, D], F16)
        stage_weights(nc, m, "ew", [a["L3_gnn_W_out"].rearrange("(c p) n -> p c n", p=P)], [w])
        bias = sb("bias", [P, D])
        hidden, x3 = sb("hidden", [P, 2, D]), sb("x3", [P, 2, D])
        z, neg, ez, res = sb("z", [P, 2, D]), sb("neg", [P, 2, D]), sb("ez", [P, 2, D]), sb("res", [P, 2, D])
        ps_z = m.ps("e_z", [P, 2, D], F32, ctx)
        turner = Turner(m, "et", ctx)
        vectors = sem("vectors")
        loaded = [sem(f"loaded{b}") for b in range(2)]
        z_ready, neg_made, ez_made, res_made = sem("z_ready"), sem("neg_made"), sem("ez_made"), sem("res_made")
        stored = [sem(f"stored{b}") for b in range(2)]

        with nc.Block() as block:
            @block.sync
            def _(sp):
                load_row_vector(sp, bias[:, :], a["L3_gnn_b_out"], vectors)

                def body(g, _):
                    for b in range(2):
                        t = 2 * g + b
                        wait(sp, res_made, t - 1)
                        sp.dma_start(hidden[:, b], m.hidden[at(t)]).then_inc(loaded[b], 16)
                        sp.dma_start(x3[:, b], m.x3[at(t)]).then_inc(loaded[b], 16)
                groups(sp, body)

            @block.tensor
            def _(pe):
                def body(g, _):
                    for b in range(2):
                        t = 2 * g + b
                        turner.tensor_turn(pe, t, b)
                        pe.wait_ge(turner.read, t + 1)
                        wait(pe, neg_made, t - 1)
                        product(pe, ps_z[:, b], turner.pairs(b, w)).then_inc(z_ready, 1)
                groups(pe, body)

            @block.gpsimd
            def _(pool):
                def body(g, _):
                    for b in range(2):
                        turner.gpsimd_low(pool, 2 * g + b, b, hidden[:, b])
                groups(pool, body)

            @block.vector
            def _(dve):
                dve.wait_ge(vectors, 16)

                def body(g, _):
                    for b in range(2):
                        t = 2 * g + b
                        dve.wait_ge(z_ready, t + 1)
                        dve.scalar_tensor_tensor(out=z[:, b], in0=ps_z[:, b], scalar=1.0 / (SS * SW), in1=bias[:, :],
                                                 op0=ALU.mult, op1=ALU.add)
                        dve.drain()
                        wait(dve, ez_made, t - 1)
                        dve.tensor_scalar(neg[:, b], z[:, b], 0.0, None, ALU.min).then_inc(neg_made, 1)
                        dve.tensor_scalar(z[:, b], z[:, b], 0.0, None, ALU.max)
                        dve.drain()
                        dve.wait_ge(ez_made, t + 1)
                        wait(dve, stored[b], 16 * g)
                        dve.scalar_tensor_tensor(out=res[:, b], in0=ez[:, b], scalar=-1.0, in1=z[:, b],
                                                 op0=ALU.add, op1=ALU.add)
                        dve.drain()
                        dve.tensor_tensor(res[:, b], res[:, b], x3[:, b], ALU.add).then_inc(res_made, 1)
                groups(dve, body)

            @block.scalar
            def _(act):
                def body(g, _):
                    for b in range(2):
                        t = 2 * g + b
                        act.wait_ge(loaded[b], 32 * (g + 1))
                        turner.scalar_high(act, t, b, hidden[:, b])
                        turner.scalar_copy(act, t, b)
                        act.wait_ge(neg_made, t + 1)
                        act.activation(ez[:, b], neg[:, b], ACT.Exp).then_inc(ez_made, 1)
                        act.wait_ge(res_made, t + 1)
                        act.dma_start(out_view[at(t)], res[:, b]).then_inc(stored[b], 16)
                groups(act, body)
                for b in range(2):
                    act.wait_ge(stored[b], 16 * G)


def stage_l2_masks(nc, m, a):
    EP, EC = 125, E_PAIRS // 125
    with ExitStack() as ctx:
        sb = lambda name, shape, dt=F32: m.sb(f"m_{name}", shape, dt, ctx)
        sem = lambda name: m.sem(f"m_{name}")
        index = sb("index", [EP, EC, 2], I32)
        subj, obj = sb("subj", [EP, EC]), sb("obj", [EP, EC])
        count_int, count = sb("count_int", [EP, N], I32), sb("count", [EP, N])
        subj_hot, obj_hot = sb("subj_hot", [EP, 2, P], F16), sb("obj_hot", [EP, 2, N], F16)
        off_diag, diag = sb("off_diag", [P, P]), sb("diag", [P, P])
        adj, factor, shift = sb("adj", [P, N]), sb("factor", [P, N]), sb("shift", [P, N])
        related = m.ps("m_related", [P, N], F32, ctx)
        loaded, counted, hot, used = sem("loaded"), sem("counted"), sem("hot"), sem("used")
        adj_loaded, made, stored = sem("adj_loaded"), sem("made"), sem("stored")

        def tiles(eng, body):
            body(0)
            with eng.Fori(1, T) as t:
                body(t)

        with nc.Block() as block:
            @block.sync
            def _(sp):
                sp.dma_start(index[:, :, :], a["L2_gnn_rel_pair_index"].rearrange("(p c) i -> p c i", p=EP)).then_inc(loaded, 16)

                def body(t):
                    wait(sp, made, t)
                    sp.dma_start(adj[:, :], m.adj_rows[at(t)]).then_inc(adj_loaded, 16)
                tiles(sp, body)

            @block.gpsimd
            def _(pool):
                pool.iota(count_int[:, :], pattern=[[1, N]], base=0, channel_multiplier=0).then_inc(counted, 1)

            @block.vector
            def _(dve):
                dve.wait_ge(loaded, 16)
                dve.wait_ge(counted, 1)
                dve.tensor_copy(subj[:, :], index[:, :, 0])
                dve.tensor_copy(obj[:, :], index[:, :, 1])
                dve.tensor_copy(count[:, :], count_int[:, :])
                dve.tensor_copy(diag[:, :], m.ident[:, :])
                dve.drain()
                dve.tensor_scalar(off_diag[:, :], diag[:, :], -1.0, 1.0, ALU.mult, ALU.add)
                dve.drain()
                dve.tensor_scalar(diag[:, :], diag[:, :], 1e-7, None, ALU.mult)
                dve.drain()

                def body(t):
                    def hots(c, b, n):
                        dve.tensor_scalar(subj_hot[:, b], count[:, 0:P], subj[:, at(c)], None, ALU.is_equal)
                        dve.tensor_scalar(obj_hot[:, b], count[:, :], obj[:, at(c)], None, ALU.is_equal).then_inc(hot, 1)
                    hots(0, 0, 0)
                    hots(1, 1, 0)
                    with dve.Fori(1, EC // 2) as c2:
                        for b in range(2):
                            dve.wait_ge(used, EC * t + 2 * c2 + b - 1)
                            hots(2 * c2 + b, b, 0)
                    dve.drain()
                    dve.tensor_scalar(subj[:, :], subj[:, :], -float(P), None, ALU.add)
                    dve.drain()
                    wait(dve, stored, 32 * t)
                    dve.wait_ge(adj_loaded, 16 * (t + 1))
                    dve.tensor_scalar(adj[:, :], adj[:, :], 1.0, None, ALU.is_equal)
                    dve.wait_ge(used, EC * (t + 1))
                    dve.tensor_scalar(factor[:, :], related[:, :], 1.0, 1.0 / math.sqrt(DH2), ALU.min, ALU.mult)
                    dve.drain()
                    dve.tensor_tensor(factor[:, :], factor[:, :], adj[:, :], ALU.mult)
                    dve.tensor_scalar(shift[:, :], adj[:, :], -1.0, 1e30, ALU.add, ALU.mult)
                    dve.drain()
                    own = at(t * P, P)
                    dve.tensor_tensor(factor[:, own], factor[:, own], off_diag[:, :], ALU.mult)
                    dve.tensor_tensor(shift[:, own], shift[:, own], off_diag[:, :], ALU.mult)
                    dve.drain()
                    dve.tensor_tensor(shift[:, own], shift[:, own], diag[:, :], ALU.add).then_inc(made, 1)
                tiles(dve, body)

            @block.tensor
            def _(pe):
                def body(t):
                    def chunk(n, b, start, stop):
                        pe.wait_ge(hot, n + 1)
                        for c in range(4):
                            last = pe.matmul(related[:, 512 * c:512 * c + 512], subj_hot[:, b],
                                             obj_hot[:, b, 512 * c:512 * c + 512], start=start, stop=stop)
                        return last
                    chunk(EC * t, 0, True, False).then_inc(used, 1)
                    chunk(EC * t + 1, 1, False, False).then_inc(used, 1)
                    with pe.Fori(1, EC // 2 - 1) as c2:
                        for b in range(2):
                            chunk(EC * t + 2 * c2 + b, b, False, False).then_inc(used, 1)
                    chunk(EC * (t + 1) - 2, 0, False, False).then_inc(used, 1)
                    chunk(EC * (t + 1) - 1, 1, False, True).then_inc(used, 1)
                tiles(pe, body)

            @block.scalar
            def _(act):
                def body(t):
                    act.wait_ge(made, t + 1)
                    act.dma_start(m.factor[at(t)], factor[:, :]).then_inc(stored, 16)
                    act.dma_start(m.shift[at(t)], shift[:, :]).then_inc(stored, 16)
                tiles(act, body)
                act.wait_ge(stored, 32 * T)


def stage_l2_attention(nc, m, a):
    with ExitStack() as ctx:
        sb = lambda name, shape, dt=F32: m.sb(f"r_{name}", shape, dt, ctx)
        sem = lambda name: m.sem(f"r_{name}")
        w = {k: sb(f"w{k}", [P, 2, DC, 2 * D], F16) for k in "qk"}
        sources, dests = [], []
        for k, name in (("q", "L2_gnn_Wq"), ("k", "L2_gnn_Wk")):
            for h in range(HEADS2):
                for twin in range(2):
                    sources.append(a[name].rearrange("(c p) n -> p c n", p=P)[:, :, h * DH2:(h + 1) * DH2])
                    dests.append(w[k][:, :, :, (2 * h + twin) * DH2:(2 * h + twin + 1) * DH2])
        stage_weights(nc, m, "rw", sources, dests)
        bias = {k: sb(f"b{k}", [P, HEADS2]) for k in "qk"}
        xt = sb("xt", [P, T, 2 * DC, P], F16)
        h3 = sb("h3", [P, T, 2, D], F16)
        total_out = sb("out", [P, T, D])
        qs, k_high, k_low = (sb(n, [P, N], F16) for n in ("qs", "k_high", "k_low"))
        part = sb("part", [P, 512])
        factor, shift, score = sb("factor", [P, N]), sb("shift", [P, N]), sb("score", [P, N])
        eh = sb("eh", [P, 2, N], F16)
        et = sb("et", [P, 2, 8, P], F16)
        stat = sb("stat", [P, 4])
        row_max, neg_max, total, inv = (stat[:, i:i + 1] for i in range(4))
        ps_l = m.ps("r_logits", [P, N], F32, ctx)
        ps_t = m.ps("r_turn", [P, 2, 8 * P], F16, ctx)
        ps_p, ps_o = m.ps("r_part", [P, 512], F32, ctx), m.ps("r_out", [P, D], F32, ctx)
        loaded, bias_scaled, masks_loaded = sem("loaded"), sem("bias_scaled"), sem("masks_loaded")
        part_ready, part_read, part_high, part_low = sem("part_ready"), sem("part_read"), sem("part_high"), sem("part_low")
        logits, scored, e_made, e_high, e_low = sem("logits"), sem("scored"), sem("e_made"), sem("e_high"), sem("e_low")
        turn_ready, turn_read, out_ready, out_read = sem("turn_ready"), sem("turn_read"), sem("out_ready"), sem("out_read")
        stored = sem("stored")

        def tiles(eng, head, body):
            if head == 0:
                body(0, 0)
                with eng.Fori(1, T) as t:
                    body(t, t)
            else:
                with eng.Fori(0, T) as t:
                    body(t, t + head * T)

        with nc.Block() as block:
            @block.sync
            def _(sp):
                sp.dma_start(xt[:, :, :, :].rearrange("p t a n -> p t (a n)"),
                             m.turned[H1].rearrange("t p n -> p t n")).then_inc(loaded, 16)
                sp.dma_start(h3[:, :, :, :].rearrange("p t a n -> p t (a n)"),
                             m.nat[H1].rearrange("t p a n -> p t (a n)")).then_inc(loaded, 16)
                sp.dma_start(total_out[:, :, :], m.x2.rearrange("t p n -> p t n")).then_inc(loaded, 16)
                with nc.allow_non_contiguous_dma(reason="a bias vector of 512, a head per column"):
                    for k, name in (("q", "L2_gnn_bq"), ("k", "L2_gnn_bk")):
                        for twin in range(2):
                            sp.dma_start(bias[k][twin * DH2:(twin + 1) * DH2, :],
                                         a[name].rearrange("(h d) -> d h", d=DH2)).then_inc(loaded, 16)
                for head in range(HEADS2):
                    def body(t, n):
                        wait(sp, scored, n)
                        sp.dma_start(factor[:, :], m.factor[at(t)]).then_inc(masks_loaded, 16)
                        sp.dma_start(shift[:, :], m.shift[at(t)]).then_inc(masks_loaded, 16)
                    tiles(sp, head, body)
                sp.wait_ge(out_read, HEADS2 * T)
                sp.dma_start(m.x3.rearrange("t p n -> p t n"), total_out[:, :, :]).then_inc(stored, 16)
                sp.wait_ge(stored, 16)

            @block.tensor
            def _(pe):
                pe.wait_ge(loaded, 16 * 7)
                for head in range(HEADS2):
                    for c in range(4):
                        for i, k in enumerate("qk"):
                            wait(pe, part_read, 8 * head + 2 * c + i)
                            cols = slice(2 * head * DH2, 2 * (head + 1) * DH2)
                            pairs = [((w[k][:, 0, d, cols], w[k][:, 1, d, cols]),
                                      (xt[:, 4 * c:4 * c + 4, d], xt[:, 4 * c:4 * c + 4, DC + d])) for d in range(DC)]
                            product(pe, ps_p[:, :], pairs).then_inc(part_ready, 1)
                    pe.wait_ge(part_low, 8 * (head + 1))

                    def body(t, n):
                        wait(pe, scored, n)
                        for c in range(4):
                            q, cols = qs[:, at(t * P, P)], slice(512 * c, 512 * c + 512)
                            pe.matmul(ps_l[:, cols], q, k_high[:, cols], start=True, stop=False)
                            last = pe.matmul(ps_l[:, cols], q, k_low[:, cols], start=False, stop=True)
                        last.then_inc(logits, 1)
                        pe.wait_ge(e_low, n + 1)
                        for c in range(4):
                            wait(pe, turn_read, 4 * n + c - 1)
                            for half in range(2):
                                for j in range(4):
                                    i = 4 * half + j
                                    last = pe.transpose(ps_t[:, c % 2, i * P:(i + 1) * P],
                                                        eh[:, half, (4 * c + j) * P:(4 * c + j + 1) * P], m.ident[:, :])
                            last.then_inc(turn_ready, 1)
                            pe.wait_ge(turn_read, 4 * n + c + 1)
                            pairs = [((et[:, c % 2, j], et[:, c % 2, 4 + j]), (h3[:, 4 * c + j, 0], h3[:, 4 * c + j, 1]))
                                     for j in range(4)]
                            if c == 0:
                                wait(pe, out_read, n)
                            last = product(pe, ps_o[:, :], pairs, start=c == 0, stop=c == 3)
                        last.then_inc(out_ready, 1)
                    tiles(pe, head, body)

            @block.scalar
            def _(act):
                act.wait_ge(bias_scaled, 2)
                for head in range(HEADS2):
                    wait(act, logits, T * head)
                    for c in range(4):
                        for i, (k, dst) in enumerate((("q", qs), ("k", k_high))):
                            u = 8 * head + 2 * c + i
                            act.wait_ge(part_ready, u + 1)
                            wait(act, part_low, u)
                            act.activation(part[:, :], ps_p[:, :], ACT.Identity, bias=bias[k][:, head:head + 1],
                                           scale=SQ / (SX * SW)).then_inc(part_read, 1)
                            act.wait_ge(part_read, u + 1)
                            act.copy(dst[:, 512 * c:512 * c + 512], part[:, :]).then_inc(part_high, 1)

                    def body(t, n):
                        act.wait_ge(scored, n + 1)
                        act.activation(score[:, :], score[:, :], ACT.Exp, bias=neg_max, accum_out=total).then_inc(e_made, 1)
                        act.wait_ge(e_made, n + 1)
                        act.copy(eh[:, 0], score[:, :]).then_inc(e_high, 1)
                    tiles(act, head, body)

            @block.gpsimd
            def _(pool):
                for head in range(HEADS2):
                    def body(t, n):
                        pool.wait_ge(e_high, n + 1)
                        pool.tensor_tensor(eh[:, 1], score[:, :], eh[:, 0], ALU.subtract).then_inc(e_low, 1)
                    tiles(pool, head, body)

            @block.vector
            def _(dve):
                dve.wait_ge(loaded, 16 * 7)
                for k in "qk":
                    dve.tensor_scalar(bias[k][:, :], bias[k][:, :], SQ, None, ALU.mult).then_inc(bias_scaled, 1)
                low = slice(DA, P)
                for head in range(HEADS2):
                    for c in range(4):
                        cols = slice(512 * c, 512 * c + 512)
                        dve.wait_ge(part_high, 8 * head + 2 * c + 1)
                        dve.tensor_tensor(qs[low, cols], part[low, :], qs[low, cols], ALU.subtract).then_inc(part_low, 1)
                        dve.wait_ge(part_high, 8 * head + 2 * c + 2)
                        dve.tensor_tensor(k_low[:, cols], part[:, :], k_high[:, cols], ALU.subtract).then_inc(part_low, 1)

                    def body(t, n):
                        dve.wait_ge(logits, n + 1)
                        dve.wait_ge(masks_loaded, 32 * (n + 1))
                        dve.scalar_tensor_tensor(out=score[:, :], in0=ps_l[:, :], scalar=1.0 / (SQ * SQ), in1=factor[:, :],
                                                 op0=ALU.mult, op1=ALU.mult)
                        dve.drain()
                        dve.tensor_tensor(score[:, :], score[:, :], shift[:, :], ALU.add)
                        dve.drain()
                        dve.tensor_reduce(row_max, score[:, :], AX.X, ALU.max)
                        dve.drain()
                        dve.tensor_scalar(neg_max, row_max, -1.0, math.log(SE), ALU.mult, ALU.add).then_inc(scored, 1)
                        for c in range(4):
                            dve.wait_ge(turn_ready, 4 * n + c + 1)
                            dve.tensor_copy(et[:, c % 2].rearrange("p k n -> p (k n)").bitcast(F32),
                                            ps_t[:, c % 2].bitcast(F32)).then_inc(turn_read, 1)
                        dve.wait_ge(e_made, n + 1)
                        dve.reciprocal(inv, total)
                        dve.drain()
                        dve.tensor_scalar(inv, inv, 1.0 / (HEADS2 * SX), None, ALU.mult)
                        dve.drain()
                        dve.wait_ge(out_ready, n + 1)
                        dve.scalar_tensor_tensor(out=total_out[:, at(t)].rearrange("p o n -> p (o n)"), in0=ps_o[:, :],
                                                 scalar=inv, in1=total_out[:, at(t)].rearrange("p o n -> p (o n)"),
                                                 op0=ALU.mult, op1=ALU.add).then_inc(out_read, 1)
                    tiles(dve, head, body)


def stage_flag(nc, m):
    m.flag = m.sb("flag", [P, 4])
    with ExitStack() as ctx:
        reduced, spread, done = m.sem("f_reduced"), m.sem("f_spread"), m.sem("f_done")
        with nc.Block() as block:
            @block.vector
            def _(dve):
                dve.tensor_reduce(m.flag[:, 0:1], m.adj_max[:, :], AX.X, ALU.max).then_inc(reduced, 1)
                dve.wait_ge(spread, 1)
                dve.tensor_scalar(m.flag[:, 2:3], m.flag[:, 1:2], 1.0, None, ALU.is_ge).then_inc(done, 1)

            @block.gpsimd
            def _(pool):
                pool.wait_ge(reduced, 1)
                pool.partition_all_reduce(m.flag[:, 1:2], m.flag[:, 0:1], P, bass.bass_isa.ReduceOp.max).then_inc(spread, 1)


def gnn_stack(nc, out, a):
    with ExitStack() as ctx:
        m = Memory(nc, ctx)
        m.nat = m.dram("nat", (8, T, P, 2, D), F16)
        m.turned = m.dram("turned", (5, T, P, 8 * P), F16)
        m.panels = m.dram("panels", (T, P, 2, T, P), F16)
        m.x1, m.x2, m.x3, m.hidden = (m.dram(n, (T, P, D)) for n in ("x1", "x2", "x3", "hidden"))
        m.factor, m.shift = m.dram("factor", (T, P, N)), m.dram("shift", (T, P, N))
        m.score2 = m.dram("score2", (HEADS3, N))
        m.adj_panels = a["adj_panels"]
        m.adj_rows = a["adj"].rearrange("(t p) n -> t p n", p=P)
        x_view = a["x"].rearrange("(t p) d -> t p d", p=P)
        out_view = out.rearrange("(t p) d -> t p d", p=P)
        m.inv_row, m.adj_max = m.sb("inv_row", [P, T]), m.sb("adj_max", [P, T])
        m.score1 = m.sb("score1", [P, T, HEADS3])
        stage_constants(nc, m)
        with ExitStack() as l0:
            m.w1, m.w3 = (m.sb(n, [P, 2, DC, P], F16, l0) for n in ("w1", "w3"))
            m.w2 = m.sb("w2", [P, 2, 1, P], F16, l0)
            m.qw, m.k_high, m.k_low = (m.sb(n, [P, N], F16, l0) for n in ("qw", "k_high", "k_low"))
            chunked = lambda w: w.rearrange("(c p) n -> p c n", p=P)
            halves = [slice(0, DA), slice(DA, P)]
            stage_weights(nc, m, "wq", [chunked(a["L0_gnn_W1"])] * 2 + [chunked(a["L0_gnn_W3"])] * 2,
                          [w[:, :, :, half] for w in (m.w1, m.w3) for half in halves])
            stage_w2(nc, m, a["L0_gnn_W2"].rearrange("p (c n) -> p c n", c=1))
            stage_norm(nc, m, "n", x_view, H1)
            m.stage_done()
            for s in range(2):
                stage_queries_keys(nc, m, s, XA1 if s else H1)
                stage_propagate(nc, m, s)
                m.stage_done()
        stage_l0_output(nc, m, a, x_view)
        m.stage_done()
        stage_l1(nc, m, a)
        stage_flag(nc, m)
        m.stage_done()
        with nc.If(nc.values_load(m.flag[0:1, 2:3].bitcast(I32)) > 0):
            stage_norm(nc, m, "h3", m.x2, H1)
            m.stage_done()
            stage_l2_masks(nc, m, a)
            m.stage_done()
            stage_l2_attention(nc, m, a)
            m.stage_done()
        stage_l3_sequence(nc, m, a)
        m.stage_done()
        stage_l3_attention(nc, m)
        m.stage_done()
        stage_l3_output(nc, m, a, out_view)


def kernel(**inputs):
    import numpy as _np
    import concourse.bacc as _bacc
    from concourse import mybir as _mybir
    from concourse.bass_utils import run_bass_kernel_spmd as _run

    def layout(a):
        return _np.ascontiguousarray(a)

    inputs = {k: _np.asarray(v) for k, v in inputs.items()}
    adj = inputs["adj"]
    arrays = {name: layout(a) for name, a in inputs.items()}
    arrays["adj_panels"] = layout(adj.reshape(16, 128, 16, 128).transpose(0, 3, 2, 1))
    for name in ("L2_gnn_Wq", "L2_gnn_Wk"):
        arrays[name] = layout(inputs[name].T)
    nc = _bacc.Bacc("TRN2", target_bir_lowering=False, num_devices=1)
    args, given = {}, {}
    for name, a in arrays.items():
        given[f"in_{name}"] = a
        args[name] = nc.dram_tensor(f"in_{name}", a.shape, _mybir.dt.from_np(a.dtype), kind="ExternalInput").ap()
    out = nc.dram_tensor("out", (2048, 512), _mybir.dt.float32, kind="ExternalOutput").ap()
    gnn_stack(nc, out, args)
    r = _run(nc, [given], core_ids=[0])
    return r.results[0]["out"]
```

```python
import math
from contextlib import ExitStack

import concourse.bass as bass
from concourse import mybir

P = 128
N = 2048
D = 512
T = N // P
G = T // 2
DC = D // P
DA = 64
HEADS3, DH3 = 16, 32
HEADS2, DH2 = 8, 64
E_PAIRS = 10000
EPS = 1e-5
MASK, ALPHA = -65500.0, 0.2
NEAR = 3
ROW3 = D + HEADS3

F32 = mybir.dt.float32
F16 = mybir.dt.float16
I32 = mybir.dt.int32
U32 = mybir.dt.uint32
ALU = mybir.AluOpType
ACT = mybir.ActivationFunctionType
AX = mybir.AxisListType

SX = 256.0
SW = 256.0
SE = 1024.0
SQ = 64.0
SS = 64.0

P_TOP = 0.9
SEARCH = ((6, 1), (9, 2))

H1, XF1, XA1, XF2, XA2, SUP, H3, SEQ = range(8)


def at(i, n=1):
    return bass.ds(i, n)


def wait(eng, sem, value):
    if not isinstance(value, int) or value > 0:
        eng.wait_ge(sem, value)


def groups(eng, body):
    body(0, 0)
    body(1, 1)
    with eng.Fori(1, G // 2 - 1) as k:
        body(2 * k, 0)
        body(2 * k + 1, 1)
    body(G - 2, 0)
    body(G - 1, 1)


class Memory:

    def __init__(self, nc, ctx):
        self.nc, self.ctx, self.made, self.sems = nc, ctx, 0, []

    def sb(self, name, shape, dt=F32, ctx=None):
        self.made += 1
        return (ctx or self.ctx).enter_context(self.nc.sbuf_tensor(f"{name}_{self.made}", shape, dt))

    def ps(self, name, shape, dt=F32, ctx=None):
        self.made += 1
        return (ctx or self.ctx).enter_context(self.nc.psum_tensor(f"{name}_{self.made}", shape, dt))

    def sem(self, name):
        self.sems.append(self.nc.alloc_semaphore(name=name))
        return self.sems[-1]

    def stage_done(self):
        self.nc.clear_and_free_semaphores(self.sems)
        self.nc.all_engine_barrier()
        self.sems = []

    def dram(self, name, shape, dt=F32):
        return self.nc.dram_tensor(name, shape, dt, kind="Internal").ap()


def stage_constants(nc, m):
    m.ident = m.sb("ident", [P, P], F16)
    m.ident_sw = m.sb("ident_sw", [P, P], F16)
    m.minus_half = m.sb("minus_half", [P, 1], F32)
    m.minus_one = m.sb("minus_one", [P, 1], F32)
    zeroed = m.sem("c_zeroed")
    with nc.Block() as block:
        @block.gpsimd
        def _(pool):
            pool.memset(m.ident[:, :], 0.0).then_inc(zeroed, 1)
            pool.memset(m.ident_sw[:, :], 0.0).then_inc(zeroed, 1)
            pool.memset(m.minus_half[:, :], -0.5).then_inc(zeroed, 1)
            pool.memset(m.minus_one[:, :], -1.0)
            pool.wait_ge(zeroed, 3)
            for tile, fill in ((m.ident, 1.0), (m.ident_sw, SW)):
                pool.affine_select(out=tile[:, :], in_=tile[:, :], compare_op=ALU.not_equal, fill=fill,
                                   base=0, pattern=[[-1, P]], channel_multiplier=1).then_inc(zeroed, 1)


def stage_weights(nc, m, name, sources, dests, early=None):
    with ExitStack() as ctx:
        width = max(s.shape[1] * s.shape[2] for s in sources)
        raw = m.sb(f"{name}_raw", [P, 2, width], F32, ctx)
        loaded = [m.sem(f"{name}_loaded{b}") for b in range(2)]
        high, low = m.sem(f"{name}_high"), m.sem(f"{name}_low")

        def raw_tile(i):
            p, c, n = sources[i].shape
            return raw[0:p, i % 2, 0:c * n].rearrange("p (c n) -> p c n", c=c)

        with nc.Block() as block:
            @block.sync
            def _(sp):
                for i, s in enumerate(sources):
                    wait(sp, low, i - 1)
                    sp.dma_start(raw_tile(i), s).then_inc(loaded[i % 2], 16)
                if early:
                    early(sp)

            @block.scalar
            def _(act):
                for i, d in enumerate(dests):
                    p = sources[i].shape[0]
                    act.wait_ge(loaded[i % 2], 16 * (i // 2 + 1))
                    act.activation(d[0:p, 0], raw_tile(i), ACT.Copy, scale=SW).then_inc(high, 1)

            @block.vector
            def _(dve):
                for i, d in enumerate(dests):
                    p = sources[i].shape[0]
                    for c in range(sources[i].shape[1]):
                        dve.wait_ge(high, i + 1)
                        last = dve.scalar_tensor_tensor(out=d[0:p, 1, c], in0=raw_tile(i)[:, c], scalar=SW,
                                                        in1=d[0:p, 0, c], op0=ALU.mult, op1=ALU.subtract)
                    last.then_inc(low, 1)


def product(pe, out, pairs, start=True, stop=True):
    n = len(pairs)
    for i, ((ah, al), (bh, bl)) in enumerate(pairs):
        pe.matmul(out, ah, bh, start=start and i == 0, stop=False)
        pe.matmul(out, ah, bl, start=False, stop=False)
        last = pe.matmul(out, al, bh, start=False, stop=stop and i == n - 1)
    return last


def transposes(pe, m, bank, split):
    for half in range(2):
        for c in range(DC):
            k = half * DC + c
            last = pe.transpose(bank[:, k * P:(k + 1) * P], split[:, half, c * P:(c + 1) * P], m.ident[:, :])
    return last

class Norm:

    def __init__(self, m, name, ctx, factor, eps=EPS):
        self.m, self.factor, self.eps = m, factor, eps
        self.stats = m.sb(f"{name}_stats", [P, 2, 6], F32, ctx)
        self.moments = m.sb(f"{name}_moments", [P, 2, 2], F32, ctx)
        self.parts = m.sb(f"{name}_parts", [P, 2, 4], F32, ctx)
        self.var, self.pow, self.done = m.sem(f"{name}_var"), m.sem(f"{name}_pow"), m.sem(f"{name}_norm_done")

    def vector(self, dve, t, b, src):
        dve.bn_stats(self.stats[:, b], src)
        dve.drain()
        dve.bn_aggr(self.moments[:, b], self.stats[:, b])
        dve.drain()
        dve.tensor_scalar(self.parts[:, b, 0:1], self.moments[:, b, 1:2], self.eps, None, ALU.add).then_inc(self.var, 1)
        dve.wait_ge(self.pow, t + 1)
        dve.tensor_scalar(self.parts[:, b, 2:3], self.parts[:, b, 1:2], self.factor, None, ALU.mult)
        dve.drain()
        dve.scalar_tensor_tensor(out=self.parts[:, b, 3:4], in0=self.moments[:, b, 0:1], scalar=-1.0,
                                 in1=self.parts[:, b, 2:3], op0=ALU.mult, op1=ALU.mult).then_inc(self.done, 1)

    def gpsimd(self, pool, t, b):
        pool.wait_ge(self.var, t + 1)
        pool.tensor_tensor(self.parts[:, b, 1:2], self.parts[:, b, 0:1], self.m.minus_half[:, 0:1],
                           ALU.pow).then_inc(self.pow, 1)

    def relu(self, act, out, src, b):
        return act.activation(out, src, ACT.Relu, bias=self.parts[:, b, 3:4], scale=self.parts[:, b, 2:3])


class Turner:

    def __init__(self, m, name, ctx):
        self.m = m
        self.split = m.sb(f"{name}_split", [P, 2, 2, D], F16, ctx)
        self.turned = m.sb(f"{name}_turned", [P, 2, 2, DC, P], F16, ctx)
        self.bank = m.ps(f"{name}_bank", [P, 2, 8 * P], F16, ctx)
        self.high, self.low = m.sem(f"{name}_high"), m.sem(f"{name}_low")
        self.ready, self.read = m.sem(f"{name}_turn_ready"), m.sem(f"{name}_turn_read")

    def scalar_high(self, act, t, b, src):
        wait(act, self.ready, t - 1)
        act.copy(self.split[:, b, 0], src).then_inc(self.high, 1)

    def gpsimd_low(self, pool, t, b, src):
        pool.wait_ge(self.high, t + 1)
        pool.tensor_tensor(self.split[:, b, 1], src, self.split[:, b, 0], ALU.subtract).then_inc(self.low, 1)

    def tensor_turn(self, pe, t, b):
        pe.wait_ge(self.low, t + 1)
        wait(pe, self.read, t - 1)
        transposes(pe, self.m, self.bank[:, b], self.split[:, b]).then_inc(self.ready, 1)

    def scalar_copy(self, act, t, b):
        act.wait_ge(self.ready, t + 1)
        act.copy(self.turned[:, b].rearrange("p a c n -> p (a c n)").bitcast(F32),
                 self.bank[:, b].bitcast(F32)).then_inc(self.read, 1)

    def pairs(self, b, w):
        return [((self.turned[:, b, 0, c], self.turned[:, b, 1, c]), (w[:, 0, c], w[:, 1, c])) for c in range(DC)]


def stage_norm(nc, m, name, x_view, kind):
    with ExitStack() as ctx:
        x = m.sb(f"{name}_x", [P, 2, D], F32, ctx)
        h = m.sb(f"{name}_h", [P, 2, D], F32, ctx)
        norm, turner = Norm(m, name, ctx, SX), Turner(m, name, ctx)
        loaded = [m.sem(f"{name}_loaded{b}") for b in range(2)]
        stored = [m.sem(f"{name}_stored{b}") for b in range(2)]
        turned_stored = [m.sem(f"{name}_turned_stored{b}") for b in range(2)]
        made = m.sem(f"{name}_made")

        with nc.Block() as block:
            @block.sync
            def _(sp):
                def body(g, _):
                    for b in range(2):
                        t = 2 * g + b
                        wait(sp, made, t - 1)
                        sp.dma_start(x[:, b], x_view[at(t)]).then_inc(loaded[b], 16)
                groups(sp, body)

            @block.vector
            def _(dve):
                def body(g, _):
                    for b in range(2):
                        t = 2 * g + b
                        dve.wait_ge(loaded[b], 16 * (g + 1))
                        wait(dve, made, t - 1)
                        norm.vector(dve, t, b, x[:, b])
                groups(dve, body)

            @block.gpsimd
            def _(pool):
                def body(g, _):
                    for b in range(2):
                        t = 2 * g + b
                        norm.gpsimd(pool, t, b)
                        turner.gpsimd_low(pool, t, b, h[:, b])
                groups(pool, body)

            @block.scalar
            def _(act):
                def store(t, b, g):
                    act.wait_ge(turner.low, t + 1)
                    act.dma_start(m.nat[kind][at(t)], turner.split[:, b]).then_inc(stored[b], 16)
                    wait(act, turned_stored[b], 16 * g)
                    turner.scalar_copy(act, t, b)
                    act.wait_ge(turner.read, t + 1)
                    act.dma_start(m.turned[kind][at(t)],
                                  turner.turned[:, b].rearrange("p a c n -> p (a c n)")).then_inc(turned_stored[b], 16)

                def body(g, _):
                    for b in range(2):
                        t = 2 * g + b
                        act.wait_ge(norm.done, t + 1)
                        wait(act, turner.low, t - 1)
                        norm.relu(act, h[:, b], x[:, b], b).then_inc(made, 1)
                        act.wait_ge(made, t + 1)
                        wait(act, stored[b], 16 * g)
                        turner.scalar_high(act, t, b, h[:, b])
                        if b:
                            store(t - 1, 0, g)
                        elif not (isinstance(g, int) and g == 0):
                            store(t - 1, 1, g - 1)
                groups(act, body)
                store(T - 1, 1, G - 1)
                for b in range(2):
                    act.wait_ge(stored[b], 16 * G)
                    act.wait_ge(turned_stored[b], 16 * G)

            @block.tensor
            def _(pe):
                def body(g, _):
                    for b in range(2):
                        turner.tensor_turn(pe, 2 * g + b, b)
                groups(pe, body)


def stage_queries_keys(nc, m, s, kind):
    with ExitStack() as ctx:
        xt = m.sb("q_xt", [P, T, 2 * DC, P], F16, ctx)
        qs = m.sb("q_qs", [P, 512], F16, ctx)
        ps_q = m.ps("q_ps_q", [P, 512], F32, ctx)
        ps_p = m.ps("q_ps_p", [P, 512], F32, ctx)
        ps_k = m.ps("q_ps_k", [P, 512], F32, ctx)
        loaded = m.sem(f"q{s}_loaded")
        q_ready, q_high, q_low = m.sem(f"q{s}_q_ready"), m.sem(f"q{s}_q_high"), m.sem(f"q{s}_q_low")
        p_ready, p_high, p_low = m.sem(f"q{s}_p_ready"), m.sem(f"q{s}_p_high"), m.sem(f"q{s}_p_low")
        k_ready, k_high, k_low = m.sem(f"q{s}_k_ready"), m.sem(f"q{s}_k_high"), m.sem(f"q{s}_k_low")
        chunks = N // 512

        with nc.Block() as block:
            @block.sync
            def _(sp):
                sp.dma_start(xt[:, :, :, :].rearrange("p t a n -> p t (a n)"),
                             m.turned[kind].rearrange("t p n -> p t n")).then_inc(loaded, 16)

            @block.tensor
            def _(pe):
                pe.wait_ge(loaded, 16)
                for c in range(chunks):
                    cols = [(xt[:, 4 * c:4 * c + 4, d], xt[:, 4 * c:4 * c + 4, DC + d]) for d in range(DC)]
                    wait(pe, q_low, c)
                    product(pe, ps_q[:, :], [((m.w1[:, 0, d], m.w1[:, 1, d]), cols[d]) for d in range(DC)]).then_inc(q_ready, 1)
                    wait(pe, k_low, c)
                    product(pe, ps_k[:, :], [((m.w3[:, 0, d], m.w3[:, 1, d]), cols[d]) for d in range(DC)]).then_inc(k_ready, 1)
                    wait(pe, p_low, c)
                    pe.wait_ge(q_low, c + 1)
                    pe.matmul(ps_p[:, :], m.w2[:, 0, 0], qs[:, :], start=True, stop=False)
                    pe.matmul(ps_p[:, :], m.w2[:, 1, 0], qs[:, :], start=False, stop=True).then_inc(p_ready, 1)

            @block.scalar
            def _(act):
                for c in range(chunks):
                    act.wait_ge(q_ready, c + 1)
                    wait(act, p_ready, c)
                    act.activation(qs[:, :], ps_q[:, :], ACT.Copy, scale=SQ / (SX * SW)).then_inc(q_high, 1)
                    act.wait_ge(k_ready, c + 1)
                    act.activation(m.k_high[:, at(512 * c, 512)], ps_k[:, :], ACT.Copy,
                                   scale=SQ / (SX * SW)).then_inc(k_high, 1)
                    act.wait_ge(p_ready, c + 1)
                    act.activation(m.qw[:, at(512 * c, 512)], ps_p[:, :], ACT.Copy, scale=1.0 / SW).then_inc(p_high, 1)

            @block.vector
            def _(dve):
                half = slice(DA, P)
                for c in range(chunks):
                    dve.wait_ge(q_high, c + 1)
                    dve.scalar_tensor_tensor(out=qs[half, :], in0=ps_q[half, :], scalar=SQ / (SX * SW),
                                             in1=qs[half, :], op0=ALU.mult, op1=ALU.subtract).then_inc(q_low, 1)
                    dve.wait_ge(k_high, c + 1)
                    dve.scalar_tensor_tensor(out=m.k_low[:, 512 * c:512 * c + 512], in0=ps_k[:, :],
                                             scalar=SQ / (SX * SW), in1=m.k_high[:, 512 * c:512 * c + 512],
                                             op0=ALU.mult, op1=ALU.subtract).then_inc(k_low, 1)
                    dve.wait_ge(p_high, c + 1)
                    q = m.qw[half, 512 * c:512 * c + 512]
                    dve.scalar_tensor_tensor(out=q, in0=ps_p[half, :], scalar=1.0 / SW, in1=q,
                                             op0=ALU.mult, op1=ALU.subtract).then_inc(p_low, 1)


def stage_propagate(nc, m, s):
    first = s == 0
    probes, rounds = SEARCH[s]
    xf_in, xa_in = (H1, H1) if first else (XF1, XA1)
    xf_out, xa_out = (XF1, XA1) if first else (XF2, XA2)
    with ExitStack() as ctx:
        sb = lambda name, shape, dt=F32: m.sb(f"a_{name}", shape, dt, ctx)
        sem = lambda name: m.sem(f"a{s}_{name}")
        xf = sb("xf", [P, T, 2, D], F16)
        xa = xf if first else sb("xa", [P, T, 2, D], F16)
        panel = sb("panel", [P, 2, 2, T, P], F16)
        if first:
            raw_panel = sb("raw_panel", [P, 2, T, P])
            adj_row = sb("adj_row", [P, N])
            row_sum = sb("row_sum", [P, 4])
        e = sb("e", [P, 4, N])
        eh = sb("eh", [P, 2, 2, N], F16)
        et = sb("et", [P, 2, 4, 8, P], F16)
        below = sb("below", [P, 2, N + 8])
        unused = sb("unused", [P, N], F16)
        mid_bits, low_bits = sb("mid_bits", [P, 2], I32), sb("low_bits", [P, 3, 2])
        half_span, raised = sb("half_span", [P, probes + 1, 2]), sb("raised", [P, 2])
        top, prefix = sb("top", [P, 2, 8]), sb("prefix", [P, 2, 9])
        wanted = sb("wanted", [P, 2, 8])
        flags, flags_t = sb("flags", [P, 32]), sb("flags_t", [P, 32])
        more, more_int = sb("more", [P, 1]), sb("more_int", [P, 1], I32)
        out32 = {"r": sb("r32", [P, 2, D]), "a": sb("a32", [P, 2, D])}
        split = {"r": sb("r_split", [P, 2, 2, D], F16), "a": sb("a_split", [P, 2, 2, D], F16)}
        turned = {"r": sb("r_turned", [P, 2, 8 * P], F16), "a": sb("a_turned", [P, 2, 8 * P], F16)}
        stat = sb("stat", [P, 16, 4])
        (neg_max, total, squares, span, f, hit, goal, kept, inv, row_max, under, picked,
         tmp) = (stat[:, i] for i in range(13))
        ps_l = m.ps("a_logits", [P, N], F32, ctx)
        ps_t = m.ps("a_turn", [P, 2, 8 * P], F16, ctx)
        ps = {"r": m.ps("a_out_r", [P, D], F32, ctx), "a": m.ps("a_out_a", [P, D], F32, ctx)}

        x_loaded = sem("x_loaded")
        raw_loaded = [sem(f"raw_loaded{b}") for b in range(2)]
        panel_loaded = [sem(f"panel_loaded{b}") for b in range(2)]
        panel_stored = [sem(f"panel_stored{b}") for b in range(2)]
        adj_loaded = sem("adj_loaded")
        panel_high, panel_low, row_summed, inv_row = sem("panel_high"), sem("panel_low"), sem("row_summed"), sem("inv_row")
        logits, max_done, e_made = sem("logits"), sem("max_done"), sem("e_made")
        exp_done, top_found, e_cut = sem("exp_done"), sem("top_found"), sem("e_cut")
        e_high, e_low = sem("e_high"), sem("e_low")
        turn_ready, turn_read = sem("turn_ready"), sem("turn_read")
        out_ready = {k: sem(f"{k}_ready") for k in "ra"}
        out_read = {k: sem(f"{k}_read") for k in "ra"}
        high = {k: sem(f"{k}_high") for k in "ra"}
        low = {k: sem(f"{k}_low") for k in "ra"}
        split_stored = {k: [sem(f"{k}_split_stored{b}") for b in range(2)] for k in "ra"}
        turned_stored = {k: [sem(f"{k}_turned_stored{b}") for b in range(2)] for k in "ra"}
        kinds = {"r": xf_out, "a": xa_out}

        def turns_before(g):
            return 0 if isinstance(g, int) and g == 0 else 12 * g - 10

        ALL = turns_before(G)

        def is_last(g):
            return isinstance(g, int) and g == G - 1

        with nc.Block() as block:
            @block.sync
            def _(sp):
                sp.dma_start(xf[:, :, :, :].rearrange("p t a n -> p t (a n)"),
                             m.nat[xf_in].rearrange("t p a n -> p t (a n)")).then_inc(x_loaded, 16)
                if not first:
                    sp.dma_start(xa[:, :, :, :].rearrange("p t a n -> p t (a n)"),
                                 m.nat[xa_in].rearrange("t p a n -> p t (a n)")).then_inc(x_loaded, 16)

                def load_raw(t, b):
                    sp.dma_start(raw_panel[:, b], m.adj_panels[at(t)]).then_inc(raw_loaded[b], 16)

                def load_row(t):
                    sp.dma_start(adj_row[:, :], m.adj_rows[at(t)]).then_inc(adj_loaded, 16)

                if first:
                    for b in range(2):
                        load_raw(b, b)
                        if b == 1:
                            sp.wait_ge(row_summed, 1)
                        load_row(b)

                def body(g, _):
                    tiles = [(b, 2 * g + b) for b in range(2)]
                    if first:
                        more = not is_last(g)
                        for b, t in tiles:
                            sp.wait_ge(panel_low, t + 1)
                            sp.dma_start(m.panels[at(t)], panel[:, b]).then_inc(panel_stored[b], 16)
                            if more:
                                load_raw(t + 2, b)
                                sp.wait_ge(row_summed, t + 2)
                                load_row(t + 2)
                        for b, t in tiles:
                            sp.wait_ge(low["r"], t + 1)
                            sp.dma_start(m.nat[xf_out][at(t)], split["r"][:, b]).then_inc(split_stored["r"][b], 16)
                    else:
                        for b, t in tiles:
                            wait(sp, out_ready["r"], t - 1)
                            sp.dma_start(panel[:, b], m.panels[at(t)]).then_inc(panel_loaded[b], 16)
                    if first and not (isinstance(g, int) and g == 0):
                        store_a(g - 1)

                def store_a(g):
                    for b in range(2):
                        t = 2 * g + b
                        sp.wait_ge(low["a"], t + 1)
                        sp.dma_start(m.nat[xa_out][at(t)], split["a"][:, b]).then_inc(split_stored["a"][b], 16)

                groups(sp, body)
                if first:
                    store_a(G - 1)
                    for b in range(2):
                        sp.wait_ge(panel_stored[b], 16 * G)
                        for k in "ra":
                            sp.wait_ge(split_stored[k][b], 16 * G)

            @block.tensor
            def _(pe):
                def turn_slot(n):
                    wait(pe, turn_read, n - 1)

                def finish(k, t, b, n, bank):
                    pe.wait_ge(low[k], t + 1)
                    turn_slot(n)
                    transposes(pe, m, ps_t[:, bank], split[k][:, b]).then_inc(turn_ready, 1)

                def attend(t, b, n, bank):
                    pe.wait_ge(e_low, t + 1)
                    for c in range(5):
                        if c < 4:
                            turn_slot(n + c)
                            for half in range(2):
                                for j in range(4):
                                    k = 4 * half + j
                                    last = pe.transpose(ps_t[:, (bank + c) % 2, k * P:(k + 1) * P],
                                                        eh[:, b, half, (4 * c + j) * P:(4 * c + j + 1) * P],
                                                        m.ident[:, :])
                            last.then_inc(turn_ready, 1)
                        if c:
                            d = c - 1
                            if d == 0:
                                wait(pe, out_read["a"], t)
                            pe.wait_ge(turn_read, n + d + 1)
                            pairs = [((et[:, b, d, j], et[:, b, d, 4 + j]),
                                      (xa[:, 4 * d + j, 0], xa[:, 4 * d + j, 1])) for j in range(4)]
                            last = product(pe, ps["a"][:, :], pairs, start=d == 0, stop=d == 3)
                    last.then_inc(out_ready["a"], 1)

                def logits_of(t):
                    wait(pe, e_made, t)
                    for c in range(4):
                        q, cols = m.qw[:, at(t * P, P)], slice(512 * c, 512 * c + 512)
                        pe.matmul(ps_l[:, cols], q, m.k_high[:, cols], start=True, stop=False)
                        last = pe.matmul(ps_l[:, cols], q, m.k_low[:, cols], start=False, stop=True)
                    last.then_inc(logits, 1)

                logits_of(0)
                logits_of(1)
                logits_of(2)
                pe.wait_ge(x_loaded, 16 if first else 32)

                def body(g, _):
                    n0 = turns_before(g)
                    with_a = not (isinstance(g, int) and g == 0)
                    for b in range(2):
                        t = 2 * g + b
                        if first:
                            pe.wait_ge(panel_low, t + 1)
                        else:
                            pe.wait_ge(panel_loaded[b], 16 * (g + 1))
                        wait(pe, out_read["r"], t)
                        pe.matmul(ps["r"][:, :], m.ident[:, :], xf[:, at(t), 0], start=True, stop=False)
                        pe.matmul(ps["r"][:, :], m.ident[:, :], xf[:, at(t), 1], start=False, stop=False)
                        pairs = [((panel[:, b, 0, j], panel[:, b, 1, j]), (xf[:, j, 0], xf[:, j, 1])) for j in range(T)]
                        product(pe, ps["r"][:, :], pairs, start=False).then_inc(out_ready["r"], 1)
                    if not is_last(g):
                        logits_of(2 * g + 3)
                    finish("r", 2 * g, 0, n0, 0)
                    if with_a:
                        attend(2 * g - 2, 0, n0 + 1, 1)
                        finish("r", 2 * g + 1, 1, n0 + 5, 1)
                        attend(2 * g - 1, 1, n0 + 6, 0)
                    else:
                        finish("r", 2 * g + 1, 1, n0 + 1, 1)
                    if not (isinstance(g, int) and g >= G - 2):
                        logits_of(2 * g + 4)
                    if with_a:
                        finish("a", 2 * g - 2, 0, n0 + 10, 0)
                        finish("a", 2 * g - 1, 1, n0 + 11, 1)

                groups(pe, body)
                attend(T - 2, 0, ALL, 0)
                attend(T - 1, 1, ALL + 4, 0)
                finish("a", T - 2, 0, ALL + 8, 0)
                finish("a", T - 1, 1, ALL + 9, 1)

            @block.scalar
            def _(act):
                def turn_copy(dst, n, bank):
                    act.wait_ge(turn_ready, n + 1)
                    act.copy(dst.bitcast(F32), ps_t[:, bank].bitcast(F32)).then_inc(turn_read, 1)

                def finish(k, t, b, g, n, bank):
                    wait(act, turned_stored[k][b], 16 * g)
                    turn_copy(turned[k][:, b], n, bank)
                    act.wait_ge(turn_read, n + 1)
                    act.dma_start(m.turned[kinds[k]][at(t)], turned[k][:, b]).then_inc(turned_stored[k][b], 16)

                def take(k, t, b, g, scale):
                    act.wait_ge(out_ready[k], t + 1)
                    wait(act, low[k], t - 1)
                    act.activation(out32[k][:, b], ps[k][:, :], ACT.Copy, scale=scale).then_inc(out_read[k], 1)
                    act.wait_ge(out_read[k], t + 1)
                    if first:
                        wait(act, split_stored[k][b], 16 * g)
                    act.copy(split[k][:, b, 0], out32[k][:, b]).then_inc(high[k], 1)

                def attend(t, b, g, n, bank, par):
                    for c in range(4):
                        turn_copy(et[:, b, c].rearrange("p k n -> p (k n)"), n + c, (bank + c) % 2)
                    take("a", t, b, g, inv[:, 2 * par + b:2 * par + b + 1])

                def e_split(t, b, par):
                    act.wait_ge(e_cut, t + 1)
                    wait(act, out_ready["a"], t - 1)
                    act.copy(eh[:, b, 0], e[:, 2 * par + b]).then_inc(e_high, 1)

                def exponentials(t, i):
                    act.wait_ge(max_done, t + 1)
                    wait(act, e_low, t - 3)
                    act.activation(e[:, i], ps_l[:, :], ACT.Exp, bias=neg_max[:, i:i + 1],
                                   scale=1.0 / (SQ * SQ), accum_out=total[:, i:i + 1]).then_inc(exp_done, 1)
                    act.wait_ge(exp_done, t + 1)
                    act.activation(ps_l[:, :], e[:, i], ACT.Square, accum_out=squares[:, i:i + 1]).then_inc(e_made, 1)

                def panel_split(t, b, g):
                    if not first:
                        return
                    act.wait_ge(raw_loaded[b], 16 * (g + 1))
                    wait(act, out_ready["r"], t - 1)
                    wait(act, panel_stored[b], 16 * g)
                    act.copy(panel[:, b, 0], raw_panel[:, b]).then_inc(panel_high, 1)

                def sum_rows(t, b, par):
                    if not first:
                        return
                    act.wait_ge(adj_loaded, 16 * (t + 1))
                    act.activation(adj_row[:, :], adj_row[:, :], ACT.Copy,
                                   accum_out=row_sum[:, 2 * par + b:2 * par + b + 1]).then_inc(row_summed, 1)

                def take_r(t, b, g):
                    if first:
                        act.wait_ge(inv_row, t + 1)
                    take("r", t, b, g, m.inv_row[:, at(t)])

                for b in range(2):
                    panel_split(b, b, 0)
                    sum_rows(b, b, 0)
                    exponentials(b, b)

                def body(g, par):
                    n0 = turns_before(g)
                    with_a = not (isinstance(g, int) and g == 0)
                    if with_a:
                        e_split(2 * g - 2, 0, 1 - par)
                        e_split(2 * g - 1, 1, 1 - par)
                    take_r(2 * g, 0, g)
                    if not is_last(g):
                        exponentials(2 * g + 2, 2 * (1 - par))
                        panel_split(2 * g + 2, 0, g + 1)
                        sum_rows(2 * g + 2, 0, 1 - par)
                    take_r(2 * g + 1, 1, g)
                    finish("r", 2 * g, 0, g, n0, 0)
                    if with_a:
                        attend(2 * g - 2, 0, g - 1, n0 + 1, 1, 1 - par)
                    if not is_last(g):
                        exponentials(2 * g + 3, 2 * (1 - par) + 1)
                        panel_split(2 * g + 3, 1, g + 1)
                    finish("r", 2 * g + 1, 1, g, n0 + (5 if with_a else 1), 1)
                    if with_a:
                        attend(2 * g - 1, 1, g - 1, n0 + 6, 0, 1 - par)
                    if not is_last(g):
                        sum_rows(2 * g + 3, 1, 1 - par)
                    if with_a:
                        finish("a", 2 * g - 2, 0, g - 1, n0 + 10, 0)
                        finish("a", 2 * g - 1, 1, g - 1, n0 + 11, 1)

                groups(act, body)
                e_split(T - 2, 0, 1)
                e_split(T - 1, 1, 1)
                attend(T - 2, 0, G - 1, ALL, 0, 1)
                attend(T - 1, 1, G - 1, ALL + 4, 0, 1)
                finish("a", T - 2, 0, G - 1, ALL + 8, 0)
                finish("a", T - 1, 1, G - 1, ALL + 9, 1)
                for k in "ra":
                    for b in range(2):
                        act.wait_ge(turned_stored[k][b], 16 * G)

            @block.gpsimd
            def _(pool):
                def e_cut_down(t, b, par):
                    pool.wait_ge(top_found, t + 1)
                    pool.tensor_tensor(e[:, 2 * par + b], e[:, 2 * par + b], below[:, b, 0:N],
                                       ALU.subtract).then_inc(e_cut, 1)

                def e_split(t, b, par):
                    pool.wait_ge(e_high, t + 1)
                    pool.tensor_tensor(eh[:, b, 1], e[:, 2 * par + b], eh[:, b, 0], ALU.subtract).then_inc(e_low, 1)

                def split_low(k, t, b):
                    pool.wait_ge(high[k], t + 1)
                    pool.tensor_tensor(split[k][:, b, 1], out32[k][:, b], split[k][:, b, 0],
                                       ALU.subtract).then_inc(low[k], 1)

                def adj_low(t, b):
                    if not first:
                        return
                    pool.wait_ge(panel_high, t + 1)
                    pool.tensor_tensor(panel[:, b, 1], raw_panel[:, b], panel[:, b, 0], ALU.subtract).then_inc(panel_low, 1)

                adj_low(0, 0)
                adj_low(1, 1)

                def body(g, par):
                    with_a = not (isinstance(g, int) and g == 0)
                    if with_a:
                        e_cut_down(2 * g - 2, 0, 1 - par)
                        e_cut_down(2 * g - 1, 1, 1 - par)
                        e_split(2 * g - 2, 0, 1 - par)
                        e_split(2 * g - 1, 1, 1 - par)
                    for b in range(2):
                        split_low("r", 2 * g + b, b)
                        if not is_last(g):
                            adj_low(2 * g + 2 + b, b)
                    for b in range(2):
                        if with_a:
                            split_low("a", 2 * g - 2 + b, b)

                groups(pool, body)
                for b in range(2):
                    e_cut_down(T - 2 + b, b, 1)
                for b in range(2):
                    e_split(T - 2 + b, b, 1)
                for b in range(2):
                    split_low("a", T - 2 + b, b)

            @block.vector
            def _(dve):
                def peak(t, i):
                    dve.wait_ge(logits, t + 1)
                    dve.tensor_reduce(row_max[:, i:i + 1], ps_l[:, :], AX.X, ALU.max)
                    dve.drain()
                    dve.tensor_scalar(neg_max[:, i:i + 1], row_max[:, i:i + 1], -1.0 / (SQ * SQ), math.log(SE),
                                      ALU.mult, ALU.add).then_inc(max_done, 1)

                def body(g, par):
                    pair = slice(2 * par, 2 * par + 2)
                    if not is_last(g):
                        peak(2 * g + 2, 2 * (1 - par))
                    if first:
                        dve.wait_ge(row_summed, 2 * g + 2)
                        dve.tensor_scalar(hit[:, pair], row_sum[:, pair], 1.0, 1e-12, ALU.add, ALU.max)
                        dve.drain()
                        dve.reciprocal(m.inv_row[:, at(2 * g, 2)], hit[:, pair]).then_inc(inv_row, 2)
                    dve.wait_ge(e_made, 2 * g + 2)
                    dve.tensor_scalar(goal[:, pair], total[:, pair], P_TOP, None, ALU.mult)
                    dve.tensor_scalar(tmp[:, pair], total[:, pair], 0.999 * (1 - P_TOP) / N, None, ALU.mult)
                    dve.drain()
                    dve.tensor_copy(low_bits[:, 2], tmp[:, pair].bitcast(I32))
                    dve.reciprocal(hit[:, pair], goal[:, pair])
                    dve.drain()
                    dve.scalar_tensor_tensor(out=tmp[:, pair], in0=squares[:, pair], scalar=1.001, in1=hit[:, pair],
                                             op0=ALU.mult, op1=ALU.mult)
                    dve.drain()
                    dve.tensor_scalar(tmp[:, pair], tmp[:, pair], 1.001 * SE, None, ALU.min)
                    dve.drain()
                    dve.tensor_tensor(span[:, pair], tmp[:, pair].bitcast(I32), low_bits[:, 2], ALU.subtract)
                    dve.drain()
                    for k in range(probes + 1):
                        dve.tensor_scalar(half_span[:, k, :], span[:, pair], 0.5 ** (k + 1), None, ALU.mult)
                    dve.tensor_copy(low_bits[:, 0], low_bits[:, 2])
                    dve.memset(raised[:, :], 0.0)
                    for k in range(probes + 1):
                        dve.drain()
                        for b in range(2):
                            dve.scalar_tensor_tensor(out=mid_bits[:, b:b + 1], in0=raised[:, b:b + 1],
                                                     scalar=half_span[:, k, b:b + 1], in1=low_bits[:, k % 2, b:b + 1],
                                                     op0=ALU.add, op1=ALU.add)
                        dve.tensor_tensor(low_bits[:, (k + 1) % 2], low_bits[:, k % 2], raised[:, :], ALU.add)
                        if k == probes:
                            break
                        dve.drain()
                        for b in range(2):
                            i = 2 * par + b
                            dve.scalar_tensor_tensor(out=unused[:, :], in0=e[:, i],
                                                     scalar=mid_bits[:, b:b + 1].bitcast(F32), in1=e[:, i],
                                                     op0=ALU.is_ge, op1=ALU.mult, accum_out=f[:, i:i + 1])
                            dve.drain()
                        for b in range(2):
                            i = 2 * par + b
                            dve.scalar_tensor_tensor(out=raised[:, b:b + 1], in0=f[:, i:i + 1], scalar=goal[:, i:i + 1],
                                                     in1=half_span[:, k, b:b + 1], op0=ALU.is_ge, op1=ALU.mult)
                        if k == (4 if first else 6) and not is_last(g):
                            peak(2 * g + 3, 2 * (1 - par) + 1)
                    dve.drain()
                    low = low_bits[:, (probes + 1) % 2]
                    dve.tensor_scalar(hit[:, pair], half_span[:, probes], 2.0, 1024.0, ALU.mult, ALU.add)
                    dve.drain()
                    dve.tensor_tensor(mid_bits[:, :], hit[:, pair], low, ALU.add)
                    dve.drain()
                    wait(dve, e_cut, 2 * g)
                    for b in range(2):
                        i = 2 * par + b
                        dve.scalar_tensor_tensor(out=below[:, b, 0:N], in0=e[:, i],
                                                 scalar=mid_bits[:, b:b + 1].bitcast(F32), in1=e[:, i],
                                                 op0=ALU.is_lt, op1=ALU.mult, accum_out=under[:, i:i + 1])
                    dve.drain()
                    dve.tensor_tensor(kept[:, pair], total[:, pair], under[:, pair], ALU.subtract)
                    dve.drain()
                    for _round in range(rounds):
                        take_top(par)
                    dve.tensor_scalar(mid_bits[:, :], low, -1024.0, None, ALU.add)
                    dve.tensor_tensor(tmp[:, pair], goal[:, pair], kept[:, pair], ALU.subtract)
                    dve.drain()
                    dve.reciprocal(hit[:, pair], mid_bits[:, :].bitcast(F32))
                    dve.tensor_scalar(under[:, pair], tmp[:, pair], 0.0, None, ALU.is_gt)
                    dve.drain()
                    dve.tensor_tensor(hit[:, pair], hit[:, pair], tmp[:, pair], ALU.mult)
                    dve.drain()
                    dve.tensor_scalar(hit[:, pair], hit[:, pair], 0.125, 1.6, ALU.mult, ALU.add)
                    dve.drain()
                    dve.tensor_tensor(hit[:, pair], hit[:, pair], under[:, pair], ALU.mult)
                    dve.drain()
                    dve.tensor_reduce(flags[:, 0:1], hit[:, pair], AX.X, ALU.max)
                    dve.drain()
                    dve.transpose(flags_t[:, :], flags[:, :])
                    dve.drain()
                    dve.tensor_reduce(more[:, :], flags_t[:, :], AX.X, ALU.max)
                    dve.drain()
                    dve.tensor_scalar(more_int[:, :], more[:, :], float(N // 8), None, ALU.min)
                    dve.drain()
                    extra = sum(dve.value_load(more_int[q:q + 1, 0:1], min_val=0, max_val=N // 8)
                                for q in range(0, P, 32))
                    with dve.If(extra > 0):
                        with dve.Fori(0, extra):
                            take_top(par)
                    for b in range(2):
                        i = 2 * par + b
                        dve.reciprocal(inv[:, i:i + 1], kept[:, i:i + 1]).then_inc(top_found, 1)

                def take_top(par):
                    pair = [(b, slice(2 * par + b, 2 * par + b + 1)) for b in range(2)]
                    for b, one in pair:
                        dve.max(top[:, b], below[:, b])
                        dve.tensor_copy(prefix[:, b, 0:1], kept[:, one])
                    dve.drain()
                    for b, one in pair:
                        dve.tensor_tensor_scan(prefix[:, b, 1:9], top[:, b], top[:, b], kept[:, one], ALU.add, ALU.max)
                    dve.drain()
                    for b, one in pair:
                        dve.scalar_tensor_tensor(out=wanted[:, b], in0=prefix[:, b, 0:8], scalar=goal[:, one], in1=top[:, b],
                                                 op0=ALU.is_lt, op1=ALU.mult, accum_out=picked[:, one])
                    dve.drain()
                    both = slice(2 * par, 2 * par + 2)
                    dve.tensor_tensor(kept[:, both], kept[:, both], picked[:, both], ALU.add)
                    for b, _ in pair:
                        dve.match_replace(below[:, b], wanted[:, b], below[:, b], 0.0)
                    dve.drain()

                dve.memset(below[:, :, N:N + 8], 0.0)
                dve.memset(flags[:, :], 0.0)
                dve.drain()
                peak(0, 0)
                peak(1, 1)
                groups(dve, body)


def stage_w2(nc, m, w2):
    with ExitStack() as ctx:
        raw = m.sb("w2_raw", [P, 1, P], F32, ctx)
        loaded, high, low = m.sem("w2_loaded"), m.sem("w2_high"), m.sem("w2_low")
        with nc.Block() as block:
            @block.sync
            def _(sp):
                for r in range(2):
                    for c in range(2):
                        sp.dma_start(raw[r * DA:(r + 1) * DA, :, c * DA:(c + 1) * DA], w2).then_inc(loaded, 16)

            @block.scalar
            def _(act):
                act.wait_ge(loaded, 64)
                act.activation(m.w2[:, 0], raw[:, :, :], ACT.Copy, scale=SW).then_inc(high, 1)

            @block.vector
            def _(dve):
                dve.wait_ge(high, 1)
                dve.scalar_tensor_tensor(out=m.w2[:, 1], in0=raw[:, :, :], scalar=SW, in1=m.w2[:, 0],
                                         op0=ALU.mult, op1=ALU.subtract).then_inc(low, 1)



def load_row_vector(sp, tile, vector, sem):
    sp.dma_start(tile, vector.partition_broadcast(P)).then_inc(sem, 16)


def stage_l0_output(nc, m, a, x_view):
    with ExitStack() as ctx:
        sb = lambda name, shape, dt=F32: m.sb(f"o_{name}", shape, dt, ctx)
        sem = lambda name: m.sem(f"o_{name}")
        names = {XF1: "L0_gnn_U1_0", XA1: "L0_gnn_U2_0", XF2: "L0_gnn_U1_1", XA2: "L0_gnn_U2_1"}
        gamma, beta = sb("gamma", [P, D]), sb("beta", [P, D])
        vectors = sem("vectors")

        def early_loads(sp):
            load_row_vector(sp, gamma[:, :], a["L0_gnn_gamma"], vectors)
            load_row_vector(sp, beta[:, :], a["L0_gnn_beta"], vectors)

        u = {k: sb(f"u{k}", [P, 2, DC, D], F16) for k in names}
        w = sb("w", [P, 2, DC, D], F16)
        chunked = lambda v: v.rearrange("(c p) n -> p c n", p=P)
        stage_weights(nc, m, "ow", [chunked(a[names[k]]) for k in names] + [chunked(a["L1_gnn_weight"])],
                      [u[k] for k in names] + [w], early_loads)
        parts = sb("parts", [P, 2, 4, 2, DC, P], F16)
        h = sb("h", [P, 2, 2, D], F16)
        x, x1 = sb("x", [P, 2, D]), sb("x1", [P, 2, D])
        adj_row = sb("adj_row", [P, 2, N])
        near_value, near_index = sb("near_value", [P, 8]), sb("near_index", [P, 8], U32)
        row_head = sb("row_head", [P, 1])
        h2, sup = sb("h2", [P, 2, D]), sb("sup", [P, 2, D])
        sup_split = sb("sup_split", [P, 2, 2, D], F16)
        ps_y = m.ps("o_y", [P, 2, D], F32, ctx)
        ps_s = m.ps("o_s", [P, 2, D], F32, ctx)
        first_norm = Norm(m, "o1", ctx, 1.0, EPS * (SX * SW) ** 2)
        second_norm = Norm(m, "o2", ctx, SX)
        turner = Turner(m, "ot", ctx)
        loaded = [sem(f"loaded{b}") for b in range(2)]
        y_ready, x1_made, h2_made = sem("y_ready"), sem("x1_made"), sem("h2_made")
        row_loaded = [sem(f"row_loaded{b}") for b in range(2)]
        ranked = sem("ranked")
        s_ready, s_read, s_high, s_low = sem("s_ready"), sem("s_read"), sem("s_high"), sem("s_low")
        x1_stored = [sem(f"x1_stored{b}") for b in range(2)]
        s_stored = [sem(f"s_stored{b}") for b in range(2)]

        with nc.Block() as block:
            @block.sync
            def _(sp):
                def body(g, _):
                    for b in range(2):
                        t = 2 * g + b
                        wait(sp, x1_made, t - 1)
                        sp.dma_start(parts[:, b].rearrange("p k a c n -> p k (a c n)"),
                                     m.turned[XF1:XA2 + 1, at(t)].rearrange("k o p n -> p (k o) n")).then_inc(loaded[b], 16)
                        sp.dma_start(h[:, b], m.nat[H1][at(t)]).then_inc(loaded[b], 16)
                        sp.dma_start(x[:, b], x_view[at(t)]).then_inc(loaded[b], 16)
                        wait(sp, ranked, t - 1)
                        sp.dma_start(adj_row[:, b], m.adj_rows[at(t)]).then_inc(row_loaded[b], 16)
                groups(sp, body)

            @block.tensor
            def _(pe):
                def y_product(g, b):
                    t = 2 * g + b
                    pe.wait_ge(loaded[b], 48 * (g + 1))
                    wait(pe, x1_made, t - 1)
                    pe.matmul(ps_y[:, b], m.ident_sw[:, :], h[:, b, 0], start=True, stop=False)
                    pe.matmul(ps_y[:, b], m.ident_sw[:, :], h[:, b, 1], start=False, stop=False)
                    pairs = [((parts[:, b, i, 0, c], parts[:, b, i, 1, c]), (u[k][:, 0, c], u[k][:, 1, c]))
                             for i, k in enumerate(names) for c in range(DC)]
                    product(pe, ps_y[:, b], pairs, start=False).then_inc(y_ready, 1)

                def s_product(t, b):
                    turner.tensor_turn(pe, t, b)
                    pe.wait_ge(turner.read, t + 1)
                    wait(pe, s_read, t - 1)
                    product(pe, ps_s[:, b], turner.pairs(b, w)).then_inc(s_ready, 1)

                def body(g, _):
                    y_product(g, 0)
                    if not (isinstance(g, int) and g == 0):
                        s_product(2 * g - 1, 1)
                    y_product(g, 1)
                    s_product(2 * g, 0)
                groups(pe, body)
                s_product(T - 1, 1)

            @block.vector
            def _(dve):
                dve.wait_ge(vectors, 32)

                def body(g, _):
                    for b in range(2):
                        t = 2 * g + b
                        dve.drain()
                        dve.wait_ge(row_loaded[b], 16 * (g + 1))
                        dve.tensor_copy(row_head[:, :], adj_row[:, b, 0:1])
                        dve.max(near_value[:, :], adj_row[:, b])
                        dve.drain()
                        dve.max_index(near_index[:, :], near_value[:, :], adj_row[:, b]).then_inc(ranked, 1)
                        dve.drain()
                        dve.tensor_copy(m.near_value[:, at(8 * t, 8)], near_value[:, :])
                        dve.tensor_copy(m.near_index[:, at(8 * t, 8)], near_index[:, :])
                        dve.wait_ge(y_ready, t + 1)
                        dve.wait_ge(loaded[b], 48 * (g + 1))
                        first_norm.vector(dve, t, b, ps_y[:, b])
                        dve.drain()
                        wait(dve, h2_made, t - 1)
                        wait(dve, x1_stored[b], 16 * g)
                        dve.tensor_scalar(x1[:, b], ps_y[:, b], first_norm.moments[:, b, 0:1],
                                          first_norm.parts[:, b, 1:2], ALU.subtract, ALU.mult)
                        dve.drain()
                        dve.tensor_tensor(x1[:, b], x1[:, b], gamma[:, :], ALU.mult)
                        dve.drain()
                        dve.tensor_tensor(x1[:, b], x1[:, b], beta[:, :], ALU.add)
                        dve.drain()
                        dve.tensor_tensor(x1[:, b], x1[:, b], x[:, b], ALU.add).then_inc(x1_made, 1)
                        dve.drain()
                        second_norm.vector(dve, t, b, x1[:, b])
                groups(dve, body)

            @block.gpsimd
            def _(pool):
                def support_low(t, b):
                    pool.wait_ge(s_high, t + 1)
                    pool.tensor_tensor(sup_split[:, b, 1], sup[:, b], sup_split[:, b, 0], ALU.subtract).then_inc(s_low, 1)

                def body(g, _):
                    for b in range(2):
                        t = 2 * g + b
                        first_norm.gpsimd(pool, t, b)
                        second_norm.gpsimd(pool, t, b)
                        turner.gpsimd_low(pool, t, b, h2[:, b])
                        support_low(t, b)
                groups(pool, body)

            @block.scalar
            def _(act):
                def body(g, _):
                    for b in range(2):
                        t = 2 * g + b
                        act.wait_ge(x1_made, t + 1)
                        act.dma_start(m.x1[at(t)], x1[:, b]).then_inc(x1_stored[b], 16)
                        act.wait_ge(second_norm.done, t + 1)
                        wait(act, turner.low, t - 1)
                        second_norm.relu(act, h2[:, b], x1[:, b], b).then_inc(h2_made, 1)
                        act.wait_ge(h2_made, t + 1)
                        turner.scalar_high(act, t, b, h2[:, b])
                        turner.scalar_copy(act, t, b)
                        act.wait_ge(s_ready, t + 1)
                        wait(act, s_low, t - 1)
                        act.activation(sup[:, b], ps_s[:, b], ACT.Copy, scale=SS / (SX * SW)).then_inc(s_read, 1)
                        act.wait_ge(s_read, t + 1)
                        wait(act, s_stored[b], 16 * g)
                        act.copy(sup_split[:, b, 0], sup[:, b]).then_inc(s_high, 1)
                        act.wait_ge(s_low, t + 1)
                        act.dma_start(m.nat[SUP][at(t)], sup_split[:, b]).then_inc(s_stored[b], 16)
                groups(act, body)
                for b in range(2):
                    act.wait_ge(x1_stored[b], 16 * G)
                    act.wait_ge(s_stored[b], 16 * G)


class Sequence:

    def __init__(self, nc, m, a, name, ctx, early=None):
        sb = lambda n, shape, dt=F32: m.sb(f"{name}_{n}", shape, dt, ctx)
        sem = lambda n: m.sem(f"{name}_{n}")
        self.m, self.a = m, a
        self.w = sb("w", [P, 2, DC, D], F16)
        stage_weights(nc, m, f"{name}w", [a[n].rearrange("(c p) n -> p c n", p=P) for n in ("L3_gnn_W_seq", "L3_gnn_W_out")],
                      [self.w, m.w_out], early)
        self.a_rows = sb("a_rows", [P, 2, 1, DH3])
        self.h, self.row = sb("h", [P, 2, D]), sb("row", [P, 2, ROW3])
        self.weighed = sb("weighed", [P, 2, HEADS3, DH3])
        self.ps_s = m.ps(f"{name}_s", [P, 2, D], F32, ctx)
        self.norm, self.turner = Norm(m, f"{name}n", ctx, SX), Turner(m, f"{name}t", ctx)
        self.stored = [sem(f"stored{b}") for b in range(2)]
        self.vectors = sem("vectors")
        self.h_made, self.ready, self.read, self.scored = sem("h_made"), sem("ready"), sem("read"), sem("scored")

    def sync_load(self, sp):
        load_row_vector(sp, self.a_rows[:, 0, 0], self.a["L3_gnn_a1"], self.vectors)
        load_row_vector(sp, self.a_rows[:, 1, 0], self.a["L3_gnn_a2"], self.vectors)

    def scalar_high(self, act, t, b, x3):
        act.wait_ge(self.norm.done, t + 1)
        wait(act, self.turner.low, t - 1)
        self.norm.relu(act, self.h[:, b], x3, b).then_inc(self.h_made, 1)
        act.wait_ge(self.h_made, t + 1)
        self.turner.scalar_high(act, t, b, self.h[:, b])

    def gpsimd_low(self, pool, t, b):
        self.turner.gpsimd_low(pool, t, b, self.h[:, b])

    def tensor_product(self, pe, t, b):
        pe.wait_ge(self.turner.read, t + 1)
        wait(pe, self.read, t - 1)
        product(pe, self.ps_s[:, b], self.turner.pairs(b, self.w)).then_inc(self.ready, 1)

    def scalar_take(self, act, t, b, g):
        act.wait_ge(self.ready, t + 1)
        wait(act, self.stored[b], 16 * g)
        act.activation(self.row[:, b, 0:D], self.ps_s[:, b], ACT.Copy, scale=SS / (SX * SW)).then_inc(self.read, 1)

    def vector_scores(self, dve, t, b):
        m = self.m
        dve.wait_ge(self.read, t + 1)
        seq = self.row[:, b, 0:D].rearrange("p (h d) -> p h d", d=DH3)
        for i in range(2):
            dve.tensor_tensor(self.weighed[:, i], seq, self.a_rows[:, i].broadcast_to([P, HEADS3, DH3]), ALU.mult)
        dve.drain()
        dve.tensor_reduce(m.score1[:, at(t)], self.weighed[:, 0], AX.X, ALU.add)
        dve.tensor_reduce(m.score2[:, at(t)], self.weighed[:, 1], AX.X, ALU.add)
        dve.drain()
        dve.tensor_copy(self.row[:, b, D:ROW3], m.score2[:, at(t)]).then_inc(self.scored, 1)

    def scalar_store(self, act, t, b):
        act.wait_ge(self.scored, t + 1)
        act.dma_start(self.m.table[at(t)], self.row[:, b]).then_inc(self.stored[b], 16)

    def scalar_end(self, act):
        for b in range(2):
            act.wait_ge(self.stored[b], 16 * G)


def stage_l1(nc, m, a):
    with ExitStack() as ctx:
        sb = lambda name, shape, dt=F32: m.sb(f"l_{name}", shape, dt, ctx)
        sem = lambda name: m.sem(f"l_{name}")
        sup = sb("sup", [P, T, 2, D], F16)
        panel = sb("panel", [P, 2, 2, T, P], F16)
        bias = sb("bias", [P, D])
        whole = sem("whole")

        def early_loads(sp):
            for part in (slice(0, T // 2), slice(T // 2, T)):
                sp.dma_start(sup[:, part].rearrange("p t a n -> p t (a n)"),
                             m.nat[SUP, part].rearrange("t p a n -> p t (a n)")).then_inc(whole, 16)
            load_row_vector(sp, bias[:, :], a["L1_gnn_bias"], whole)

        seq = Sequence(nc, m, a, "ls", ctx, early_loads)
        x1, x2, x3 = sb("x1", [P, 2, D]), sb("x2", [P, 2, D]), sb("x3", [P, 2, D])
        h3 = sb("h3", [P, 2, D])
        ps_o = m.ps("l_o", [P, 2, D], F32, ctx)
        norm = Norm(m, "ln", ctx, 1.0)
        loaded = [sem(f"loaded{b}") for b in range(2)]
        ready, x2_made, h3_made, x3_made = sem("ready"), sem("x2_made"), sem("h3_made"), sem("x3_made")
        x2_stored = [sem(f"x2_stored{b}") for b in range(2)]
        x3_stored = [sem(f"x3_stored{b}") for b in range(2)]

        def lagging(g, b, lag):
            t = 2 * g + b - lag
            if isinstance(t, int) and t < 0:
                return None
            b2 = (b - lag) % 2
            return t, b2, g - (lag - b + b2) // 2

        with nc.Block() as block:
            @block.sync
            def _(sp):
                seq.sync_load(sp)

                def body(g, _):
                    for b in range(2):
                        t = 2 * g + b
                        wait(sp, x2_made, t - 1)
                        sp.dma_start(panel[:, b], m.panels[at(t)]).then_inc(loaded[b], 16)
                        sp.dma_start(x1[:, b], m.x1[at(t)]).then_inc(loaded[b], 16)
                groups(sp, body)

            @block.tensor
            def _(pe):
                pe.wait_ge(whole, 48)

                def body(g, _):
                    for b in range(2):
                        t = 2 * g + b
                        pe.wait_ge(loaded[b], 32 * (g + 1))
                        wait(pe, x2_made, t - 1)
                        pairs = [((panel[:, b, 0, j], panel[:, b, 1, j]), (sup[:, j, 0], sup[:, j, 1])) for j in range(T)]
                        product(pe, ps_o[:, b], pairs).then_inc(ready, 1)
                        one, two = lagging(g, b, 1), lagging(g, b, 2)
                        if one:
                            seq.turner.tensor_turn(pe, one[0], one[1])
                        if two:
                            seq.tensor_product(pe, two[0], two[1])
                groups(pe, body)
                seq.turner.tensor_turn(pe, T - 1, 1)
                seq.tensor_product(pe, T - 2, 0)
                seq.tensor_product(pe, T - 1, 1)

            @block.vector
            def _(dve):
                dve.wait_ge(whole, 48)
                dve.wait_ge(seq.vectors, 32)

                def body(g, _):
                    for b in range(2):
                        t = 2 * g + b
                        dve.wait_ge(ready, t + 1)
                        dve.wait_ge(loaded[b], 32 * (g + 1))
                        wait(dve, x2_stored[b], 16 * g)
                        dve.scalar_tensor_tensor(out=x2[:, b], in0=ps_o[:, b], scalar=1.0 / SS, in1=x1[:, b],
                                                 op0=ALU.mult, op1=ALU.add)
                        dve.drain()
                        dve.tensor_tensor(x2[:, b], x2[:, b], bias[:, :], ALU.add).then_inc(x2_made, 1)
                        dve.drain()
                        norm.vector(dve, t, b, x2[:, b])
                        dve.wait_ge(h3_made, t + 1)
                        wait(dve, x3_stored[b], 16 * g)
                        dve.tensor_tensor(x3[:, b], h3[:, b], x2[:, b], ALU.add).then_inc(x3_made, 1)
                        dve.drain()
                        seq.norm.vector(dve, t, b, x3[:, b])
                        three = lagging(g, b, 3)
                        if three:
                            seq.vector_scores(dve, three[0], three[1])
                groups(dve, body)
                for t in (T - 3, T - 2, T - 1):
                    seq.vector_scores(dve, t, t % 2)

            @block.gpsimd
            def _(pool):
                def body(g, _):
                    for b in range(2):
                        norm.gpsimd(pool, 2 * g + b, b)
                        seq.norm.gpsimd(pool, 2 * g + b, b)
                        seq.gpsimd_low(pool, 2 * g + b, b)
                groups(pool, body)

            @block.scalar
            def _(act):
                def body(g, _):
                    for b in range(2):
                        t = 2 * g + b
                        one, two, three = (lagging(g, b, n) for n in (1, 2, 3))
                        act.wait_ge(x2_made, t + 1)
                        act.dma_start(m.x2[at(t)], x2[:, b]).then_inc(x2_stored[b], 16)
                        act.wait_ge(norm.done, t + 1)
                        norm.relu(act, h3[:, b], x2[:, b], b).then_inc(h3_made, 1)
                        act.wait_ge(x3_made, t + 1)
                        act.dma_start(m.x3[at(t)], x3[:, b]).then_inc(x3_stored[b], 16)
                        seq.scalar_high(act, t, b, x3[:, b])
                        if one:
                            seq.turner.scalar_copy(act, one[0], one[1])
                        if two:
                            seq.scalar_take(act, *two)
                        if three:
                            seq.scalar_store(act, three[0], three[1])
                groups(act, body)
                seq.turner.scalar_copy(act, T - 1, 1)
                seq.scalar_take(act, T - 2, 0, G - 1)
                seq.scalar_store(act, T - 3, 1)
                seq.scalar_take(act, T - 1, 1, G - 1)
                seq.scalar_store(act, T - 2, 0)
                seq.scalar_store(act, T - 1, 1)
                seq.scalar_end(act)
                for b in range(2):
                    act.wait_ge(x2_stored[b], 16 * G)
                    act.wait_ge(x3_stored[b], 16 * G)


def stage_l3_sequence(nc, m, a):
    with ExitStack() as ctx:
        seq = Sequence(nc, m, a, "s", ctx)
        x = m.sb("s_x", [P, 2, D], F32, ctx)
        loaded = [m.sem(f"s_loaded{b}") for b in range(2)]

        with nc.Block() as block:
            @block.sync
            def _(sp):
                seq.sync_load(sp)

                def body(g, _):
                    for b in range(2):
                        t = 2 * g + b
                        wait(sp, seq.h_made, t - 1)
                        sp.dma_start(x[:, b], m.x3[at(t)]).then_inc(loaded[b], 16)
                groups(sp, body)

            @block.vector
            def _(dve):
                dve.wait_ge(seq.vectors, 32)

                def body(g, _):
                    for b in range(2):
                        t = 2 * g + b
                        dve.wait_ge(loaded[b], 16 * (g + 1))
                        wait(dve, seq.h_made, t - 1)
                        seq.norm.vector(dve, t, b, x[:, b])
                        seq.vector_scores(dve, t, b)
                groups(dve, body)

            @block.gpsimd
            def _(pool):
                def body(g, _):
                    for b in range(2):
                        seq.norm.gpsimd(pool, 2 * g + b, b)
                        seq.gpsimd_low(pool, 2 * g + b, b)
                groups(pool, body)

            @block.tensor
            def _(pe):
                def body(g, _):
                    for b in range(2):
                        seq.turner.tensor_turn(pe, 2 * g + b, b)
                        seq.tensor_product(pe, 2 * g + b, b)
                groups(pe, body)

            @block.scalar
            def _(act):
                def body(g, _):
                    for b in range(2):
                        t = 2 * g + b
                        seq.scalar_high(act, t, b, x[:, b])
                        seq.turner.scalar_copy(act, t, b)
                        seq.scalar_take(act, t, b, g)
                        seq.scalar_store(act, t, b)
                groups(act, body)
                seq.scalar_end(act)


def stage_l3_flags(nc, m):
    m.flag3 = m.sb("flag3", [P, 2])
    with ExitStack() as ctx:
        sb = lambda name, shape: m.sb(f"f3_{name}", shape, F32, ctx)
        gap, extent, bound, widest = sb("gap", [P, T]), sb("extent", [P, 2]), sb("bound", [P, 2]), sb("widest", [P, 2])
        reduced, spread, done = m.sem("f3_reduced"), m.sem("f3_spread"), m.sem("f3_done")
        values = m.near_value[:, :].rearrange("p (t k) -> p t k", k=8)
        with nc.Block() as block:
            @block.vector
            def _(dve):
                dve.tensor_tensor(gap[:, :], values[:, :, NEAR], values[:, :, 0], ALU.subtract)
                dve.tensor_reduce(extent[:, 0:1], m.score2[:, :, :], AX.XY, ALU.max)
                dve.tensor_reduce(extent[:, 1:2], m.score2[:, :, :], AX.XY, ALU.min)
                dve.drain()
                dve.tensor_reduce(bound[:, 0:1], gap[:, :], AX.X, ALU.max)
                dve.scalar_tensor_tensor(out=bound[:, 1:2], in0=extent[:, 1:2], scalar=-1.0, in1=extent[:, 0:1],
                                         op0=ALU.mult, op1=ALU.max).then_inc(reduced, 1)
                dve.wait_ge(spread, 1)
                dve.tensor_scalar(extent[:, 0:1], widest[:, 1:2], 2.0 / SS, 110.0, ALU.mult, ALU.add)
                dve.drain()
                dve.scalar_tensor_tensor(out=extent[:, 1:2], in0=widest[:, 0:1], scalar=-MASK, in1=extent[:, 0:1],
                                         op0=ALU.mult, op1=ALU.add)
                dve.drain()
                dve.tensor_scalar(m.flag3[:, 0:1], extent[:, 1:2], 0.0, None, ALU.is_lt)
                dve.drain()
                dve.tensor_scalar(m.flag3[:, 1:2], m.flag3[:, 0:1], -1.0, 1.0, ALU.mult, ALU.add).then_inc(done, 1)

            @block.gpsimd
            def _(pool):
                pool.wait_ge(reduced, 1)
                pool.partition_all_reduce(widest[:, :], bound[:, :], P, bass.bass_isa.ReduceOp.max).then_inc(spread, 1)


def stage_l3_near(nc, m, a, out_view):
    K = NEAR
    with ExitStack() as ctx:
        sb = lambda name, shape, dt=F32: m.sb(f"z_{name}", shape, dt, ctx)
        sem = lambda name: m.sem(f"z_{name}")
        w = m.w_out
        bias = sb("bias", [P, 2, D])
        index = sb("index", [P, 2, 16], U32)
        near = sb("near", [P, 2, 2, K, ROW3])
        score, weight = sb("score", [P, 2, K, HEADS3]), sb("weight", [P, 2, K, HEADS3])
        mask = sb("mask", [P, 2, K])
        peak, total, inv = (sb(n, [P, 2, HEADS3]) for n in ("peak", "total", "inv"))
        hidden, x3 = sb("hidden", [P, 2, D]), sb("x3", [P, 2, 2, D])
        z, neg, ez, res = sb("z", [P, 2, D]), sb("neg", [P, 2, D]), sb("ez", [P, 2, D]), sb("res", [P, 2, 2, D])
        ps_z = m.ps("z_z", [P, 2, D], F32, ctx)
        turner = Turner(m, "zt", ctx)
        vectors, indexed = sem("vectors"), sem("indexed")
        gathered = [sem(f"gathered{s}") for s in range(2)]
        loaded = [sem(f"loaded{s}") for s in range(2)]
        stored = [sem(f"stored{s}") for s in range(2)]
        scored, exp_made, hidden_made, z_ready = sem("scored"), sem("exp_made"), sem("hidden_made"), sem("z_ready")
        neg_made, ez_made, res_made = sem("neg_made"), sem("ez_made"), sem("res_made")

        def turn_of(g, par, per_group):
            return (per_group // 2) * (g - par) + per_group

        def is_first(g):
            return isinstance(g, int) and g == 0

        with nc.Block() as block:
            @block.sync
            def _(sp):
                load_row_vector(sp, bias[:, 0], a["L3_gnn_b_out"], vectors)
                load_row_vector(sp, bias[:, 1], a["L3_gnn_b_out"], vectors)

                def store(g, par):
                    sp.wait_ge(res_made, g + 1)
                    sp.dma_start(out_view[at(2 * g, 2)].rearrange("t p n -> p t n"), res[:, par]).then_inc(stored[par], 16)

                def body(g, par):
                    sp.dma_start(x3[:, par], m.x3[at(2 * g, 2)].rearrange("t p n -> p t n")).then_inc(loaded[par], 16)
                    if not is_first(g):
                        store(g - 1, 1 - par)
                groups(sp, body)
                store(G - 1, 1)
                for par in range(2):
                    sp.wait_ge(stored[par], 16 * (G // 2))

            @block.gpsimd
            def _(pool):
                def gather(par):
                    for b in range(2):
                        for k in range(K):
                            pool.indirect_dma_start(near[:, par, b, k], None, m.table.rearrange("t p n -> (t p) n"),
                                                    bass.IndirectOffsetOnAxis(index[:, par, 8 * b + k:8 * b + k + 1], 0)
                                                    ).then_inc(gathered[par], 16)

                pool.wait_ge(indexed, 2)
                gather(0)
                gather(1)

                def body(g, par):
                    more = not (isinstance(g, int) and g >= G - 2)
                    if more:
                        pool.wait_ge(indexed, g + 3)
                    for b in range(2):
                        turner.gpsimd_low(pool, 2 * g + b, b, hidden[:, b])
                    if more:
                        gather(par)
                groups(pool, body)

            @block.tensor
            def _(pe):
                def body(g, _):
                    for b in range(2):
                        turner.tensor_turn(pe, 2 * g + b, b)
                    for b in range(2):
                        pe.wait_ge(turner.read, 2 * g + b + 1)
                        wait(pe, neg_made, g)
                        product(pe, ps_z[:, b], turner.pairs(b, w)).then_inc(z_ready, 1)
                groups(pe, body)

            @block.scalar
            def _(act):
                def exp_neg(g):
                    act.wait_ge(neg_made, g + 1)
                    wait(act, res_made, g)
                    act.activation(ez[:, :], neg[:, :], ACT.Exp).then_inc(ez_made, 1)

                def exp_scores(g):
                    act.wait_ge(scored, g + 1)
                    act.activation(weight[:, :, :, :], score[:, :, :, :], ACT.Exp).then_inc(exp_made, 1)

                exp_scores(0)

                def body(g, _):
                    for b in range(2):
                        act.wait_ge(hidden_made, 2 * g + b + 1)
                        turner.scalar_high(act, 2 * g + b, b, hidden[:, b])
                    for b in range(2):
                        turner.scalar_copy(act, 2 * g + b, b)
                    if not is_first(g):
                        exp_neg(g - 1)
                    if not (isinstance(g, int) and g == G - 1):
                        exp_scores(g + 1)
                groups(act, body)
                exp_neg(G - 1)

            @block.vector
            def _(dve):
                shape = [P, 2, K, HEADS3]

                def take_index(g, par):
                    dve.tensor_copy(index[:, par], m.near_index[:, at(16 * g, 16)]).then_inc(indexed, 1)

                take_index(0, 0)
                take_index(1, 1)

                def scores(g, par):
                    dve.wait_ge(gathered[par], turn_of(g, par, 16 * 2 * K))
                    dve.tensor_tensor(score[:, :, :, :], near[:, par, :, :, D:ROW3],
                                      m.score1[:, at(2 * g, 2)].unsqueeze(2).broadcast_to(shape), ALU.add)
                    values = m.near_value[:, at(16 * g, 16)].rearrange("p (t k) -> p t k", k=8)
                    dve.tensor_scalar(mask[:, :, :], values[:, :, 0:K], -1.0, 1.0, ALU.mult, ALU.add)
                    dve.drain()
                    dve.tensor_scalar(score[:, :, :, :], score[:, :, :, :], 1.0 / SS, None, ALU.mult)
                    dve.tensor_scalar(mask[:, :, :], mask[:, :, :], MASK, None, ALU.mult)
                    dve.drain()
                    dve.scalar_tensor_tensor(out=score[:, :, :, :], in0=score[:, :, :, :], scalar=ALPHA,
                                             in1=score[:, :, :, :], op0=ALU.mult, op1=ALU.max)
                    dve.drain()
                    dve.tensor_tensor(score[:, :, :, :], score[:, :, :, :], mask[:, :, :].unsqueeze(3).broadcast_to(shape),
                                      ALU.add)
                    dve.drain()
                    dve.tensor_reduce(peak[:, :, :], score[:, :, :, :].rearrange("p b k h -> p b h k"), AX.X, ALU.max)
                    dve.drain()
                    dve.tensor_tensor(score[:, :, :, :], score[:, :, :, :], peak[:, :, :].unsqueeze(2).broadcast_to(shape),
                                      ALU.subtract).then_inc(scored, 1)

                def weigh(g, par):
                    if not (isinstance(g, int) and g >= G - 2):
                        take_index(g + 2, par)
                    dve.wait_ge(exp_made, g + 1)
                    dve.tensor_reduce(total[:, :, :], weight[:, :, :, :].rearrange("p b k h -> p b h k"), AX.X, ALU.add)
                    dve.drain()
                    dve.reciprocal(inv[:, :, :], total[:, :, :])
                    dve.drain()
                    dve.tensor_tensor(weight[:, :, :, :], weight[:, :, :, :], inv[:, :, :].unsqueeze(2).broadcast_to(shape),
                                      ALU.mult)
                    dve.drain()
                    for b in range(2):
                        rows = near[:, par, b, :, 0:D].rearrange("p k (h d) -> p k h d", d=DH3)
                        for k in range(K):
                            dve.tensor_tensor(rows[:, k], rows[:, k],
                                              weight[:, b, k].unsqueeze(2).broadcast_to([P, HEADS3, DH3]), ALU.mult)
                    dve.drain()
                    for b in range(2):
                        dve.tensor_tensor(near[:, par, b, 0, 0:D], near[:, par, b, 0, 0:D], near[:, par, b, 1, 0:D], ALU.add)
                    dve.drain()
                    for b in range(2):
                        wait(dve, turner.low, 2 * g - 1 + b)
                        dve.tensor_tensor(hidden[:, b], near[:, par, b, 0, 0:D], near[:, par, b, 2, 0:D],
                                          ALU.add).then_inc(hidden_made, 1)

                def elu_parts(g):
                    dve.wait_ge(z_ready, 2 * g + 2)
                    dve.scalar_tensor_tensor(out=z[:, :, :], in0=ps_z[:, :, :], scalar=1.0 / (SS * SW), in1=bias[:, :, :],
                                             op0=ALU.mult, op1=ALU.add)
                    dve.drain()
                    wait(dve, ez_made, g)
                    dve.tensor_scalar(neg[:, :, :], z[:, :, :], 0.0, None, ALU.min).then_inc(neg_made, 1)
                    dve.tensor_scalar(z[:, :, :], z[:, :, :], 0.0, None, ALU.max)

                def elu(g, par):
                    dve.drain()
                    dve.wait_ge(ez_made, g + 1)
                    wait(dve, stored[par], turn_of(g, par, 16) - 16)
                    dve.scalar_tensor_tensor(out=res[:, par], in0=ez[:, :, :], scalar=-1.0, in1=z[:, :, :],
                                             op0=ALU.add, op1=ALU.add)
                    dve.drain()
                    dve.wait_ge(loaded[par], turn_of(g, par, 16))
                    dve.tensor_tensor(res[:, par], res[:, par], x3[:, par], ALU.add).then_inc(res_made, 1)

                dve.wait_ge(vectors, 32)

                scores(0, 0)

                def body(g, par):
                    weigh(g, par)
                    if not is_first(g):
                        elu_parts(g - 1)
                    if not (isinstance(g, int) and g == G - 1):
                        scores(g + 1, 1 - par)
                    if not is_first(g):
                        elu(g - 1, 1 - par)
                groups(dve, body)
                elu_parts(G - 1)
                elu(G - 1, 1)


def stage_l3_far_rows(nc, m):
    with ExitStack() as ctx:
        sb = lambda name, shape, dt=F32: m.sb(f"v_{name}", shape, dt, ctx)
        sem = lambda name: m.sem(f"v_{name}")
        row, split = sb("row", [P, 2, ROW3]), sb("split", [P, 2, 2, D], F16)
        ident32, score2_t = sb("ident32", [P, P]), sb("score2_t", [HEADS3, N])
        ps_t = m.ps("w_t", [P, 2, D], F32, ctx)
        loaded = [sem(f"loaded{b}") for b in range(2)]
        stored = [sem(f"stored{b}") for b in range(2)]
        made, high, low, t_ready, t_read = sem("made"), sem("high"), sem("low"), sem("t_ready"), sem("t_read")
        scores_stored = sem("scores_stored")

        with nc.Block() as block:
            @block.sync
            def _(sp):
                def body(g, _):
                    for b in range(2):
                        t = 2 * g + b
                        wait(sp, low, t - 1)
                        wait(sp, t_ready, t - 1)
                        sp.dma_start(row[:, b], m.table[at(t)]).then_inc(loaded[b], 16)
                groups(sp, body)
                sp.wait_ge(t_read, T)
                sp.dma_start(m.score2_rows, score2_t[:, :]).then_inc(scores_stored, 16)
                sp.wait_ge(scores_stored, 16)

            @block.vector
            def _(dve):
                dve.tensor_copy(ident32[:, :], m.ident[:, :]).then_inc(made, 1)

            @block.scalar
            def _(act):
                def body(g, _):
                    for b in range(2):
                        t = 2 * g + b
                        act.wait_ge(loaded[b], 16 * (g + 1))
                        wait(act, stored[b], 16 * g)
                        act.copy(split[:, b, 0], row[:, b, 0:D]).then_inc(high, 1)
                        act.wait_ge(t_ready, t + 1)
                        act.copy(score2_t[:, at(t * P, P)], ps_t[0:HEADS3, b, 0:P]).then_inc(t_read, 1)
                        act.wait_ge(low, t + 1)
                        act.dma_start(m.nat[SEQ][at(t)], split[:, b]).then_inc(stored[b], 16)
                groups(act, body)
                for b in range(2):
                    act.wait_ge(stored[b], 16 * G)

            @block.gpsimd
            def _(pool):
                def body(g, _):
                    for b in range(2):
                        pool.wait_ge(high, 2 * g + b + 1)
                        pool.tensor_tensor(split[:, b, 1], row[:, b, 0:D], split[:, b, 0], ALU.subtract).then_inc(low, 1)
                groups(pool, body)

            @block.tensor
            def _(pe):
                pe.wait_ge(made, 1)

                def body(g, _):
                    for b in range(2):
                        t = 2 * g + b
                        pe.wait_ge(loaded[b], 16 * (g + 1))
                        wait(pe, t_read, t - 1)
                        pe.transpose(ps_t[0:HEADS3, b, 0:P], row[:, b, D:ROW3], ident32[:, :]).then_inc(t_ready, 1)
                groups(pe, body)


def stage_l3_attention(nc, m):
    HH = 8
    with ExitStack() as ctx:
        sb = lambda name, shape, dt=F32: m.sb(f"g_{name}", shape, dt, ctx)
        sem = lambda name: m.sem(f"g_{name}")
        seq = sb("seq", [P, T, 2, D], F16)
        row2 = sb("row2", [P, HH, N])
        mask = sb("mask", [P, N])
        sums = sb("sums", [P, 2, N])
        score = sb("score", [P, 1, N])
        eh = sb("eh", [P, 2, 2, N], F16)
        et = sb("et", [P, 2, 4, 8, P], F16)
        bias1 = sb("bias1", [P, HH])
        stat = sb("stat", [P, 4, 2])
        row_max, neg_max, total, inv = (stat[:, i] for i in range(4))
        hidden = sb("hidden", [P, HH * DH3])
        ps_t = m.ps("g_turn", [P, 2, 8 * P], F16, ctx)
        ps_o = m.ps("g_out", [P, 2, 512], F32, ctx)
        seq_loaded, row2_loaded, adj_loaded = sem("seq_loaded"), sem("row2_loaded"), sem("adj_loaded")
        mask_made, bias_made, sum_made, scored = sem("mask_made"), sem("bias_made"), sem("sum_made"), sem("scored")
        e_made, e_high, e_low = sem("e_made"), sem("e_high"), sem("e_low")
        turn_ready, turn_read, out_ready, out_read = sem("turn_ready"), sem("turn_read"), sem("out_ready"), sem("out_read")
        stored, half_done = sem("stored"), sem("half_done")

        def tiles(eng, half, body):
            if half == 0:
                body(0, 0)
                with eng.Fori(1, T) as t:
                    body(t, t)
            else:
                with eng.Fori(0, T) as t:
                    body(t, t + T)

        with nc.Block() as block:
            @block.sync
            def _(sp):
                sp.dma_start(seq[:, :, :, :].rearrange("p t a n -> p t (a n)"),
                             m.nat[SEQ].rearrange("t p a n -> p t (a n)")).then_inc(seq_loaded, 16)
                for half in range(2):
                    wait(sp, out_read, half * T * HH)
                    for k in range(HH):
                        sp.dma_start(row2[:, k], m.score2_rows[half * HH + k].partition_broadcast(P)).then_inc(row2_loaded, 16)

                    def body(t, n):
                        wait(sp, scored, HH * n)
                        sp.dma_start(mask[:, :], m.adj_rows[at(t)]).then_inc(adj_loaded, 16)
                    tiles(sp, half, body)

            @block.vector
            def _(dve):
                for half in range(2):
                    def turn_copies(n, k):
                        for c in range(4):
                            dve.wait_ge(turn_ready, 4 * (HH * n + k) + c + 1)
                            dve.tensor_copy(et[:, k % 2, c].rearrange("p k n -> p (k n)").bitcast(F32),
                                            ps_t[:, c % 2].bitcast(F32)).then_inc(turn_read, 1)

                    def body(t, n):
                        dve.wait_ge(adj_loaded, 16 * (n + 1))
                        dve.tensor_scalar(mask[:, :], mask[:, :], -1.0, 1.0, ALU.mult, ALU.add)
                        dve.drain()
                        dve.tensor_scalar(mask[:, :], mask[:, :], MASK, None, ALU.mult)
                        wait(dve, sum_made, HH * n)
                        dve.tensor_scalar(bias1[:, :], m.score1[:, at(t), half * HH:(half + 1) * HH], 1.0 / SS, None,
                                          ALU.mult).then_inc(bias_made, 1)
                        dve.drain()
                        for k in range(HH + 1):
                            if k < HH:
                                u = HH * n + k
                                dve.wait_ge(sum_made, u + 1)
                                wait(dve, e_made, u)
                                one = slice(k % 2, k % 2 + 1)
                                dve.scalar_tensor_tensor(out=score[:, 0], in0=sums[:, k % 2], scalar=ALPHA,
                                                         in1=sums[:, k % 2], op0=ALU.mult, op1=ALU.max)
                                dve.drain()
                                dve.tensor_tensor(score[:, 0], score[:, 0], mask[:, :], ALU.add)
                                dve.drain()
                                dve.tensor_reduce(row_max[:, one], score[:, 0], AX.X, ALU.max)
                                dve.drain()
                                dve.tensor_scalar(neg_max[:, one], row_max[:, one], -1.0, math.log(SE),
                                                  ALU.mult, ALU.add).then_inc(scored, 1)
                            if k:
                                turn_copies(n, k - 1)
                    tiles(dve, half, body)

            @block.scalar
            def _(act):
                for half in range(2):
                    act.wait_ge(row2_loaded, 16 * HH * (half + 1))

                    def body(t, n):
                        act.wait_ge(bias_made, n + 1)
                        wait(act, stored, 16 * n)
                        for k in range(HH + 2):
                            if k < HH:
                                wait(act, e_low, HH * n + k - 1)
                                act.activation(sums[:, k % 2], row2[:, k], ACT.Identity, bias=bias1[:, k:k + 1],
                                               scale=1.0 / SS).then_inc(sum_made, 1)
                            if 1 <= k <= HH:
                                u, b = HH * n + k - 1, (k - 1) % 2
                                act.wait_ge(scored, u + 1)
                                act.activation(sums[:, b], score[:, 0], ACT.Exp, bias=neg_max[:, b:b + 1],
                                               accum_out=total[:, b:b + 1]).then_inc(e_made, 1)
                                act.wait_ge(e_made, u + 1)
                                wait(act, out_ready, u - 1)
                                act.copy(eh[:, b, 0], sums[:, b]).then_inc(e_high, 1)
                            if k >= 2:
                                u, b = HH * n + k - 2, k % 2
                                act.wait_ge(out_ready, u + 1)
                                act.activation(hidden[:, (k - 2) * DH3:(k - 1) * DH3], ps_o[:, b, 0:DH3], ACT.Copy,
                                               scale=inv[:, b:b + 1]).then_inc(out_read, 1)
                        act.wait_ge(out_read, HH * (n + 1))
                        act.dma_start(m.hidden[at(t), :, half * HH * DH3:(half + 1) * HH * DH3].rearrange("o p n -> p (o n)"),
                                      hidden[:, :]).then_inc(stored, 16)
                    tiles(act, half, body)
                act.wait_ge(stored, 16 * 2 * T)

            @block.gpsimd
            def _(pool):
                for half in range(2):
                    def body(t, n):
                        for k in range(HH):
                            b = k % 2
                            pool.wait_ge(e_high, HH * n + k + 1)
                            pool.tensor_tensor(inv[:, b:b + 1], total[:, b:b + 1], m.minus_one[:, 0:1], ALU.pow)
                            pool.tensor_tensor(eh[:, b, 1], sums[:, b], eh[:, b, 0], ALU.subtract).then_inc(e_low, 1)
                    tiles(pool, half, body)

            @block.tensor
            def _(pe):
                pe.wait_ge(seq_loaded, 16)
                for half in range(2):
                    def body(t, n):
                        for k in range(HH):
                            u, b = HH * n + k, k % 2
                            pe.wait_ge(e_low, u + 1)
                            for c in range(5):
                                if c < 4:
                                    wait(pe, turn_read, 4 * u + c - 1)
                                    for h in range(2):
                                        for j in range(4):
                                            q = 4 * h + j
                                            last = pe.transpose(ps_t[:, c % 2, q * P:(q + 1) * P],
                                                                eh[:, b, h, (4 * c + j) * P:(4 * c + j + 1) * P], m.ident[:, :])
                                    last.then_inc(turn_ready, 1)
                                if c:
                                    d = c - 1
                                    if d == 0:
                                        wait(pe, out_read, u - 1)
                                    pe.wait_ge(turn_read, 4 * u + d + 1)
                                    cols = slice((half * HH + k) * DH3, (half * HH + k + 1) * DH3)
                                    pairs = [((et[:, b, d, j], et[:, b, d, 4 + j]),
                                              (seq[:, 4 * d + j, 0, cols], seq[:, 4 * d + j, 1, cols])) for j in range(4)]
                                    last = product(pe, ps_o[:, b, 0:DH3], pairs, start=d == 0, stop=d == 3)
                            last.then_inc(out_ready, 1)
                    tiles(pe, half, body)


def stage_l3_output(nc, m, a, out_view):
    with ExitStack() as ctx:
        sb = lambda name, shape, dt=F32: m.sb(f"e_{name}", shape, dt, ctx)
        sem = lambda name: m.sem(f"e_{name}")
        w = m.w_out
        bias = sb("bias", [P, D])
        hidden, x3 = sb("hidden", [P, 2, D]), sb("x3", [P, 2, D])
        z, neg, ez, res = sb("z", [P, 2, D]), sb("neg", [P, 2, D]), sb("ez", [P, 2, D]), sb("res", [P, 2, D])
        ps_z = m.ps("e_z", [P, 2, D], F32, ctx)
        turner = Turner(m, "et", ctx)
        vectors = sem("vectors")
        loaded = [sem(f"loaded{b}") for b in range(2)]
        z_ready, neg_made, ez_made, res_made = sem("z_ready"), sem("neg_made"), sem("ez_made"), sem("res_made")
        stored = [sem(f"stored{b}") for b in range(2)]

        with nc.Block() as block:
            @block.sync
            def _(sp):
                load_row_vector(sp, bias[:, :], a["L3_gnn_b_out"], vectors)

                def body(g, _):
                    for b in range(2):
                        t = 2 * g + b
                        wait(sp, res_made, t - 1)
                        sp.dma_start(hidden[:, b], m.hidden[at(t)]).then_inc(loaded[b], 16)
                        sp.dma_start(x3[:, b], m.x3[at(t)]).then_inc(loaded[b], 16)
                groups(sp, body)

            @block.tensor
            def _(pe):
                def body(g, _):
                    for b in range(2):
                        t = 2 * g + b
                        turner.tensor_turn(pe, t, b)
                        pe.wait_ge(turner.read, t + 1)
                        wait(pe, neg_made, t - 1)
                        product(pe, ps_z[:, b], turner.pairs(b, w)).then_inc(z_ready, 1)
                groups(pe, body)

            @block.gpsimd
            def _(pool):
                def body(g, _):
                    for b in range(2):
                        turner.gpsimd_low(pool, 2 * g + b, b, hidden[:, b])
                groups(pool, body)

            @block.vector
            def _(dve):
                dve.wait_ge(vectors, 16)

                def body(g, _):
                    for b in range(2):
                        t = 2 * g + b
                        dve.wait_ge(z_ready, t + 1)
                        dve.scalar_tensor_tensor(out=z[:, b], in0=ps_z[:, b], scalar=1.0 / (SS * SW), in1=bias[:, :],
                                                 op0=ALU.mult, op1=ALU.add)
                        dve.drain()
                        wait(dve, ez_made, t - 1)
                        dve.tensor_scalar(neg[:, b], z[:, b], 0.0, None, ALU.min).then_inc(neg_made, 1)
                        dve.tensor_scalar(z[:, b], z[:, b], 0.0, None, ALU.max)
                        dve.drain()
                        dve.wait_ge(ez_made, t + 1)
                        wait(dve, stored[b], 16 * g)
                        dve.scalar_tensor_tensor(out=res[:, b], in0=ez[:, b], scalar=-1.0, in1=z[:, b],
                                                 op0=ALU.add, op1=ALU.add)
                        dve.drain()
                        dve.tensor_tensor(res[:, b], res[:, b], x3[:, b], ALU.add).then_inc(res_made, 1)
                groups(dve, body)

            @block.scalar
            def _(act):
                def body(g, _):
                    for b in range(2):
                        t = 2 * g + b
                        act.wait_ge(loaded[b], 32 * (g + 1))
                        turner.scalar_high(act, t, b, hidden[:, b])
                        turner.scalar_copy(act, t, b)
                        act.wait_ge(neg_made, t + 1)
                        act.activation(ez[:, b], neg[:, b], ACT.Exp).then_inc(ez_made, 1)
                        act.wait_ge(res_made, t + 1)
                        act.dma_start(out_view[at(t)], res[:, b]).then_inc(stored[b], 16)
                groups(act, body)
                for b in range(2):
                    act.wait_ge(stored[b], 16 * G)


def stage_l2_masks(nc, m, a):
    EP, EC = 125, E_PAIRS // 125
    with ExitStack() as ctx:
        sb = lambda name, shape, dt=F32: m.sb(f"m_{name}", shape, dt, ctx)
        sem = lambda name: m.sem(f"m_{name}")
        index = sb("index", [EP, EC, 2], I32)
        subj, obj = sb("subj", [EP, EC]), sb("obj", [EP, EC])
        count_int, count = sb("count_int", [EP, N], I32), sb("count", [EP, N])
        subj_hot, obj_hot = sb("subj_hot", [EP, 2, P], F16), sb("obj_hot", [EP, 2, N], F16)
        off_diag, diag = sb("off_diag", [P, P]), sb("diag", [P, P])
        adj, factor, shift = sb("adj", [P, N]), sb("factor", [P, N]), sb("shift", [P, N])
        related = m.ps("m_related", [P, N], F32, ctx)
        loaded, counted, hot, used = sem("loaded"), sem("counted"), sem("hot"), sem("used")
        adj_loaded, made, stored = sem("adj_loaded"), sem("made"), sem("stored")

        def tiles(eng, body):
            body(0)
            with eng.Fori(1, T) as t:
                body(t)

        with nc.Block() as block:
            @block.sync
            def _(sp):
                sp.dma_start(index[:, :, :], a["L2_gnn_rel_pair_index"].rearrange("(p c) i -> p c i", p=EP)).then_inc(loaded, 16)

                def body(t):
                    wait(sp, made, t)
                    sp.dma_start(adj[:, :], m.adj_rows[at(t)]).then_inc(adj_loaded, 16)
                tiles(sp, body)

            @block.gpsimd
            def _(pool):
                pool.iota(count_int[:, :], pattern=[[1, N]], base=0, channel_multiplier=0).then_inc(counted, 1)

            @block.vector
            def _(dve):
                dve.wait_ge(loaded, 16)
                dve.wait_ge(counted, 1)
                dve.tensor_copy(subj[:, :], index[:, :, 0])
                dve.tensor_copy(obj[:, :], index[:, :, 1])
                dve.tensor_copy(count[:, :], count_int[:, :])
                dve.tensor_copy(diag[:, :], m.ident[:, :])
                dve.drain()
                dve.tensor_scalar(off_diag[:, :], diag[:, :], -1.0, 1.0, ALU.mult, ALU.add)
                dve.drain()
                dve.tensor_scalar(diag[:, :], diag[:, :], 1e-7, None, ALU.mult)
                dve.drain()

                def body(t):
                    def hots(c, b, n):
                        dve.tensor_scalar(subj_hot[:, b], count[:, 0:P], subj[:, at(c)], None, ALU.is_equal)
                        dve.tensor_scalar(obj_hot[:, b], count[:, :], obj[:, at(c)], None, ALU.is_equal).then_inc(hot, 1)
                    hots(0, 0, 0)
                    hots(1, 1, 0)
                    with dve.Fori(1, EC // 2) as c2:
                        for b in range(2):
                            dve.wait_ge(used, EC * t + 2 * c2 + b - 1)
                            hots(2 * c2 + b, b, 0)
                    dve.drain()
                    dve.tensor_scalar(subj[:, :], subj[:, :], -float(P), None, ALU.add)
                    dve.drain()
                    wait(dve, stored, 32 * t)
                    dve.wait_ge(adj_loaded, 16 * (t + 1))
                    dve.tensor_scalar(adj[:, :], adj[:, :], 1.0, None, ALU.is_equal)
                    dve.wait_ge(used, EC * (t + 1))
                    dve.tensor_scalar(factor[:, :], related[:, :], 1.0, 1.0 / math.sqrt(DH2), ALU.min, ALU.mult)
                    dve.drain()
                    dve.tensor_tensor(factor[:, :], factor[:, :], adj[:, :], ALU.mult)
                    dve.tensor_scalar(shift[:, :], adj[:, :], -1.0, 1e30, ALU.add, ALU.mult)
                    dve.drain()
                    own = at(t * P, P)
                    dve.tensor_tensor(factor[:, own], factor[:, own], off_diag[:, :], ALU.mult)
                    dve.tensor_tensor(shift[:, own], shift[:, own], off_diag[:, :], ALU.mult)
                    dve.drain()
                    dve.tensor_tensor(shift[:, own], shift[:, own], diag[:, :], ALU.add).then_inc(made, 1)
                tiles(dve, body)

            @block.tensor
            def _(pe):
                def body(t):
                    def chunk(n, b, start, stop):
                        pe.wait_ge(hot, n + 1)
                        for c in range(4):
                            last = pe.matmul(related[:, 512 * c:512 * c + 512], subj_hot[:, b],
                                             obj_hot[:, b, 512 * c:512 * c + 512], start=start, stop=stop)
                        return last
                    chunk(EC * t, 0, True, False).then_inc(used, 1)
                    chunk(EC * t + 1, 1, False, False).then_inc(used, 1)
                    with pe.Fori(1, EC // 2 - 1) as c2:
                        for b in range(2):
                            chunk(EC * t + 2 * c2 + b, b, False, False).then_inc(used, 1)
                    chunk(EC * (t + 1) - 2, 0, False, False).then_inc(used, 1)
                    chunk(EC * (t + 1) - 1, 1, False, True).then_inc(used, 1)
                tiles(pe, body)

            @block.scalar
            def _(act):
                def body(t):
                    act.wait_ge(made, t + 1)
                    act.dma_start(m.factor[at(t)], factor[:, :]).then_inc(stored, 16)
                    act.dma_start(m.shift[at(t)], shift[:, :]).then_inc(stored, 16)
                tiles(act, body)
                act.wait_ge(stored, 32 * T)


def stage_l2_attention(nc, m, a):
    with ExitStack() as ctx:
        sb = lambda name, shape, dt=F32: m.sb(f"r_{name}", shape, dt, ctx)
        sem = lambda name: m.sem(f"r_{name}")
        w = {k: sb(f"w{k}", [P, 2, DC, 2 * D], F16) for k in "qk"}
        sources, dests = [], []
        for k, name in (("q", "L2_gnn_Wq"), ("k", "L2_gnn_Wk")):
            for h in range(HEADS2):
                for twin in range(2):
                    sources.append(a[name].rearrange("(c p) n -> p c n", p=P)[:, :, h * DH2:(h + 1) * DH2])
                    dests.append(w[k][:, :, :, (2 * h + twin) * DH2:(2 * h + twin + 1) * DH2])
        stage_weights(nc, m, "rw", sources, dests)
        bias = {k: sb(f"b{k}", [P, HEADS2]) for k in "qk"}
        xt = sb("xt", [P, T, 2 * DC, P], F16)
        h3 = sb("h3", [P, T, 2, D], F16)
        total_out = sb("out", [P, T, D])
        qs, k_high, k_low = (sb(n, [P, N], F16) for n in ("qs", "k_high", "k_low"))
        part = sb("part", [P, 512])
        factor, shift, score = sb("factor", [P, N]), sb("shift", [P, N]), sb("score", [P, N])
        eh = sb("eh", [P, 2, N], F16)
        et = sb("et", [P, 2, 8, P], F16)
        stat = sb("stat", [P, 4])
        row_max, neg_max, total, inv = (stat[:, i:i + 1] for i in range(4))
        ps_l = m.ps("r_logits", [P, N], F32, ctx)
        ps_t = m.ps("r_turn", [P, 2, 8 * P], F16, ctx)
        ps_p, ps_o = m.ps("r_part", [P, 512], F32, ctx), m.ps("r_out", [P, D], F32, ctx)
        loaded, bias_scaled, masks_loaded = sem("loaded"), sem("bias_scaled"), sem("masks_loaded")
        part_ready, part_read, part_high, part_low = sem("part_ready"), sem("part_read"), sem("part_high"), sem("part_low")
        logits, scored, e_made, e_high, e_low = sem("logits"), sem("scored"), sem("e_made"), sem("e_high"), sem("e_low")
        turn_ready, turn_read, out_ready, out_read = sem("turn_ready"), sem("turn_read"), sem("out_ready"), sem("out_read")
        stored = sem("stored")

        def tiles(eng, head, body):
            if head == 0:
                body(0, 0)
                with eng.Fori(1, T) as t:
                    body(t, t)
            else:
                with eng.Fori(0, T) as t:
                    body(t, t + head * T)

        with nc.Block() as block:
            @block.sync
            def _(sp):
                sp.dma_start(xt[:, :, :, :].rearrange("p t a n -> p t (a n)"),
                             m.turned[H1].rearrange("t p n -> p t n")).then_inc(loaded, 16)
                sp.dma_start(h3[:, :, :, :].rearrange("p t a n -> p t (a n)"),
                             m.nat[H1].rearrange("t p a n -> p t (a n)")).then_inc(loaded, 16)
                sp.dma_start(total_out[:, :, :], m.x2.rearrange("t p n -> p t n")).then_inc(loaded, 16)
                with nc.allow_non_contiguous_dma(reason="a bias vector of 512, a head per column"):
                    for k, name in (("q", "L2_gnn_bq"), ("k", "L2_gnn_bk")):
                        for twin in range(2):
                            sp.dma_start(bias[k][twin * DH2:(twin + 1) * DH2, :],
                                         a[name].rearrange("(h d) -> d h", d=DH2)).then_inc(loaded, 16)
                for head in range(HEADS2):
                    def body(t, n):
                        wait(sp, scored, n)
                        sp.dma_start(factor[:, :], m.factor[at(t)]).then_inc(masks_loaded, 16)
                        sp.dma_start(shift[:, :], m.shift[at(t)]).then_inc(masks_loaded, 16)
                    tiles(sp, head, body)
                sp.wait_ge(out_read, HEADS2 * T)
                sp.dma_start(m.x3.rearrange("t p n -> p t n"), total_out[:, :, :]).then_inc(stored, 16)
                sp.wait_ge(stored, 16)

            @block.tensor
            def _(pe):
                pe.wait_ge(loaded, 16 * 7)
                for head in range(HEADS2):
                    for c in range(4):
                        for i, k in enumerate("qk"):
                            wait(pe, part_read, 8 * head + 2 * c + i)
                            cols = slice(2 * head * DH2, 2 * (head + 1) * DH2)
                            pairs = [((w[k][:, 0, d, cols], w[k][:, 1, d, cols]),
                                      (xt[:, 4 * c:4 * c + 4, d], xt[:, 4 * c:4 * c + 4, DC + d])) for d in range(DC)]
                            product(pe, ps_p[:, :], pairs).then_inc(part_ready, 1)
                    pe.wait_ge(part_low, 8 * (head + 1))

                    def body(t, n):
                        wait(pe, scored, n)
                        for c in range(4):
                            q, cols = qs[:, at(t * P, P)], slice(512 * c, 512 * c + 512)
                            pe.matmul(ps_l[:, cols], q, k_high[:, cols], start=True, stop=False)
                            last = pe.matmul(ps_l[:, cols], q, k_low[:, cols], start=False, stop=True)
                        last.then_inc(logits, 1)
                        pe.wait_ge(e_low, n + 1)
                        for c in range(4):
                            wait(pe, turn_read, 4 * n + c - 1)
                            for half in range(2):
                                for j in range(4):
                                    i = 4 * half + j
                                    last = pe.transpose(ps_t[:, c % 2, i * P:(i + 1) * P],
                                                        eh[:, half, (4 * c + j) * P:(4 * c + j + 1) * P], m.ident[:, :])
                            last.then_inc(turn_ready, 1)
                            pe.wait_ge(turn_read, 4 * n + c + 1)
                            pairs = [((et[:, c % 2, j], et[:, c % 2, 4 + j]), (h3[:, 4 * c + j, 0], h3[:, 4 * c + j, 1]))
                                     for j in range(4)]
                            if c == 0:
                                wait(pe, out_read, n)
                            last = product(pe, ps_o[:, :], pairs, start=c == 0, stop=c == 3)
                        last.then_inc(out_ready, 1)
                    tiles(pe, head, body)

            @block.scalar
            def _(act):
                act.wait_ge(bias_scaled, 2)
                for head in range(HEADS2):
                    wait(act, logits, T * head)
                    for c in range(4):
                        for i, (k, dst) in enumerate((("q", qs), ("k", k_high))):
                            u = 8 * head + 2 * c + i
                            act.wait_ge(part_ready, u + 1)
                            wait(act, part_low, u)
                            act.activation(part[:, :], ps_p[:, :], ACT.Identity, bias=bias[k][:, head:head + 1],
                                           scale=SQ / (SX * SW)).then_inc(part_read, 1)
                            act.wait_ge(part_read, u + 1)
                            act.copy(dst[:, 512 * c:512 * c + 512], part[:, :]).then_inc(part_high, 1)

                    def body(t, n):
                        act.wait_ge(scored, n + 1)
                        act.activation(score[:, :], score[:, :], ACT.Exp, bias=neg_max, accum_out=total).then_inc(e_made, 1)
                        act.wait_ge(e_made, n + 1)
                        act.copy(eh[:, 0], score[:, :]).then_inc(e_high, 1)
                    tiles(act, head, body)

            @block.gpsimd
            def _(pool):
                for head in range(HEADS2):
                    def body(t, n):
                        pool.wait_ge(e_high, n + 1)
                        pool.tensor_tensor(eh[:, 1], score[:, :], eh[:, 0], ALU.subtract).then_inc(e_low, 1)
                    tiles(pool, head, body)

            @block.vector
            def _(dve):
                dve.wait_ge(loaded, 16 * 7)
                for k in "qk":
                    dve.tensor_scalar(bias[k][:, :], bias[k][:, :], SQ, None, ALU.mult).then_inc(bias_scaled, 1)
                low = slice(DA, P)
                for head in range(HEADS2):
                    for c in range(4):
                        cols = slice(512 * c, 512 * c + 512)
                        dve.wait_ge(part_high, 8 * head + 2 * c + 1)
                        dve.tensor_tensor(qs[low, cols], part[low, :], qs[low, cols], ALU.subtract).then_inc(part_low, 1)
                        dve.wait_ge(part_high, 8 * head + 2 * c + 2)
                        dve.tensor_tensor(k_low[:, cols], part[:, :], k_high[:, cols], ALU.subtract).then_inc(part_low, 1)

                    def body(t, n):
                        dve.wait_ge(logits, n + 1)
                        dve.wait_ge(masks_loaded, 32 * (n + 1))
                        dve.scalar_tensor_tensor(out=score[:, :], in0=ps_l[:, :], scalar=1.0 / (SQ * SQ), in1=factor[:, :],
                                                 op0=ALU.mult, op1=ALU.mult)
                        dve.drain()
                        dve.tensor_tensor(score[:, :], score[:, :], shift[:, :], ALU.add)
                        dve.drain()
                        dve.tensor_reduce(row_max, score[:, :], AX.X, ALU.max)
                        dve.drain()
                        dve.tensor_scalar(neg_max, row_max, -1.0, math.log(SE), ALU.mult, ALU.add).then_inc(scored, 1)
                        for c in range(4):
                            dve.wait_ge(turn_ready, 4 * n + c + 1)
                            dve.tensor_copy(et[:, c % 2].rearrange("p k n -> p (k n)").bitcast(F32),
                                            ps_t[:, c % 2].bitcast(F32)).then_inc(turn_read, 1)
                        dve.wait_ge(e_made, n + 1)
                        dve.reciprocal(inv, total)
                        dve.drain()
                        dve.tensor_scalar(inv, inv, 1.0 / (HEADS2 * SX), None, ALU.mult)
                        dve.drain()
                        dve.wait_ge(out_ready, n + 1)
                        dve.scalar_tensor_tensor(out=total_out[:, at(t)].rearrange("p o n -> p (o n)"), in0=ps_o[:, :],
                                                 scalar=inv, in1=total_out[:, at(t)].rearrange("p o n -> p (o n)"),
                                                 op0=ALU.mult, op1=ALU.add).then_inc(out_read, 1)
                    tiles(dve, head, body)


def stage_flag(nc, m):
    m.flag = m.sb("flag", [P, 4])
    with ExitStack() as ctx:
        reduced, spread, done = m.sem("f_reduced"), m.sem("f_spread"), m.sem("f_done")
        with nc.Block() as block:
            @block.vector
            def _(dve):
                dve.tensor_reduce(m.flag[:, 0:1], m.near_value[:, :], AX.X, ALU.max).then_inc(reduced, 1)
                dve.wait_ge(spread, 1)
                dve.tensor_scalar(m.flag[:, 2:3], m.flag[:, 1:2], 1.0, None, ALU.is_ge).then_inc(done, 1)

            @block.gpsimd
            def _(pool):
                pool.wait_ge(reduced, 1)
                pool.partition_all_reduce(m.flag[:, 1:2], m.flag[:, 0:1], P, bass.bass_isa.ReduceOp.max).then_inc(spread, 1)


def gnn_stack(nc, out, a):
    with ExitStack() as ctx:
        m = Memory(nc, ctx)
        m.nat = m.dram("nat", (8, T, P, 2, D), F16)
        m.turned = m.dram("turned", (5, T, P, 8 * P), F16)
        m.panels = m.dram("panels", (T, P, 2, T, P), F16)
        m.x1, m.x2, m.x3, m.hidden = (m.dram(n, (T, P, D)) for n in ("x1", "x2", "x3", "hidden"))
        m.factor, m.shift = m.dram("factor", (T, P, N)), m.dram("shift", (T, P, N))
        m.table = m.dram("table", (T, P, ROW3))
        m.score2_rows = m.dram("score2_rows", (HEADS3, N))
        m.adj_panels = a["adj_panels"]
        m.adj_rows = a["adj"].rearrange("(t p) n -> t p n", p=P)
        x_view = a["x"].rearrange("(t p) d -> t p d", p=P)
        out_view = out.rearrange("(t p) d -> t p d", p=P)
        m.inv_row = m.sb("inv_row", [P, T])
        m.near_value, m.near_index = m.sb("near_value", [P, T * 8]), m.sb("near_index", [P, T * 8], U32)
        stage_constants(nc, m)
        with ExitStack() as l0:
            m.w1, m.w3 = (m.sb(n, [P, 2, DC, P], F16, l0) for n in ("w1", "w3"))
            m.w2 = m.sb("w2", [P, 2, 1, P], F16, l0)
            m.qw, m.k_high, m.k_low = (m.sb(n, [P, N], F16, l0) for n in ("qw", "k_high", "k_low"))
            chunked = lambda w: w.rearrange("(c p) n -> p c n", p=P)
            halves = [slice(0, DA), slice(DA, P)]
            stage_weights(nc, m, "wq", [chunked(a["L0_gnn_W1"])] * 2 + [chunked(a["L0_gnn_W3"])] * 2,
                          [w[:, :, :, half] for w in (m.w1, m.w3) for half in halves])
            stage_w2(nc, m, a["L0_gnn_W2"].rearrange("p (c n) -> p c n", c=1))
            stage_norm(nc, m, "n", x_view, H1)
            m.stage_done()
            for s in range(2):
                stage_queries_keys(nc, m, s, XA1 if s else H1)
                stage_propagate(nc, m, s)
                m.stage_done()
        stage_l0_output(nc, m, a, x_view)
        m.stage_done()
        m.score1, m.score2 = m.sb("score1", [P, T, HEADS3]), m.sb("score2", [P, T, HEADS3])
        m.w_out = m.sb("w_out", [P, 2, DC, D], F16)
        stage_l1(nc, m, a)
        stage_flag(nc, m)
        m.stage_done()
        with nc.If(nc.values_load(m.flag[0:1, 2:3].bitcast(I32)) > 0):
            stage_norm(nc, m, "h3", m.x2, H1)
            m.stage_done()
            stage_l2_masks(nc, m, a)
            m.stage_done()
            stage_l2_attention(nc, m, a)
            m.stage_done()
            stage_l3_sequence(nc, m, a)
            m.stage_done()
        stage_l3_flags(nc, m)
        m.stage_done()
        near = nc.values_load(m.flag3[0:1, 0:1].bitcast(I32))
        with nc.If(near > 0):
            stage_l3_near(nc, m, a, out_view)
            m.stage_done()
        far = nc.values_load(m.flag3[0:1, 1:2].bitcast(I32))
        with nc.If(far > 0):
            stage_l3_far_rows(nc, m)
            m.stage_done()
            stage_l3_attention(nc, m)
            m.stage_done()
            stage_l3_output(nc, m, a, out_view)


def kernel(**inputs):
    import numpy as _np
    import concourse.bacc as _bacc
    from concourse import mybir as _mybir
    from concourse.bass_utils import run_bass_kernel_spmd as _run

    def layout(a):
        return _np.ascontiguousarray(a)

    inputs = {k: _np.asarray(v) for k, v in inputs.items()}
    adj = inputs["adj"]
    arrays = {name: layout(a) for name, a in inputs.items()}
    arrays["adj_panels"] = layout(adj.reshape(16, 128, 16, 128).transpose(0, 3, 2, 1))
    for name in ("L2_gnn_Wq", "L2_gnn_Wk"):
        arrays[name] = layout(inputs[name].T)
    nc = _bacc.Bacc("TRN2", target_bir_lowering=False, num_devices=1)
    args, given = {}, {}
    for name, a in arrays.items():
        given[f"in_{name}"] = a
        args[name] = nc.dram_tensor(f"in_{name}", a.shape, _mybir.dt.from_np(a.dtype), kind="ExternalInput").ap()
    out = nc.dram_tensor("out", (2048, 512), _mybir.dt.float32, kind="ExternalOutput").ap()
    gnn_stack(nc, out, args)
    r = _run(nc, [given], core_ids=[0])
    return r.results[0]["out"]
```
